# Optimizing a Trainium2 kernel written in Bass

```python
import numpy as np
import jax
import jax.numpy as jnp

def _softmax(x, axis=-1):
    return jax.nn.softmax(x, axis=axis)

def _gelu(x):
    return jax.nn.gelu(x, approximate=True)

def _silu(x):
    return jax.nn.silu(x)

def _sigmoid(x):
    return jax.nn.sigmoid(x)

def _layernorm(x, axis=-1, eps=1e-05):
    m = jnp.mean(x, axis=axis, keepdims=True)
    v = jnp.var(x, axis=axis, keepdims=True)
    return (x - m) / jnp.sqrt(v + eps)

def _scatter_add(tgt, idx, src, axis=0):
    return tgt.at[idx].add(src)

def _segment_sum(src, seg, n):
    return jax.ops.segment_sum(src, seg, n)
kernel_name = 'mk_sandwich_d1_jaxref_r4_c7c149'

def setup_inputs(seed: int=0):
    np.random.seed(seed)
    _w = jnp.asarray

    def _L0_attn_setup():
        import jax, jax.numpy as jnp
        import numpy as np
        D_MODEL = 256
        EXPAND = 2
        D_INNER = EXPAND * D_MODEL
        D_STATE = 16
        D_CONV = 4
        DT_RANK = D_INNER
        BATCH, SEQ = (2, 256)
        EPS = 1e-05

        def _rmsnorm(x, w):
            var = jnp.mean(jnp.square(x), axis=-1, keepdims=True)
            return x * jax.lax.rsqrt(var + EPS) * w

        def _forward(x, rms_w, W_in, conv_w, conv_b, W_x, W_dt, A_log, W_out):
            B, L, _ = x.shape
            residual = x
            xn = _rmsnorm(x, rms_w)
            xr = xn @ W_in
            xs, res = jnp.split(xr, 2, axis=-1)
            xc = jnp.transpose(xs, (0, 2, 1))
            xc = jnp.pad(xc, ((0, 0), (0, 0), (D_CONV - 1, 0)))
            xc = jax.lax.conv_general_dilated(xc, conv_w, window_strides=(1,), padding='VALID', dimension_numbers=('NCH', 'OIH', 'NCH'), feature_group_count=D_INNER)
            xc = xc + conv_b[None, :, None]
            xs = jax.nn.silu(jnp.transpose(xc, (0, 2, 1)))
            x_ssm = xs @ W_x
            dt, Bm, Cm = jnp.split(x_ssm, [D_INNER, D_INNER + D_STATE], axis=-1)
            dt = jax.nn.softplus(dt @ W_dt)
            A = -jnp.exp(A_log)
            A_disc = jnp.exp(A[None, None] * dt[..., None])
            Bx = dt[..., None] * Bm[:, :, None, :] * xs[..., None]

            def step(h, inp):
                Ad_t, Bx_t, C_t = inp
                h = Ad_t * h + Bx_t
                y = jnp.einsum('bdn,bn->bd', h, C_t)
                return (h, y)
            h0 = jnp.zeros((B, D_INNER, D_STATE), xs.dtype)
            _, ys = jax.lax.scan(step, h0, (jnp.transpose(A_disc, (1, 0, 2, 3)), jnp.transpose(Bx, (1, 0, 2, 3)), jnp.transpose(Cm, (1, 0, 2))))
            y = jnp.transpose(ys, (1, 0, 2))
            y = y * jax.nn.silu(res)
            out = y @ W_out
            return residual + out
        key = jax.random.key(seed)
        ks = jax.random.split(key, 9)
        s = 0.02
        return {'x': jax.random.normal(ks[0], (BATCH, SEQ, D_MODEL), jnp.float32), 'rms_w': jnp.ones((D_MODEL,), jnp.float32), 'W_in': jax.random.normal(ks[1], (D_MODEL, 2 * D_INNER), jnp.float32) * s, 'conv_w': jax.random.normal(ks[2], (D_INNER, 1, D_CONV), jnp.float32) * 0.2, 'conv_b': jax.random.normal(ks[3], (D_INNER,), jnp.float32) * 0.02, 'W_x': jax.random.normal(ks[4], (D_INNER, DT_RANK + 2 * D_STATE), jnp.float32) * s, 'W_dt': jax.random.normal(ks[5], (DT_RANK, D_INNER), jnp.float32) * s, 'A_log': jax.random.normal(ks[6], (D_INNER, D_STATE), jnp.float32), 'W_out': jax.random.normal(ks[7], (D_INNER, D_MODEL), jnp.float32) * s}
    _L0_attn_in = _L0_attn_setup()

    def _L0_ffn_setup():
        import jax, jax.numpy as jnp
        import numpy as np
        import math
        B, S, D = (4, 512, 256)
        E, DFF = (16, 512)
        CAP_FACTOR = 2.0
        ROUTER_HIDDEN = 128
        CAPACITY = int(math.ceil(S * CAP_FACTOR / E))
        key = jax.random.key(seed)
        ks = jax.random.split(key, 6)

        def uinit(k, shape, fan_in):
            bound = math.sqrt(3.0) * math.sqrt(1.0 / 3.0) / math.sqrt(fan_in)
            return jax.random.uniform(k, shape, jnp.float32, -bound, bound)
        return {'hidden_states': jax.random.normal(ks[0], (B, S, D), jnp.float32), 'router_w1': jax.random.normal(ks[1], (D, ROUTER_HIDDEN), jnp.float32) / math.sqrt(D), 'router_w2': jax.random.normal(ks[2], (ROUTER_HIDDEN, E), jnp.float32) / math.sqrt(ROUTER_HIDDEN), 'w1': uinit(ks[3], (E, D, DFF), D), 'w2': uinit(ks[4], (E, D, DFF), D), 'w3': uinit(ks[5], (E, DFF, D), DFF)}
    _L0_ffn_in = _L0_ffn_setup()
    _d = {'L0_attn_x': _L0_attn_in['x'], 'L0_attn_rms_w': _L0_attn_in['rms_w'], 'L0_attn_W_in': _L0_attn_in['W_in'], 'L0_attn_conv_w': _L0_attn_in['conv_w'], 'L0_attn_conv_b': _L0_attn_in['conv_b'], 'L0_attn_W_x': _L0_attn_in['W_x'], 'L0_attn_W_dt': _L0_attn_in['W_dt'], 'L0_attn_A_log': _L0_attn_in['A_log'], 'L0_attn_W_out': _L0_attn_in['W_out'], 'L0_ffn_router_w1': _L0_ffn_in['router_w1'], 'L0_ffn_router_w2': _L0_ffn_in['router_w2'], 'L0_ffn_w1': _L0_ffn_in['w1'], 'L0_ffn_w2': _L0_ffn_in['w2'], 'L0_ffn_w3': _L0_ffn_in['w3']}
    _x0 = _d['L0_attn_x']
    _d['L0_attn_x'] = jax.random.normal(jax.random.fold_in(jax.random.key(seed), 1), (2, 4096, 256), dtype=_x0.dtype)
    del _x0
    return _d

def reference(L0_attn_x, L0_attn_rms_w, L0_attn_W_in, L0_attn_conv_w, L0_attn_conv_b, L0_attn_W_x, L0_attn_W_dt, L0_attn_A_log, L0_attn_W_out, L0_ffn_router_w1, L0_ffn_router_w2, L0_ffn_w1, L0_ffn_w2, L0_ffn_w3):

    def _L0_attn_ref(x, rms_w, W_in, conv_w, conv_b, W_x, W_dt, A_log, W_out):
        import jax, jax.numpy as jnp
        import numpy as np
        D_MODEL = 256
        EXPAND = 2
        D_INNER = EXPAND * D_MODEL
        D_STATE = 16
        D_CONV = 4
        DT_RANK = D_INNER
        BATCH, SEQ = (2, 256)
        EPS = 1e-05

        def _rmsnorm(x, w):
            var = jnp.mean(jnp.square(x), axis=-1, keepdims=True)
            return x * jax.lax.rsqrt(var + EPS) * w

        def _forward(x, rms_w, W_in, conv_w, conv_b, W_x, W_dt, A_log, W_out):
            B, L, _ = x.shape
            residual = x
            xn = _rmsnorm(x, rms_w)
            xr = xn @ W_in
            xs, res = jnp.split(xr, 2, axis=-1)
            xc = jnp.transpose(xs, (0, 2, 1))
            xc = jnp.pad(xc, ((0, 0), (0, 0), (D_CONV - 1, 0)))
            xc = jax.lax.conv_general_dilated(xc, conv_w, window_strides=(1,), padding='VALID', dimension_numbers=('NCH', 'OIH', 'NCH'), feature_group_count=D_INNER)
            xc = xc + conv_b[None, :, None]
            xs = jax.nn.silu(jnp.transpose(xc, (0, 2, 1)))
            x_ssm = xs @ W_x
            dt, Bm, Cm = jnp.split(x_ssm, [D_INNER, D_INNER + D_STATE], axis=-1)
            dt = jax.nn.softplus(dt @ W_dt)
            A = -jnp.exp(A_log)
            A_disc = jnp.exp(A[None, None] * dt[..., None])
            Bx = dt[..., None] * Bm[:, :, None, :] * xs[..., None]

            def step(h, inp):
                Ad_t, Bx_t, C_t = inp
                h = Ad_t * h + Bx_t
                y = jnp.einsum('bdn,bn->bd', h, C_t)
                return (h, y)
            h0 = jnp.zeros((B, D_INNER, D_STATE), xs.dtype)
            _, ys = jax.lax.scan(step, h0, (jnp.transpose(A_disc, (1, 0, 2, 3)), jnp.transpose(Bx, (1, 0, 2, 3)), jnp.transpose(Cm, (1, 0, 2))))
            y = jnp.transpose(ys, (1, 0, 2))
            y = y * jax.nn.silu(res)
            out = y @ W_out
            return residual + out
        return _forward(x, rms_w, W_in, conv_w, conv_b, W_x, W_dt, A_log, W_out)

    def _L0_ffn_ref(hidden_states, router_w1, router_w2, w1, w2, w3):
        import jax, jax.numpy as jnp
        import numpy as np
        import math
        B, S, D = (4, 512, 256)
        E, DFF = (16, 512)
        CAP_FACTOR = 2.0
        ROUTER_HIDDEN = 128
        CAPACITY = int(math.ceil(S * CAP_FACTOR / E))
        b, s, d = hidden_states.shape
        e = w1.shape[0]
        cap = CAPACITY
        router_logits = jax.nn.silu(hidden_states @ router_w1) @ router_w2
        expert_probs = jax.nn.softmax(router_logits.transpose(0, 2, 1), axis=-1)
        expert_weights, token_indices = jax.lax.top_k(expert_probs, cap)
        expert_weights = expert_weights / (expert_weights.sum(-1, keepdims=True) + 1e-09)
        expert_inputs = jax.vmap(lambda h, i: h[i])(hidden_states, token_indices)
        gate = jax.nn.silu(jnp.einsum('becd,edf->becf', expert_inputs, w1))
        value = jnp.einsum('becd,edf->becf', expert_inputs, w2)
        expert_out = jnp.einsum('becf,efd->becd', gate * value, w3)
        weighted = expert_out * expert_weights[..., None]

        def combine(idx, vals):
            return jnp.zeros((s, d), vals.dtype).at[idx.reshape(-1)].add(vals.reshape(-1, d))
        output = jax.vmap(combine)(token_indices, weighted)
        return output
    x = L0_attn_x
    x = x + _layernorm(_L0_attn_ref(_layernorm(x, axis=-1), L0_attn_rms_w, L0_attn_W_in, L0_attn_conv_w, L0_attn_conv_b, L0_attn_W_x, L0_attn_W_dt, L0_attn_A_log, L0_attn_W_out), axis=-1)
    x = x + _layernorm(_L0_ffn_ref(_layernorm(x, axis=-1), L0_ffn_router_w1, L0_ffn_router_w2, L0_ffn_w1, L0_ffn_w2, L0_ffn_w3), axis=-1)
    return x

_drawn_inputs = setup_inputs


def setup_inputs(seed=0):
    import zlib

    import numpy as np

    out = dict(_drawn_inputs(seed))
    spreads = {'L0_attn_rms_w': (1.0, 0.6)}
    factors = {'L0_attn_W_in': 8.0,
     'L0_attn_conv_w': 8.0,
     'L0_attn_conv_b': 8.0,
     'L0_attn_W_x': 8.0,
     'L0_attn_W_dt': 8.0,
     'L0_attn_A_log': 8.0,
     'L0_attn_W_out': 8.0}
    for name, (base, spread) in spreads.items():
        noise = np.random.default_rng([zlib.crc32(name.encode()), seed]).standard_normal(out[name].shape)
        drawn = base * np.exp(spread * noise) if base else spread * noise
        out[name] = jnp.asarray(drawn.astype(out[name].dtype))
    for name, factor in factors.items():
        out[name] = (out[name] * factor).astype(out[name].dtype)
    return out
```

```python
from contextlib import ExitStack

import concourse.bass as bass
from concourse import mybir

ALU = mybir.AluOpType
ACT = mybir.ActivationFunctionType
AX = mybir.AxisListType
F32 = mybir.dt.float32
BF16 = mybir.dt.bfloat16
U32 = mybir.dt.uint32

P = 128
T = 512
SUB = T // P
DM = 256
DI = 512
NS = 16
TAPS = 4
KC = DM // P
DC = DI // P
GROUPS = DI // 8
QUADS = GROUPS // 4
EPS = 1e-5
ROUTER = 128
E = 16
DFF = 512
CAP = 64
FC = DFF // P
AHEAD = 4
EV_ACT = 13
PARTS = 3
STK_DMAS = 4 * PARTS * 16

XS_AT, RES_AT, CONV_AT, SILU_AT, BC_AT, DT_AT, DT_EVERY = 16, 24, 19, 32, 34, 37, 11


def atleast(eng, sem, value):
    if isinstance(value, int) and value <= 0:
        return
    eng.wait_ge(sem, value)


def sandwich(nc, x, rms_w, W_in, conv_w, conv_b, W_x, W_dt, A_log, W_out, r_w1, r_w2, w1, w2, w3, out):
    B, S, _ = x.shape
    assert B == 2 and S % T == 0
    TILES = B * (S // T)
    xf = x.rearrange("b s d -> (b s) d")
    outf = out.rearrange("b s d -> (b s) d")
    hid_dram = nc.dram_tensor("hidden_scratch", [B * S, DM], F32, kind="Internal").ap()
    acc_dram = nc.dram_tensor("combine_scratch", [B * S, DM], F32, kind="Internal").ap()
    lg_dram = nc.dram_tensor("logits_scratch", [B * E, S], F32, kind="Internal").ap()

    with ExitStack() as whole:
        def sem(name):
            return whole.enter_context(nc.semaphore(name))

        ident = whole.enter_context(nc.sbuf_tensor("ident", [P, P], F32))
        mhalf = whole.enter_context(nc.sbuf_tensor("mhalf", [P, 2 * SUB], F32))

        scan_layers(nc, sem, TILES, S, ident, mhalf, xf, outf, rms_w, W_in, conv_w, conv_b, W_x, W_dt, A_log, W_out,
                    r_w1, r_w2, hid_dram, acc_dram, lg_dram)
        experts(nc, sem, B, S, ident, mhalf, outf, w1, w2, w3, hid_dram, acc_dram, lg_dram)


def scan_layers(nc, sem, TILES, S, ident, mhalf, xf, outf, rms_w, W_in, conv_w, conv_b, W_x, W_dt, A_log, W_out,
                r_w1, r_w2, hid_dram, acc_dram, lg_dram):
    with ExitStack() as ctx:
        def sb(name, shape, dt=F32):
            return ctx.enter_context(nc.sbuf_tensor(name, shape, dt))

        def ps(name, shape):
            return ctx.enter_context(nc.psum_tensor(name, shape, F32))

        pdt = ps("pdt", [P, 2, T])
        pu = ps("pu", [P, 2, T])
        py = ps("py", [P, T])
        pp = ps("pp", [P, 2, T])
        po = ps("po", [P, T])

        w_in = sb("w_in", [P, KC, 2 * DI])
        w_dtx = sb("w_dtx", [P, DC, DI])
        w_bc = sb("w_bc", [P, DC, 2 * NS])
        w_out = sb("w_out", [P, DC, DM])
        rw1 = sb("rw1", [P, KC, ROUTER])
        rw2 = sb("rw2", [P, E])
        cw = sb("cw", [P, DC, TAPS])
        cb = sb("cb", [P, DC])
        rms = sb("rms", [P, KC])
        neg_a = sb("neg_a", [P, GROUPS])
        a_rows = sb("a_rows", [GROUPS, P])
        blk = sb("blk", [P, 32])
        sel_rep = sb("sel_rep", [P, 4, P], BF16)
        sel_sum = sb("sel_sum", [P, 4, 32])
        sel_b = sb("sel_b", [P, P])
        sel_c = sb("sel_c", [P, P])
        m8 = sb("m8", [P, 8])

        xt = sb("xt", [P, SUB, DM])
        xnt = sb("xnt", [P, KC, T])
        st = sb("st", [P, SUB, 6])
        mv = sb("mv", [P, SUB, 2])
        var = sb("var", [P, 2 * SUB])
        rs = sb("rs", [P, 2 * SUB])
        nm = sb("nm", [P, SUB])
        pad = sb("pad", [P, 1], U32)
        r1 = sb("r1", [P, 2, SUB])
        xsp = sb("xsp", [P, 2, T + TAPS - 1])
        halo = sb("halo", [P, 2, DC, TAPS - 1])
        xs = sb("xs", [P, DC, T])
        gate = sb("gate", [P, 2, DC, T])
        bc = sb("bc", [P, T])
        b_rep = sb("b_rep", [P, 2, T])
        c_rep = sb("c_rep", [P, 2, T])
        spe = sb("spe", [P, T])
        spl = sb("spl", [P, T])
        spt = sb("spt", [P, T])
        dtv = sb("dtv", [P, 2, T])
        uv = sb("uv", [P, 2, T])
        rem = sb("rem", [P, 2, T])
        parts = sb("parts", [P, 2, 2, PARTS, T], BF16)
        stk = sb("stk", [P, 2, 4 * DC, T], BF16)

        decay = sb("decay", [P, 8, T])
        bx = sb("bx", [P, 2, T])
        h = sb("h", [P, 8, T])
        hc = sb("hc", [P, 8, T])
        carry = sb("carry", [P, 2, GROUPS])

        xo = sb("xo", [P, SUB, DM])
        z = sb("z", [P, SUB, DM])
        st2 = sb("st2", [P, SUB, 6])
        mv2 = sb("mv2", [P, SUB, 2])
        var2 = sb("var2", [P, SUB])
        rs2 = sb("rs2", [P, SUB])
        nm2 = sb("nm2", [P, SUB])
        hid = sb("hid", [P, SUB, DM])
        ht = sb("ht", [P, KC, T])

        d_w, d_a = sem("d_w"), sem("d_a")
        s_set, s_setv, s_sett, s_seta = sem("s_set"), sem("s_setv"), sem("s_sett"), sem("s_seta")

        wxs = h[:, 0:DC, :]
        wxt = h[:, 4:4 + DC, :]
        wdt = hc[:, 0:DC, :]
        with nc.Block() as block:
            @block.sync
            def _(sp):
                sp.dma_start(wxs, W_x[:, 0:DI].rearrange("(c p) j -> p c j", p=P)).then_inc(d_w, 16)
                sp.dma_start(wdt, W_dt.rearrange("(c p) j -> p c j", p=P)).then_inc(d_w, 16)
                sp.dma_start(a_rows[:], A_log.rearrange("(g e) n -> g (e n)", e=8)).then_inc(d_a, 16)
                sp.dma_start(w_in[:], W_in.rearrange("(c p) j -> p c j", p=P)).then_inc(d_w, 16)
                sp.dma_start(w_bc[:], W_x[:, DI:DI + 2 * NS].rearrange("(c p) j -> p c j", p=P)).then_inc(d_w, 16)
                sp.dma_start(w_out[:], W_out.rearrange("(c p) j -> p c j", p=P)).then_inc(d_w, 16)
                sp.dma_start(rw1[:], r_w1.rearrange("(c p) j -> p c j", p=P)).then_inc(d_w, 16)
                sp.dma_start(rw2[:], r_w2).then_inc(d_w, 16)
                sp.dma_start(cw[:], conv_w.rearrange("(c p) o k -> p c (o k)", p=P)).then_inc(d_w, 16)
                sp.dma_start(cb[:], conv_b.rearrange("(c p) -> p c", p=P), allow_slow_non_contiguous=True).then_inc(d_w, 16)
                sp.dma_start(rms[:], rms_w.rearrange("(c p) -> p c", p=P), allow_slow_non_contiguous=True).then_inc(d_w, 16)
                sp.wait_ge(s_setv, 1)
                for r in range(0, acc_dram.shape[0], T):
                    sp.dma_start(acc_dram[r:r + T, :].rearrange("(s p) d -> p s d", p=P), hid[:]).then_inc(d_a, 16)
                sp.wait_ge(d_a, 16 * (1 + acc_dram.shape[0] // T))
                sp.wait_ge(d_w, 160)

            @block.gpsimd
            def _(pool):
                pool.memset(ident[:], 1.0).then_inc(s_set, 1)
                pool.memset(m8[:], 1.0).then_inc(s_set, 1)
                pool.wait_ge(s_set, 2)
                pool.affine_select(out=ident[:], in_=ident[:], compare_op=ALU.is_equal, fill=0.0, base=0,
                                   pattern=[[-1, P]], channel_multiplier=1).then_inc(s_set, 1)
                pool.affine_select(out=m8[:], in_=m8[:], compare_op=ALU.is_ge, fill=0.0, base=0,
                                   pattern=[[-16, 8]], channel_multiplier=1).then_inc(s_set, 1)
                pool.wait_ge(s_set, 4)
                pool.affine_select(out=m8[:], in_=m8[:], compare_op=ALU.is_ge, fill=0.0, base=15,
                                   pattern=[[16, 8]], channel_multiplier=-1).then_inc(s_set, 1)

            @block.vector
            def _(v):
                v.memset(hid[:], 0.0).then_inc(s_setv, 1)
                v.memset(mhalf[:], -0.5)
                v.memset(carry[:], 0.0)
                v.memset(halo[:], 0.0)
                v.memset(sel_sum[:], 0.0).then_inc(s_setv, 1)
                v.wait_ge(s_set, 5)
                v.tensor_reduce(blk[:], ident[:].rearrange("p (k r) -> p r k", r=32), AX.X, ALU.add).then_inc(s_setv, 1)
                v.wait_ge(s_setv, 3)
                for s in range(4):
                    v.tensor_copy(sel_rep[:, s, :].rearrange("p (e n) -> p e n", n=NS),
                                  blk[:, 8 * s:8 * s + 8].unsqueeze(2).broadcast_to((P, 8, NS)))
                    v.tensor_copy(sel_sum[:, s, 8 * s:8 * s + 8], m8[:])
                v.tensor_copy(sel_b[:].rearrange("p (e n) -> p e n", n=NS),
                              blk[:, 0:NS].unsqueeze(1).broadcast_to((P, 8, NS)))
                v.tensor_copy(sel_c[:].rearrange("p (e n) -> p e n", n=NS),
                              blk[:, NS:2 * NS].unsqueeze(1).broadcast_to((P, 8, NS)))
                v.wait_ge(d_w, 160)
                for c in range(KC):
                    v.tensor_scalar(w_in[:, c, :], w_in[:, c, :], rms[:, c:c + 1], None, ALU.mult)
                v.wait_ge(s_seta, 1)
                v.tensor_scalar(neg_a[:], neg_a[:], -1.0, None, ALU.mult)

            @block.tensor
            def _(pe):
                pe.wait_ge(s_set, 5)
                pe.wait_ge(d_a, 16)
                pe.wait_ge(d_w, 160)
                pe.transpose(po[:, 0:GROUPS], a_rows[:], ident[0:GROUPS, 0:GROUPS]).then_inc(s_sett, 1)
                for j in range(DC):
                    if j >= 2:
                        pe.wait_ge(s_seta, j)
                    for k in range(DC):
                        mm = pe.transpose(pp[:, j % 2, k * P:(k + 1) * P], wxs[:, k, j * P:(j + 1) * P], ident[:])
                    mm.then_inc(s_sett, 1)
                for k in range(DC):
                    pe.wait_ge(s_seta, DC + 1 if k < 2 else DC + k)
                    for j in range(DC):
                        mm = pe.matmul(pp[:, k % 2, :], wxt[:, j, k * P:(k + 1) * P], wdt[:, j, :],
                                       start=(j == 0), stop=(j == DC - 1))
                    mm.then_inc(s_sett, 1)

            @block.scalar
            def _(act):
                act.wait_ge(s_sett, 1)
                act.activation(neg_a[:], po[:, 0:GROUPS], ACT.Exp).then_inc(s_seta, 1)
                for j in range(DC):
                    act.wait_ge(s_sett, 2 + j)
                    act.copy(wxt[:, j, :], pp[:, j % 2, :]).then_inc(s_seta, 1)
                for k in range(DC):
                    act.wait_ge(s_sett, 2 + DC + k)
                    act.copy(w_dtx[:, k, :], pp[:, k % 2, :]).then_inc(s_seta, 1)

        s_rdt, s_ru = sem("rep_dt_ready"), sem("rep_u_ready")
        s_exp, s_bx, s_scan, s_carry = sem("decay_ready"), sem("bx_ready"), sem("h_ready"), sem("carry_saved")
        s_hc, s_sum, s_gate = sem("hc_ready"), sem("y_summed"), sem("y_gated")
        d_x, s_st, s_pw, s_xn = sem("x_loaded"), sem("stats_step"), sem("rstd_ready"), sem("x_normalised")
        s_r1 = sem("r1_kept")
        s_pp, s_ev = sem("prep_bank_full"), sem("prep_bank_copied")
        s_halo, s_conv = sem("halo_step"), sem("conv_step")
        s_xs, s_sg = sem("xs_ready"), sem("gate_ready")
        s_sp, s_spl, s_spv, s_dt = sem("softplus_e"), sem("softplus_ln"), sem("softplus_step"), sem("dt_ready")
        s_u, s_remd, s_lod, s_remu, s_lou = (sem("u_ready"), sem("dt_rest"), sem("dt_last_part"), sem("u_rest"),
                                             sem("u_last_part"))
        s_xd, s_xu = sem("dt_parts_ready"), sem("u_parts_ready")
        d_stk = [sem(f"stack_loaded_{c}") for c in range(DC)]
        d_xo, s_wo, s_z, s_dp, s_pw2 = (sem("xo_loaded"), sem("out_product"), sem("z_ready"), sem("post_step"),
                                        sem("post_rstd"))
        s_z2, s_x1, d_x1, s_hid, d_hid = (sem("z_normalised"), sem("x1_ready"), sem("x1_stored"), sem("hid_ready"),
                                          sem("hid_stored"))
        s_ht, s_hte, s_rh, s_rs, s_w2, s_lg, d_lg = (sem("ht_bank"), sem("ht_copied"), sem("router_hidden"),
                                                     sem("router_silu"), sem("logits_bank"), sem("logits_ready"),
                                                     sem("logits_stored"))

        def rows(i, par):
            if isinstance(i, int):
                return par * S + (i // 2) * T
            return (i - par) * (T // 2) + par * S

        def all_steps(eng, run):
            run(0, 0, False, True, True)
            run(1, 1, True, True, True)
            with eng.Fori(0, (TILES - 4) // 2) as k:
                run(2 * k + 2, 0, True, True, True)
                run(2 * k + 3, 1, True, True, True)
            run(TILES - 2, 0, True, True, True)
            run(TILES - 1, 1, True, True, False)
            run(TILES, 0, True, False, False)

        with nc.Block() as block:
            @block.sync
            def _(sp):
                def load_x(i, par):
                    atleast(sp, s_pp, 17 * i - 15)
                    sp.dma_start(xt[:], xf[bass.ds(rows(i, par), T), :].rearrange("(s p) d -> p s d", p=P)).then_inc(d_x, 16)

                def stack(c, i):
                    made, used = 4 * i + c + 1, 64 * (i - 1) + 16 * (c + 1)
                    if not isinstance(i, int):
                        sp.compute_val(made)
                        sp.compute_val(used)
                    sp.wait_ge(s_xd, made)
                    sp.wait_ge(s_xu, made)
                    sp.wait_ge(s_lod, made)
                    sp.wait_ge(s_lou, made)
                    atleast(sp, s_rdt, used)
                    atleast(sp, s_ru, used)
                    for q in range(4):
                        for m in range(PARTS):
                            sp.dma_start(stk[32 * m:32 * m + 32, :, 4 * c + q, :],
                                         parts[32 * q:32 * q + 32, c % 2, :, m, :]).then_inc(d_stk[c], 16)

                def prep(t, i, par):
                    for c in range(DC):
                        if t == DT_AT + DT_EVERY * c + 17:
                            stack(c, i)

                def post(t, j, par):
                    if t == 0:
                        atleast(sp, s_x1, j)
                        sp.dma_start(xo[:], xf[bass.ds(rows(j, par), T), :].rearrange("(s p) d -> p s d", p=P)).then_inc(d_xo, 16)
                    if t == 40:
                        sp.wait_ge(s_x1, j + 1)
                        sp.dma_start(outf[bass.ds(rows(j, par), T), :].rearrange("(s p) d -> p s d", p=P), z[:]).then_inc(d_x1, 16)
                    if t == 52:
                        sp.wait_ge(s_hid, j + 1)
                        sp.dma_start(hid_dram[bass.ds(rows(j, par), T), :].rearrange("(s p) d -> p s d", p=P), hid[:]).then_inc(d_hid, 16)
                    if t == 63:
                        col = (j // 2) * T if isinstance(j, int) else (j - par) * (T // 2)
                        if not isinstance(j, int):
                            sp.compute_val(col * 4)
                        sp.wait_ge(s_lg, j + 1)
                        sp.dma_start(lg_dram[par * E:(par + 1) * E, bass.ds(col, T)], ht[0:E, 1, :]).then_inc(d_lg, 16)

                def step(i, par, has_prev, has_cur, has_next):
                    for t in range(GROUPS):
                        if has_cur:
                            prep(64 + t, i, par)
                        if has_next:
                            prep(t, i + 1, 1 - par)
                        if has_prev:
                            post(t, i - 1, 1 - par)
                        if has_next and t == 20:
                            if isinstance(i, int) and i + 2 >= TILES:
                                continue
                            load_x(i + 2, par)

                load_x(0, 0)
                for t in range(GROUPS):
                    prep(t, 0, 0)
                    if t == 20:
                        load_x(1, 1)
                all_steps(sp, step)
                sp.wait_ge(d_x1, 16 * TILES)
                sp.wait_ge(d_hid, 16 * TILES)
                sp.wait_ge(d_lg, 16 * TILES)

            @block.tensor
            def _(pe):
                def bank_free(n, i):
                    if n < 2:
                        atleast(pe, s_dt, 4 * (i - 1) + 3 + n)
                    elif n < EV_ACT + 2:
                        pe.wait_ge(s_ev, EV_ACT * i + n - 1)
                    else:
                        pe.wait_ge(s_dt, 4 * i + n - EV_ACT - 1)

                def spread_dt(t, i, par):
                    c, s, q = t // 16, t // 4 % 4, t % 4
                    if t % 16 == 0:
                        pe.wait_ge(d_stk[c], STK_DMAS * (i + 1))
                    atleast(pe, s_exp, 64 * i + t - 1)
                    pe.matmul(pdt[:, t % 2, :], sel_rep[0:96, s, :], stk[0:96, 0, 4 * c + q, :],
                              start=True, stop=True).then_inc(s_rdt, 1)

                def spread_u(t, i, par):
                    c, s, q = t // 16, t // 4 % 4, t % 4
                    atleast(pe, s_bx, 64 * i + t - 1)
                    pe.matmul(pu[:, t % 2, :], sel_rep[0:96, s, :], stk[0:96, 1, 4 * c + q, :],
                              start=True, stop=True).then_inc(s_ru, 1)

                def sum_states(quad, i):
                    c, s = quad // 4, quad % 4
                    pe.wait_ge(s_hc, 32 * i + 2 * quad + 2)
                    if s == 0:
                        atleast(pe, s_gate, 4 * i + c)
                    for q in range(4):
                        mm = pe.matmul(py[32 * q:32 * q + 32, :], sel_sum[:, s, :], hc[:, (4 * quad + q) % 8, :],
                                       start=(s == 0), stop=(s == 3), tile_position=(0, 32 * q))
                    mm.then_inc(s_sum, 1)

                def prep(t, i, par):
                    def bank(n):
                        return pp[:, (par + n) % 2, :]

                    for k in range(KC):
                        if t == 12 + k:
                            pe.wait_ge(s_xn, i + 1)
                            bank_free(k, i)
                            for s in range(SUB):
                                mm = pe.transpose(bank(k)[:, s * P:(s + 1) * P], xt[:, s, k * P:(k + 1) * P], ident[:])
                            mm.then_inc(s_pp, 1)
                    for m in range(2 * DC):
                        if t == XS_AT + 2 * m:
                            if m == 0:
                                pe.wait_ge(s_ev, EV_ACT * i + 2)
                            bank_free(2 + m, i)
                            for k in range(KC):
                                mm = pe.matmul(bank(2 + m), w_in[:, k, m * P:(m + 1) * P], xnt[:, k, :],
                                               start=(k == 0), stop=(k == KC - 1))
                            mm.then_inc(s_pp, 1)
                    if t == BC_AT:
                        pe.wait_ge(s_xs, i + 1)
                        bank_free(10, i)
                        for k in range(DC):
                            mm = pe.matmul(bank(10)[32 * k:32 * k + 32, :], w_bc[:, k, :], xs[:, k, :],
                                           start=True, stop=True, tile_position=(0, 32 * k))
                        mm.then_inc(s_pp, 1)
                    if t == BC_AT + 2:
                        pe.wait_ge(s_ev, EV_ACT * i + 11)
                        bank_free(11, i)
                        pe.matmul(bank(11), sel_b[:], bc[:], start=True, stop=True).then_inc(s_pp, 1)
                        bank_free(12, i)
                        pe.matmul(bank(12), sel_c[:], bc[:], start=True, stop=True).then_inc(s_pp, 1)
                    for c in range(DC):
                        at = DT_AT + DT_EVERY * c
                        if at <= t < at + 2:
                            if t == at:
                                bank_free(13 + c, i)
                            for k in range(2 * (t - at), 2 * (t - at) + 2):
                                mm = pe.matmul(bank(13 + c), w_dtx[:, k, c * P:(c + 1) * P], xs[:, k, :],
                                               start=(k == 0), stop=(k == DC - 1))
                            if t == at + 1:
                                mm.then_inc(s_pp, 1)

                def post(t, j, par):
                    for half, at in ((0, 9), (1, 18)):
                        if at <= t < at + 4:
                            if t == 9:
                                pe.wait_ge(s_gate, 4 * j + 4)
                                atleast(pe, s_lg, j)
                            if t == 18:
                                pe.wait_ge(s_z, 2 * j + 1)
                            s, k0 = 2 * half + (t - at) // 2, 2 * ((t - at) % 2)
                            for k in range(k0, k0 + 2):
                                mm = pe.matmul(po[:, (s % 2) * DM:(s % 2 + 1) * DM], gate[:, par, k, s * P:(s + 1) * P],
                                               w_out[:, k, :], start=(k == 0), stop=(k == DC - 1))
                            if t == at + 3:
                                mm.then_inc(s_wo, 1)
                    for k, at in ((0, 52), (1, 54)):
                        if t == at:
                            pe.wait_ge(s_hid, j + 1)
                            if k == 0:
                                pe.wait_ge(s_z, 2 * j + 2)
                            else:
                                pe.wait_ge(s_hte, 2 * j + 1)
                            for s in range(SUB):
                                mm = pe.transpose(po[:, s * P:(s + 1) * P], hid[:, s, k * P:(k + 1) * P], ident[:])
                            mm.then_inc(s_ht, 1)
                    if t == 57:
                        pe.wait_ge(s_hte, 2 * j + 2)
                        for k in range(KC):
                            mm = pe.matmul(po[:], rw1[:, k, :], ht[:, k, :], start=(k == 0), stop=(k == KC - 1))
                        mm.then_inc(s_rh, 1)
                    if t == 61:
                        pe.wait_ge(s_rs, j + 1)
                        pe.matmul(po[0:E, :], rw2[:], ht[:, 0, :], start=True, stop=True).then_inc(s_w2, 1)

                def step(i, par, has_prev, has_cur, has_next):
                    for t in range(GROUPS):
                        if has_cur and t + AHEAD < GROUPS:
                            spread_dt(t + AHEAD, i, par)
                        elif has_next:
                            spread_dt(t + AHEAD - GROUPS, i + 1, 1 - par)
                        if has_cur and t + 1 < GROUPS:
                            spread_u(t + 1, i, par)
                        elif has_next:
                            spread_u(0, i + 1, 1 - par)
                        if has_cur:
                            prep(64 + t, i, par)
                        if has_next:
                            prep(t, i + 1, 1 - par)
                        if t % 4 == 1:
                            quad = (t - 9) // 4
                            if quad < 0 and has_prev:
                                sum_states(QUADS + quad, i - 1)
                            elif quad >= 0 and has_cur:
                                sum_states(quad, i)
                        if has_prev:
                            post(t, i - 1, 1 - par)

                for t in range(GROUPS):
                    prep(t, 0, 0)
                for t in range(AHEAD):
                    spread_dt(t, 0, 0)
                spread_u(0, 0, 0)
                all_steps(pe, step)

            @block.scalar
            def _(act):
                def prep(t, i, par):
                    def bank(n):
                        return pp[:, (par + n) % 2, :]

                    if t == 10:
                        act.wait_ge(s_pw, i + 1)
                        act.wait_ge(s_st, 4 * i + 4)
                        for s in range(SUB):
                            ins = act.activation(xt[:, s, :], xt[:, s, :], ACT.Identity, scale=rs[:, SUB + s:SUB + s + 1],
                                                 bias=nm[:, s:s + 1])
                        ins.then_inc(s_xn, 1)
                    for k in range(KC):
                        if t == 13 + k:
                            act.wait_ge(s_pp, 17 * i + k + 1)
                            if k == 0:
                                atleast(act, s_pp, 17 * i - 7)
                            act.copy(xnt[:, k, :], bank(k)).then_inc(s_ev, 1)
                    for m in range(2 * DC):
                        if t == XS_AT + 1 + 2 * m:
                            act.wait_ge(s_pp, 17 * i + 3 + m)
                            if m < DC:
                                c = m
                                atleast(act, s_conv, 12 * i + 3 * (c - 1))
                                act.copy(xsp[:, c % 2, TAPS - 1:], bank(2 + m))
                                atleast(act, s_pp, 17 * i)
                                atleast(act, s_u, 4 * i + c - 3)
                                act.activation(xs[:, c, :], bank(2 + m), ACT.Identity, scale=cw[:, c, TAPS - 1:TAPS],
                                               bias=cb[:, c:c + 1]).then_inc(s_ev, 1)
                            else:
                                if m == DC:
                                    atleast(act, s_wo, 2 * (i - 1))
                                act.copy(gate[:, par, m - DC, :], bank(2 + m)).then_inc(s_ev, 1)
                    if t == SILU_AT:
                        act.wait_ge(s_conv, 12 * i + 12)
                        act.activation(xs[:], xs[:], ACT.Silu).then_inc(s_xs, 1)
                        act.wait_ge(s_ev, EV_ACT * i + 10)
                        act.activation(gate[:, par], gate[:, par], ACT.Silu).then_inc(s_sg, 1)
                    if t == BC_AT + 1:
                        act.wait_ge(s_pp, 17 * i + 11)
                        act.copy(bc[:], bank(10)).then_inc(s_ev, 1)
                    if t == BC_AT + 3:
                        act.wait_ge(s_pp, 17 * i + 12)
                        atleast(act, s_bx, 64 * (i - 1))
                        act.copy(b_rep[:, par, :], bank(11)).then_inc(s_ev, 1)
                    if t == BC_AT + 4:
                        act.wait_ge(s_pp, 17 * i + 13)
                        atleast(act, s_hc, 32 * (i - 1))
                        act.copy(c_rep[:, par, :], bank(12)).then_inc(s_ev, 1)
                    for c in range(DC):
                        at = DT_AT + DT_EVERY * c
                        if t == at + 2:
                            act.wait_ge(s_pp, 17 * i + 14 + c)
                            atleast(act, s_dt, 4 * i + c)
                            act.activation(spe[:], bank(13 + c), ACT.Abs).then_inc(s_sp, 1)
                            act.wait_ge(s_sp, 2 * (4 * i + c) + 1)
                            act.activation(spe[:], spe[:], ACT.Exp, scale=-1.0).then_inc(s_sp, 1)
                            act.wait_ge(s_sp, 2 * (4 * i + c) + 2)
                            act.activation(spl[:], spe[:], ACT.Ln, bias=1.0).then_inc(s_spl, 1)
                        if t == at + 12:
                            parts_free(c, i)
                            act.wait_ge(s_remd, 4 * i + c + 1)
                            extract(0, dtv, c)
                            extract(1, None, c, 0).then_inc(s_xd, 1)
                        if t == at + 16:
                            act.wait_ge(s_remu, 4 * i + c + 1)
                            extract(0, uv, c, 1)
                            extract(1, None, c, 1).then_inc(s_xu, 1)

                def parts_free(c, i):
                    if c >= 2:
                        act.wait_ge(d_stk[c - 2], STK_DMAS * (i + 1))
                    else:
                        atleast(act, d_stk[c + 2], STK_DMAS * i)

                def extract(part, src, c, tensor=0):
                    words = src[:, c % 2, :] if part == 0 else rem[:, tensor, :]
                    return act.copy(parts[:, c % 2, tensor, part, :], words.bitcast(BF16)[:, 1::2])

                def post(t, j, par):
                    if t == 34:
                        act.wait_ge(s_dp, 8 * j + 4)
                        for s in range(SUB):
                            ins = act.activation(z[:, s, :], z[:, s, :], ACT.Identity, scale=rs2[:, s:s + 1],
                                                 bias=nm2[:, s:s + 1])
                        ins.then_inc(s_z2, 1)
                    if t == 50:
                        act.wait_ge(s_dp, 8 * j + 8)
                        atleast(act, d_hid, 16 * j)
                        atleast(act, s_ht, 2 * j)
                        for s in range(SUB):
                            ins = act.activation(hid[:, s, :], z[:, s, :], ACT.Identity, scale=rs2[:, s:s + 1],
                                                 bias=nm2[:, s:s + 1])
                        ins.then_inc(s_hid, 1)
                    for k, at in ((0, 53), (1, 55)):
                        if t == at:
                            act.wait_ge(s_ht, 2 * j + k + 1)
                            if k == 0:
                                atleast(act, d_lg, 16 * j)
                                atleast(act, s_w2, j)
                            act.copy(ht[:, k, :], po[:]).then_inc(s_hte, 1)
                    if t == 59:
                        act.wait_ge(s_rh, j + 1)
                        act.activation(ht[:, 0, :], po[:], ACT.Silu).then_inc(s_rs, 1)
                    if t == 62:
                        act.wait_ge(s_w2, j + 1)
                        act.copy(ht[0:E, 1, :], po[0:E, :]).then_inc(s_lg, 1)

                def decays(t, i):
                    act.wait_ge(s_rdt, 64 * i + t + 1)
                    atleast(act, s_scan, 64 * i + t - 7)
                    act.activation(decay[:, t % 8, :], pdt[:, t % 2, :], ACT.Exp,
                                   scale=neg_a[:, group_column(t):group_column(t) + 1]).then_inc(s_exp, 1)

                def step(i, par, has_prev, has_cur, has_next):
                    for t in range(GROUPS):
                        if has_cur and t + AHEAD - 2 < GROUPS:
                            decays(t + AHEAD - 2, i)
                        elif has_next:
                            decays(t + AHEAD - 2 - GROUPS, i + 1)
                        if has_cur:
                            prep(64 + t, i, par)
                        if has_next:
                            prep(t, i + 1, 1 - par)
                        if has_prev:
                            post(t, i - 1, 1 - par)

                for t in range(GROUPS):
                    prep(t, 0, 0)
                for t in range(AHEAD - 2):
                    decays(t, 0)
                all_steps(act, step)

            @block.vector
            def _(v):
                def prep(t, i, par):
                    def bank(n):
                        return pp[:, (par + n) % 2, :]

                    if t == 0:
                        v.wait_ge(d_x, 16 * (i + 1))
                        for s in range(SUB):
                            ins = v.bn_stats(st[:, s, :], xt[:, s, :])
                        ins.then_inc(s_st, 1)
                    if t == 1:
                        v.wait_ge(s_st, 4 * i + 1)
                        v.memset(pad[:], 0)
                        for s in range(SUB):
                            ins = v.bn_aggr(mv[:, s, :], st[:, s, :])
                        ins.then_inc(s_st, 1)
                    if t == 2:
                        v.wait_ge(s_st, 4 * i + 2)
                        atleast(v, s_pw, i)
                        v.tensor_scalar(var[:, 0:SUB], mv[:, :, 1], EPS, None, ALU.add)
                        v.tensor_scalar(var[:, SUB:], mv[:, :, 1], 1.0 + EPS, EPS * EPS, ALU.mult, ALU.add).then_inc(s_st, 1)
                    if t == 8:
                        v.wait_ge(s_pw, i + 1)
                        atleast(v, s_xn, i)
                        v.scalar_tensor_tensor(out=nm[:], in0=mv[:, :, 0], scalar=-1.0, in1=rs[:, SUB:], op0=ALU.mult,
                                               op1=ALU.mult).then_inc(s_st, 1)
                    if t == 30:
                        v.tensor_copy(r1[:, par, :], rs[:, 0:SUB]).then_inc(s_r1, 1)
                    for c in range(DC):
                        if t == CONV_AT - 1 + 3 * c:
                            atleast(v, s_halo, 8 * i)
                            v.tensor_copy(xsp[:, c % 2, 0:TAPS - 1], halo[:, par, c, :]).then_inc(s_halo, 1)
                        for tap in range(TAPS - 1):
                            if t == CONV_AT + 3 * c + tap:
                                if tap == 0:
                                    v.wait_ge(s_ev, EV_ACT * i + 3 + c)
                                    v.wait_ge(s_halo, 8 * i + 2 * c + 1)
                                else:
                                    v.wait_ge(s_conv, 12 * i + 3 * c + tap)
                                v.scalar_tensor_tensor(out=xs[:, c, :], in0=xsp[:, c % 2, tap:tap + T],
                                                       scalar=cw[:, c, tap:tap + 1], in1=xs[:, c, :], op0=ALU.mult,
                                                       op1=ALU.add).then_inc(s_conv, 1)
                                if tap == 0:
                                    v.wait_ge(s_halo, 8 * i + 2 * c + 1)
                                    v.tensor_copy(halo[:, par, c, :], xsp[:, c % 2, T:]).then_inc(s_halo, 1)
                    for c in range(DC):
                        at = DT_AT + DT_EVERY * c
                        n = 4 * i + c
                        if t == at + 3:
                            v.wait_ge(s_sp, 2 * n + 2)
                            v.tensor_scalar(spt[:], spe[:], 1.0, -1.0, ALU.add, ALU.add).then_inc(s_spv, 1)
                        if t == at + 4:
                            v.wait_ge(s_spv, 3 * n + 1)
                            v.wait_ge(s_spl, n + 1)
                            v.tensor_tensor(spe[:], spe[:], spt[:], ALU.subtract).then_inc(s_spv, 1)
                        if t == at + 5:
                            v.wait_ge(s_spv, 3 * n + 2)
                            v.tensor_tensor(spl[:], spe[:], spl[:], ALU.add).then_inc(s_spv, 1)
                        if t == at + 6:
                            v.wait_ge(s_spv, 3 * n + 3)
                            atleast(v, s_lod, n - 1)
                            atleast(v, s_xd, n - 1)
                            atleast(v, s_u, n - 1)
                            v.scalar_tensor_tensor(out=dtv[:, c % 2, :], in0=bank(13 + c), scalar=0.0, in1=spl[:],
                                                   op0=ALU.max, op1=ALU.add).then_inc(s_dt, 1)

                def stats(src, base, j, at):
                    if at == 0:
                        for s in range(SUB):
                            ins = v.bn_stats(st2[:, s, :], src[:, s, :])
                        ins.then_inc(s_dp, 1)
                    if at == 1:
                        v.wait_ge(s_dp, 8 * j + base + 1)
                        v.memset(pad[:], 0)
                        for s in range(SUB):
                            ins = v.bn_aggr(mv2[:, s, :], st2[:, s, :])
                        ins.then_inc(s_dp, 1)
                    if at == 2:
                        v.wait_ge(s_dp, 8 * j + base + 2)
                        v.tensor_scalar(var2[:], mv2[:, :, 1], EPS, None, ALU.add).then_inc(s_dp, 1)

                def post(t, j, par):
                    for half, at in ((0, 15), (1, 24)):
                        if t == at:
                            v.wait_ge(s_wo, 2 * j + half + 1)
                            if half == 0:
                                v.wait_ge(d_xo, 16 * (j + 1))
                                v.wait_ge(s_r1, j + 1)
                                atleast(v, d_x1, 16 * j)
                                atleast(v, s_hid, j)
                            for s in (2 * half, 2 * half + 1):
                                ins = v.scalar_tensor_tensor(out=z[:, s, :], in0=xo[:, s, :], scalar=r1[:, par, s:s + 1],
                                                             in1=po[:, (s % 2) * DM:(s % 2 + 1) * DM], op0=ALU.mult,
                                                             op1=ALU.add)
                            ins.then_inc(s_z, 1)
                    for k in range(3):
                        if t == 25 + k:
                            if k == 0:
                                v.wait_ge(s_z, 2 * j + 2)
                            stats(z, 0, j, k)
                        if t == 40 + k:
                            if k == 0:
                                v.wait_ge(s_x1, j + 1)
                            stats(z, 4, j, k)
                    for n, at in ((0, 33), (1, 49)):
                        if t == at:
                            v.wait_ge(s_pw2, 2 * j + n + 1)
                            v.scalar_tensor_tensor(out=nm2[:], in0=mv2[:, :, 0], scalar=-1.0, in1=rs2[:], op0=ALU.mult,
                                                   op1=ALU.mult).then_inc(s_dp, 1)

                def inject(t, i, par):
                    v.wait_ge(s_ru, 64 * i + t + 1)
                    if t == 0:
                        v.wait_ge(s_ev, EV_ACT * (i + 1))
                    atleast(v, s_scan, 64 * i + t - 1)
                    v.tensor_tensor(bx[:, t % 2, :], pu[:, t % 2, :], b_rep[:, par, :], ALU.mult).then_inc(s_bx, 1)

                def scan(t, i, par):
                    v.wait_ge(s_exp, 64 * i + t + 1)
                    v.wait_ge(s_bx, 64 * i + t + 1)
                    if t % 2 == 0:
                        atleast(v, s_hc, 32 * i + t // 2 - 3)
                    if t == 0:
                        atleast(v, s_carry, 16 * (i - 1))
                    v.tensor_tensor_scan(h[:, t % 8, :], decay[:, t % 8, :], bx[:, t % 2, :], carry[:, par, t:t + 1],
                                         ALU.mult, ALU.add).then_inc(s_scan, 1)

                def save(quad, i, par):
                    v.wait_ge(s_scan, 64 * i + 4 * quad + 4)
                    b = 4 * (quad % 2)
                    v.tensor_copy(carry[:, par, 4 * quad:4 * quad + 4], h[:, b:b + 4, T - 1]).then_inc(s_carry, 1)

                def gated(c, i, par):
                    v.wait_ge(s_sum, 16 * i + 4 * c + 4)
                    v.wait_ge(s_sg, i + 1)
                    v.tensor_tensor(gate[:, par, c, :], py[:], gate[:, par, c, :], ALU.mult).then_inc(s_gate, 1)

                def step(i, par, has_prev, has_cur, has_next):
                    for t in range(GROUPS):
                        if has_cur:
                            inject(t, i, par)
                            prep(64 + t, i, par)
                        if has_next:
                            prep(t, i + 1, 1 - par)
                        if t == 7 and has_prev:
                            gated(3, i - 1, 1 - par)
                        if t % 16 == 7 and t > 16 and has_cur:
                            gated(t // 16 - 1, i, par)
                        if has_prev:
                            post(t, i - 1, 1 - par)
                        if t == 0 and has_prev:
                            scan(GROUPS - 1, i - 1, 1 - par)
                        elif t > 0 and has_cur:
                            scan(t - 1, i, par)
                        if t == 2 and has_prev:
                            save(QUADS - 1, i - 1, 1 - par)
                        elif t % 4 == 2 and t > 2 and has_cur:
                            save(t // 4 - 1, i, par)

                for t in range(GROUPS):
                    prep(t, 0, 0)
                all_steps(v, step)

            @block.gpsimd
            def _(pool):
                def prep(t, i, par):
                    if t == 4:
                        pool.wait_ge(s_st, 4 * i + 3)
                        atleast(pool, s_xn, i)
                        atleast(pool, s_r1, i)
                        pool.tensor_tensor(rs[:], var[:], mhalf[:], ALU.pow).then_inc(s_pw, 1)
                    for c in range(DC):
                        at = DT_AT + DT_EVERY * c
                        n = 4 * i + c
                        if t == at + 7:
                            pool.wait_ge(s_dt, n + 1)
                            pool.wait_ge(s_xs, i + 1)
                            atleast(pool, s_xu, n - 1)
                            pool.tensor_tensor(uv[:, c % 2, :], dtv[:, c % 2, :], xs[:, c, :], ALU.mult).then_inc(s_u, 1)
                        for k, src, s_rem, s_lo, s_ext in ((0, dtv, s_remd, s_lod, s_xd), (1, uv, s_remu, s_lou, s_xu)):
                            if t == at + 9 + 4 * k:
                                if k == 1:
                                    pool.wait_ge(s_u, n + 1)
                                atleast(pool, s_ext, n)
                                pool.tensor_tensor(rem[:, k, :], src[:, c % 2, :], src[:, c % 2, :].bitcast(BF16)[:, 1::2],
                                                   ALU.subtract).then_inc(s_rem, 1)
                            if t == at + 11 + 4 * k:
                                pool.wait_ge(s_rem, n + 1)
                                if c >= 2:
                                    pool.wait_ge(d_stk[c - 2], STK_DMAS * (i + 1))
                                else:
                                    atleast(pool, d_stk[c + 2], STK_DMAS * i)
                                pool.tensor_tensor(parts[:, c % 2, k, 2, :], rem[:, k, :], rem[:, k, :].bitcast(BF16)[:, 1::2],
                                                   ALU.subtract).then_inc(s_lo, 1)

                def post(t, j, par):
                    for n, at in ((0, 29), (1, 44)):
                        if t == at:
                            pool.wait_ge(s_dp, 8 * j + 4 * n + 3)
                            if n == 0:
                                atleast(pool, s_hid, j)
                            else:
                                pool.wait_ge(s_z2, j + 1)
                            pool.tensor_tensor(rs2[:], var2[:], mhalf[:, 0:SUB], ALU.pow).then_inc(s_pw2, 1)
                    if t == 36:
                        pool.wait_ge(s_z2, j + 1)
                        pool.tensor_tensor(z[:], z[:], xo[:], ALU.add).then_inc(s_x1, 1)

                def pair(m, i, par):
                    pool.wait_ge(s_scan, 64 * i + 2 * m + 2)
                    atleast(pool, s_sum, 16 * i + m // 2 - 1)
                    b = (2 * m) % 8
                    pool.tensor_tensor(hc[:, b:b + 2, :], h[:, b:b + 2, :],
                                       c_rep[:, par, :].unsqueeze(1).broadcast_to((P, 2, T)), ALU.mult).then_inc(s_hc, 1)

                def step(i, par, has_prev, has_cur, has_next):
                    for t in range(GROUPS):
                        if has_cur:
                            prep(64 + t, i, par)
                        if has_next:
                            prep(t, i + 1, 1 - par)
                        if has_prev:
                            post(t, i - 1, 1 - par)
                        if t == 1 and has_prev:
                            pair(GROUPS // 2 - 1, i - 1, 1 - par)
                        elif t % 2 == 1 and t > 1 and has_cur:
                            if t == 3:
                                pool.wait_ge(s_ev, EV_ACT * (i + 1))
                            pair(t // 2 - 1, i, par)

                for t in range(GROUPS):
                    prep(t, 0, 0)
                all_steps(pool, step)


def group_column(t):
    c, s, q = t // 16, t // 4 % 4, t % 4
    return 16 * c + 4 * q + s


def experts(nc, sem, B, S, ident, mhalf, outf, w1, w2, w3, hid_dram, acc_dram, lg_dram):
    R = B * E
    RING = 4
    ROUNDS = CAP // 8
    with ExitStack() as ctx:
        def sb(name, shape, dt=F32):
            return ctx.enter_context(nc.sbuf_tensor(name, shape, dt))

        def ps(name, shape):
            return ctx.enter_context(nc.psum_tensor(name, shape, F32))

        lg = sb("lg", [R, S])
        prob = sb("prob", [R, S])
        small = sb("small", [R, 8])
        vals = sb("vals", [R, CAP])
        ids = sb("ids", [R, CAP], U32)
        idf = sb("idf", [R, CAP])
        of_batch = sb("of_batch", [R, B])
        pick = sb("pick", [R, E])
        spread = sb("spread", [R, 2, B * CAP])
        rowid = sb("rowid", [P, E], U32)
        weight = sb("weight", [P, E])
        w1s = sb("w1s", [P, RING, KC, DFF])
        w2s = sb("w2s", [P, RING, KC, DFF])
        w3s = sb("w3s", [P, RING, FC, DM])
        taken = sb("taken", [P, RING, DM])
        tT = sb("tT", [P, RING, KC, P])
        act1 = sb("act1", [P, 2, DFF])
        yv = sb("yv", [P, RING, DM])
        x1 = sb("x1", [P, E, DM])
        comb = sb("comb", [P, E, DM])
        fst = sb("fst", [P, E, 6])
        fmv = sb("fmv", [P, E, 2])
        fvar = sb("fvar", [P, E])
        frs = sb("frs", [P, E])
        fnm = sb("fnm", [P, E])
        mh16 = sb("mh16", [P, E])
        pt = ps("pt", [P, 512])
        pg = ps("pg", [P, 2, DFF])
        pv = ps("pv", [P, 2, DFF])
        pY = ps("pY", [P, 2, 512])

        d_lg, s_k, s_ka, s_kt, s_ids = sem("lg_loaded"), sem("topk_step"), sem("topk_exp"), sem("topk_spread"), sem("ids_ready")
        d_wt = [sem(f"weights_loaded_{r}") for r in range(RING)]
        d_tk = [sem(f"taken_loaded_{r}") for r in range(RING)]
        s_tr, s_tc, s_g, s_v = sem("taken_transposed"), sem("taken_copied"), sem("gate_product"), sem("value_product")
        s_sl, s_m, s_o, s_y = sem("gate_silu"), sem("gated_value"), sem("expert_product"), sem("expert_ready")
        d_add, d_x1, d_cb, d_fin = sem("combined"), sem("x1_loaded"), sem("combined_loaded"), sem("final_stored")
        s_f, s_fp, s_fa, s_fo = sem("final_step"), sem("final_pow"), sem("final_normalised"), sem("final_sum")

        def ring_loop(eng, run):
            run(0, True, False)
            with eng.Fori(1, E // RING - 1) as k:
                run(k * RING, False, False)
            run(E - RING, False, True)

        with nc.Block() as block:
            @block.sync
            def _(sp):
                sp.dma_start(lg[:], lg_dram).then_inc(d_lg, 16)

                def load(e0, first, last):
                    for r in range(RING):
                        e = e0 + r
                        if not first:
                            sp.wait_ge(s_o, e0 + r - RING + 1)
                        for w, dst in ((w1, w1s), (w2, w2s), (w3, w3s)):
                            sp.dma_start(dst[:, r], w[bass.ds(e, 1)].rearrange("o (c p) f -> p (o c) f", p=P)).then_inc(d_wt[r], 16)

                ring_loop(sp, load)

            @block.vector
            def _(v):
                n = [0]

                def link(ins):
                    n[0] += 1
                    ins.then_inc(s_k, 1)
                    v.wait_ge(s_k, n[0])

                v.memset(mh16[:], -0.5)
                v.tensor_tensor(pick[:], ident[0:R, 0:E], ident[0:R, E:2 * E], ALU.add)
                for b in range(B):
                    v.tensor_reduce(of_batch[:, b:b + 1], ident[0:R, b * E:(b + 1) * E], AX.X, ALU.add)
                v.wait_ge(d_lg, 16)
                link(v.tensor_reduce(small[:, 0:1], lg[:], AX.X, ALU.max))
                link(v.tensor_scalar(small[:, 1:2], small[:, 0:1], -1.0, None, ALU.mult))
                v.wait_ge(s_ka, 1)
                link(v.reciprocal(small[:, 3:4], small[:, 2:3]))
                link(v.tensor_scalar(prob[:], prob[:], small[:, 3:4], None, ALU.mult))
                for r in range(ROUNDS):
                    eight = vals[:, 8 * r:8 * r + 8]
                    link(v.max(eight, prob[:]))
                    v.max_index(ids[:, 8 * r:8 * r + 8], eight, prob[:])
                    link(v.match_replace(prob[:], eight, prob[:], -1.0))
                link(v.tensor_reduce(small[:, 4:5], vals[:], AX.X, ALU.add))
                link(v.tensor_scalar(small[:, 4:5], small[:, 4:5], 1e-9, None, ALU.add))
                link(v.reciprocal(small[:, 5:6], small[:, 4:5]))
                link(v.tensor_copy(idf[:], ids[:]))
                for b in range(B):
                    cols = slice(b * CAP, (b + 1) * CAP)
                    v.tensor_scalar(spread[:, 0, cols], idf[:], float(b * S), of_batch[:, b:b + 1], ALU.add, ALU.mult)
                    ins = v.tensor_scalar(spread[:, 1, cols], vals[:], small[:, 5:6], of_batch[:, b:b + 1], ALU.mult, ALU.mult)
                link(ins)
                v.wait_ge(s_kt, 1)
                v.tensor_copy(rowid[:], pg[:, 0, 0:E])
                v.tensor_copy(weight[:], pg[:, 1, 0:E]).then_inc(s_ids, 1)

                def ffn(e0, first, last):
                    for r in range(RING):
                        e = e0 + r
                        v.wait_ge(s_sl, e + 1)
                        v.wait_ge(s_v, e + 1)
                        v.tensor_tensor(act1[:, r % 2, :], act1[:, r % 2, :], pv[:, r % 2, :], ALU.mult).then_inc(s_m, 1)

                ring_loop(v, ffn)

                v.wait_ge(d_cb, 16 * E)
                for e in range(E):
                    ins = v.bn_stats(fst[:, e, :], comb[:, e, :])
                ins.then_inc(s_f, 1)
                v.wait_ge(s_f, 1)
                for e in range(E):
                    ins = v.bn_aggr(fmv[:, e, :], fst[:, e, :])
                ins.then_inc(s_f, 1)
                v.wait_ge(s_f, 2)
                v.tensor_scalar(fvar[:], fmv[:, :, 1], EPS, None, ALU.add).then_inc(s_f, 1)
                v.wait_ge(s_fp, 1)
                v.scalar_tensor_tensor(out=fnm[:], in0=fmv[:, :, 0], scalar=-1.0, in1=frs[:], op0=ALU.mult,
                                       op1=ALU.mult).then_inc(s_f, 1)
                v.wait_ge(d_x1, 16 * E)
                for e in range(E):
                    v.wait_ge(s_fa, e + 1)
                    v.tensor_tensor(comb[:, e, :], comb[:, e, :], x1[:, e, :], ALU.add).then_inc(s_fo, 1)

            @block.scalar
            def _(act):
                act.wait_ge(s_k, 2)
                act.activation(prob[:], lg[:], ACT.Exp, bias=small[:, 1:2], accum_out=small[:, 2:3]).then_inc(s_ka, 1)

                def ffn(e0, first, last):
                    for r in range(RING):
                        e = e0 + r
                        act.wait_ge(s_tr, e + 1)
                        if not first:
                            act.wait_ge(s_v, e - RING + 1)
                        act.copy(tT[:, r], pt[:, 0:KC * P]).then_inc(s_tc, 1)
                        act.wait_ge(s_g, e + 1)
                        if not (first and r < 2):
                            act.wait_ge(s_o, e - 1)
                        act.activation(act1[:, r % 2, :], pg[:, r % 2, :], ACT.Silu).then_inc(s_sl, 1)
                        if not (first and r == 0):
                            weighted(e - 1, (r - 1) % RING, first and r == 0, first)

                def weighted(e, r, skip, first):
                    act.wait_ge(s_o, e + 1)
                    if not first:
                        act.wait_ge(d_add, 16 * (e - RING + 1))
                    act.activation(yv[:, r, :], pY[:, r % 2, 0:DM], ACT.Identity,
                                   scale=weight[:, bass.ds(e, 1)]).then_inc(s_y, 1)

                ring_loop(act, ffn)
                weighted(E - 1, RING - 1, False, False)

                act.wait_ge(s_f, 4)
                for e in range(E):
                    act.activation(comb[:, e, :], comb[:, e, :], ACT.Identity, scale=frs[:, e:e + 1],
                                   bias=fnm[:, e:e + 1]).then_inc(s_fa, 1)

            @block.tensor
            def _(pe):
                pe.wait_ge(s_k, 5 + 2 * ROUNDS + 4)
                for k in range(2):
                    mm = pe.matmul(pg[:, k, 0:E], spread[:, k, :], pick[:], start=True, stop=True)
                mm.then_inc(s_kt, 1)

                def transposed(e, r, first):
                    pe.wait_ge(d_tk[r], 16 * e_round(e, r))
                    if not first:
                        pe.wait_ge(s_tc, e)
                    for k in range(KC):
                        mm = pe.transpose(pt[:, k * P:(k + 1) * P], taken[:, r, k * P:(k + 1) * P], ident[:])
                    mm.then_inc(s_tr, 1)

                def e_round(e, r):
                    if isinstance(e, int):
                        return e // RING + 1
                    return (e - r) // RING + 1

                def product(e, r):
                    pe.wait_ge(s_m, e + 1)
                    if not (isinstance(e, int) and e < 2):
                        pe.wait_ge(s_y, e - 1)
                    for f in range(FC):
                        mm = pe.matmul(pY[:, r % 2, 0:DM], act1[:, r % 2, f * P:(f + 1) * P], w3s[:, r, f, :],
                                       start=(f == 0), stop=(f == FC - 1))
                    mm.then_inc(s_o, 1)

                def ffn(e0, first, last):
                    for r in range(RING):
                        e = e0 + r
                        if first and r == 0:
                            pe.wait_ge(s_ids, 1)
                            transposed(0, 0, True)
                        pe.wait_ge(d_wt[r], 48 * (1 if first else (e0 // RING + 1)))
                        pe.wait_ge(s_tc, e + 1)
                        if not (first and r < 2):
                            pe.wait_ge(s_m, e - 1)
                        for w, bank, s_w in ((w1s, pg, s_g), (w2s, pv, s_v)):
                            for f in range(FC):
                                for k in range(KC):
                                    mm = pe.matmul(bank[:, r % 2, f * P:(f + 1) * P], w[:, r, k, f * P:(f + 1) * P],
                                                   tT[:, r, k, :], start=(k == 0), stop=(k == KC - 1))
                            mm.then_inc(s_w, 1)
                        if not (last and r == RING - 1):
                            transposed(e + 1, (r + 1) % RING, False)
                        if not (first and r == 0):
                            product(e - 1, (r - 1) % RING)

                ring_loop(pe, ffn)
                product(E - 1, RING - 1)

            @block.gpsimd
            def _(pool):
                def rows_of(e):
                    return bass.IndirectOffsetOnAxis(ap=rowid[:, e:e + 1], axis=0)

                pool.wait_ge(s_ids, 1)

                def take(e):
                    if e >= RING:
                        pool.wait_ge(s_tr, e - RING + 1)
                    pool.indirect_dma_start(taken[:, e % RING, :], None, hid_dram, rows_of(e)).then_inc(d_tk[e % RING], 16)

                for e in range(RING):
                    take(e)
                for e in range(E):
                    pool.indirect_dma_start(x1[:, e, :], None, outf, rows_of(e)).then_inc(d_x1, 16)
                for e in range(E):
                    pool.wait_ge(s_y, e + 1)
                    if e > 0:
                        pool.wait_ge(d_add, 16 * e)
                    pool.indirect_dma_start(acc_dram, rows_of(e), yv[:, e % RING, :], None,
                                            compute_op=ALU.add).then_inc(d_add, 16)
                    if e + RING < E:
                        take(e + RING)
                pool.wait_ge(d_add, 16 * E)
                for e in range(E):
                    pool.indirect_dma_start(comb[:, e, :], None, acc_dram, rows_of(e)).then_inc(d_cb, 16)
                pool.wait_ge(s_f, 3)
                pool.tensor_tensor(frs[:], fvar[:], mh16[:], ALU.pow).then_inc(s_fp, 1)
                pool.wait_ge(d_x1, 16 * E)
                for e in range(E):
                    pool.wait_ge(s_fo, e + 1)
                    if e > 0:
                        pool.wait_ge(d_fin, 16 * e)
                    pool.indirect_dma_start(outf, rows_of(e), comb[:, e, :], None).then_inc(d_fin, 16)
                pool.wait_ge(d_fin, 16 * E)


_INS = ['L0_attn_x', 'L0_attn_rms_w', 'L0_attn_W_in', 'L0_attn_conv_w', 'L0_attn_conv_b', 'L0_attn_W_x', 'L0_attn_W_dt',
        'L0_attn_A_log', 'L0_attn_W_out', 'L0_ffn_router_w1', 'L0_ffn_router_w2', 'L0_ffn_w1', 'L0_ffn_w2', 'L0_ffn_w3']


def kernel(**inputs):
    import numpy as _np
    import concourse.bacc as _bacc
    from concourse import mybir as _mybir
    from concourse.bass_utils import run_bass_kernel_spmd as _run

    nc = _bacc.Bacc("TRN2", target_bir_lowering=False, num_devices=1)
    arrays, args = {}, []
    for name in _INS:
        a = _np.ascontiguousarray(inputs[name])
        arrays[f"in_{name}_dram"] = a
        args.append(nc.dram_tensor(f"in_{name}_dram", a.shape, _mybir.dt.from_np(a.dtype), kind="ExternalInput").ap())
    out = nc.dram_tensor("out_dram", inputs['L0_attn_x'].shape, _mybir.dt.float32, kind="ExternalOutput").ap()
    sandwich(nc, *args, out)
    r = _run(nc, [arrays], core_ids=[0])
    return r.results[0]["out_dram"]
```

```python
from contextlib import ExitStack

import concourse.bass as bass
from concourse import mybir

ALU = mybir.AluOpType
ACT = mybir.ActivationFunctionType
AX = mybir.AxisListType
F32 = mybir.dt.float32
BF16 = mybir.dt.bfloat16
U32 = mybir.dt.uint32

P = 128
T = 512
SUB = T // P
DM = 256
DI = 512
NS = 16
TAPS = 4
KC = DM // P
DC = DI // P
GROUPS = DI // 8
QUADS = GROUPS // 4
EPS = 1e-5
ROUTER = 128
E = 16
DFF = 512
CAP = 64
FC = DFF // P
CW = DM + 4
AHEAD = 4
PARTS = 3
STK_DMAS = 4 * PARTS * 16

PREP = dict(
    pe_turn=(5, 9), act_turn=(4, 7), pe_in=(10, 11, 13, 14, 15, 17, 18, 19, 24, 26, 39, 40, 51, 52, 66, 67),
    act_in=(12, 16, 18, 21, 28, 42, 57, 69), conv=(14, 17, 20, 23), silu=25, pe_bc=38, act_bc=40, pe_b=42,
    act_b=42, pe_c=44, act_c=43, pe_dt=(32, 34, 35, 36, 46, 47, 48, 50, 54, 55, 56, 58, 59, 60, 62, 64),
    act_dt=(35, 52, 60, 65), dve_dt=(40, 55, 63, 68), pool_dt=(44, 59, 66, 72), act_ext=(48, 62, 69, 75),
    stack=(53, 67, 74, 80), gate=78)
POST = dict(
    load=0, pe_out=(19, 20, 22, 23, 27, 28, 30, 31), dve_z=(25, 33), stats=(34, 48), pow=(35, 51), nm=(40,
    54), z2=41, x1=44, store_x1=50, hid=57, store_hid=60, pe_ht=(60, 63), act_ht=(61, 63), pe_w1=(69, 71),
    silu=72, pe_w2=74, act_lg=81, store_lg=72)
HEAD_AT = 48
GATED_AT = 8

USES = sorted([(PREP["pe_turn"][k], "turn", k) for k in range(KC)]
              + [(PREP["pe_in"][2 * m], "in", m) for m in range(2 * DC)]
              + [(PREP["pe_bc"], "bc", 0), (PREP["pe_b"], "b", 0), (PREP["pe_c"], "c", 0)]
              + [(PREP["pe_dt"][4 * c], "dt", c) for c in range(DC)])
NU = len(USES)


def use(name, k=0):
    return [(n, m) for _, n, m in USES].index((name, k))


def atleast(eng, sem, value):
    if isinstance(value, int) and value <= 0:
        return
    eng.wait_ge(sem, value)


def sandwich(nc, x, rms_w, W_in, conv_w, conv_b, W_x, W_dt, A_log, W_out, r_w1, r_w2, w1, w2, w3, out):
    B, S, _ = x.shape
    assert B == 2 and S % T == 0
    TILES = B * (S // T)
    xf = x.rearrange("b s d -> (b s) d")
    outf = out.rearrange("b s d -> (b s) d")
    hid_dram = nc.dram_tensor("hidden_scratch", [B * S, DM], F32, kind="Internal").ap()
    acc_dram = nc.dram_tensor("combine_scratch", [B * S, CW], F32, kind="Internal").ap()
    lg_dram = nc.dram_tensor("logits_scratch", [B * E, S], F32, kind="Internal").ap()

    tab_dram = nc.dram_tensor("token_table", [B * E * (P // (B * E)) * CAP, 1], U32, kind="Internal").ap()

    with ExitStack() as whole:
        def sem(name):
            return whole.enter_context(nc.semaphore(name))

        ident = whole.enter_context(nc.sbuf_tensor("ident", [P, P], F32))
        mhalf = whole.enter_context(nc.sbuf_tensor("mhalf", [P, 2 * SUB], F32))

        scan_layers(nc, sem, TILES, S, ident, mhalf, xf, outf, rms_w, W_in, conv_w, conv_b, W_x, W_dt, A_log, W_out,
                    r_w1, r_w2, hid_dram, acc_dram, lg_dram)
        experts(nc, sem, B, S, ident, mhalf, outf, w1, w2, w3, hid_dram, acc_dram, lg_dram, tab_dram)


def scan_layers(nc, sem, TILES, S, ident, mhalf, xf, outf, rms_w, W_in, conv_w, conv_b, W_x, W_dt, A_log, W_out,
                r_w1, r_w2, hid_dram, acc_dram, lg_dram):
    with ExitStack() as ctx:
        def sb(name, shape, dt=F32):
            return ctx.enter_context(nc.sbuf_tensor(name, shape, dt))

        def ps(name, shape):
            return ctx.enter_context(nc.psum_tensor(name, shape, F32))

        pdt = ps("pdt", [P, 2, T])
        pu = ps("pu", [P, 2, T])
        py = ps("py", [P, T])
        pp = ps("pp", [P, 2, T])
        po = ps("po", [P, T])

        w_in = sb("w_in", [P, KC, 2 * DI])
        w_dtx = sb("w_dtx", [P, DC, DI])
        w_bc = sb("w_bc", [P, DC, 2 * NS])
        w_out = sb("w_out", [P, DC, DM])
        rw1 = sb("rw1", [P, KC, ROUTER])
        rw2 = sb("rw2", [P, E])
        cw = sb("cw", [P, DC, TAPS])
        cb = sb("cb", [P, DC])
        rms = sb("rms", [P, KC])
        neg_a = sb("neg_a", [P, GROUPS])
        a_rows = sb("a_rows", [GROUPS, P])
        blk = sb("blk", [P, 32])
        sel_rep = sb("sel_rep", [P, 4, P], BF16)
        sel_sum = sb("sel_sum", [P, 4, 32])
        sel_b = sb("sel_b", [P, P])
        sel_c = sb("sel_c", [P, P])
        m8 = sb("m8", [P, 8])

        xt = sb("xt", [P, SUB, DM])
        xnt = sb("xnt", [P, KC, T])
        st = sb("st", [P, SUB, 6])
        mv = sb("mv", [P, SUB, 2])
        var = sb("var", [P, 2 * SUB])
        rs = sb("rs", [P, 2 * SUB])
        nm = sb("nm", [P, SUB])
        pad = sb("pad", [P, 1], U32)
        r1 = sb("r1", [P, 2, SUB])
        xsp = sb("xsp", [P, 2, T + TAPS - 1])
        halo = sb("halo", [P, 2, DC, TAPS - 1])
        xs = sb("xs", [P, DC, T])
        gate = sb("gate", [P, 2, DC, T])
        bc = sb("bc", [P, T])
        b_rep = sb("b_rep", [P, 2, T])
        c_rep = sb("c_rep", [P, 2, T])
        spe = sb("spe", [P, T])
        spl = sb("spl", [P, T])
        spt = sb("spt", [P, T])
        spr = sb("spr", [P, T])
        dtv = sb("dtv", [P, 2, T])
        uv = sb("uv", [P, 2, T])
        rem = sb("rem", [P, 2, T])
        parts = sb("parts", [P, 2, 2, PARTS, T], BF16)
        stk = sb("stk", [P, 2, 4 * DC, T], BF16)

        decay = sb("decay", [P, 8, T])
        bx = sb("bx", [P, 2, T])
        h = sb("h", [P, 8, T])
        hc = sb("hc", [P, 8, T])
        carry = sb("carry", [P, 2, GROUPS])

        xo = sb("xo", [P, SUB, DM])
        z = sb("z", [P, SUB, DM])
        st2 = sb("st2", [P, SUB, 6])
        pad2 = sb("pad2", [P, 1], U32)
        mv2 = sb("mv2", [P, SUB, 2])
        var2 = sb("var2", [P, SUB])
        rs2 = sb("rs2", [P, SUB])
        nm2 = sb("nm2", [P, SUB])
        hid = sb("hid", [P, SUB, DM])
        ht = sb("ht", [P, KC, T])

        d_w, d_a = sem("d_w"), sem("d_a")
        s_set, s_setv, s_sett, s_seta = sem("s_set"), sem("s_setv"), sem("s_sett"), sem("s_seta")

        wxs = h[:, 0:DC, :]
        wxt = h[:, 4:4 + DC, :]
        wdt = hc[:, 0:DC, :]
        zeros = decay[:].rearrange("p a b -> p (a b)")[:, 0:SUB * CW].rearrange("p (s d) -> p s d", d=CW)
        with nc.Block() as block:
            @block.sync
            def _(sp):
                sp.dma_start(wxs, W_x[:, 0:DI].rearrange("(c p) j -> p c j", p=P)).then_inc(d_w, 16)
                sp.dma_start(wdt, W_dt.rearrange("(c p) j -> p c j", p=P)).then_inc(d_w, 16)
                sp.dma_start(a_rows[:], A_log.rearrange("(g e) n -> g (e n)", e=8)).then_inc(d_a, 16)
                sp.dma_start(w_in[:], W_in.rearrange("(c p) j -> p c j", p=P)).then_inc(d_w, 16)
                sp.dma_start(w_bc[:], W_x[:, DI:DI + 2 * NS].rearrange("(c p) j -> p c j", p=P)).then_inc(d_w, 16)
                sp.dma_start(w_out[:], W_out.rearrange("(c p) j -> p c j", p=P)).then_inc(d_w, 16)
                sp.dma_start(rw1[:], r_w1.rearrange("(c p) j -> p c j", p=P)).then_inc(d_w, 16)
                sp.dma_start(rw2[:], r_w2).then_inc(d_w, 16)
                sp.dma_start(cw[:], conv_w.rearrange("(c p) o k -> p c (o k)", p=P)).then_inc(d_w, 16)
                sp.dma_start(cb[:], conv_b.rearrange("(c p) -> p c", p=P), allow_slow_non_contiguous=True).then_inc(d_w, 16)
                sp.dma_start(rms[:], rms_w.rearrange("(c p) -> p c", p=P), allow_slow_non_contiguous=True).then_inc(d_w, 16)
                sp.wait_ge(s_setv, 1)
                for r in range(0, acc_dram.shape[0], T):
                    sp.dma_start(acc_dram[r:r + T, :].rearrange("(s p) d -> p s d", p=P), zeros).then_inc(d_a, 16)
                sp.wait_ge(d_a, 16 * (1 + acc_dram.shape[0] // T))
                sp.wait_ge(d_w, 160)

            @block.gpsimd
            def _(pool):
                pool.memset(ident[:], 1.0).then_inc(s_set, 1)
                pool.memset(m8[:], 1.0).then_inc(s_set, 1)
                pool.wait_ge(s_set, 2)
                pool.affine_select(out=ident[:], in_=ident[:], compare_op=ALU.is_equal, fill=0.0, base=0,
                                   pattern=[[-1, P]], channel_multiplier=1).then_inc(s_set, 1)
                pool.affine_select(out=m8[:], in_=m8[:], compare_op=ALU.is_ge, fill=0.0, base=0,
                                   pattern=[[-16, 8]], channel_multiplier=1).then_inc(s_set, 1)
                pool.wait_ge(s_set, 4)
                pool.affine_select(out=m8[:], in_=m8[:], compare_op=ALU.is_ge, fill=0.0, base=15,
                                   pattern=[[16, 8]], channel_multiplier=-1).then_inc(s_set, 1)

            @block.vector
            def _(v):
                v.memset(zeros, 0.0).then_inc(s_setv, 1)
                v.memset(mhalf[:], -0.5)
                v.memset(carry[:], 0.0)
                v.memset(halo[:], 0.0)
                v.memset(sel_sum[:], 0.0).then_inc(s_setv, 1)
                v.wait_ge(s_set, 5)
                v.tensor_reduce(blk[:], ident[:].rearrange("p (k r) -> p r k", r=32), AX.X, ALU.add).then_inc(s_setv, 1)
                v.wait_ge(s_setv, 3)
                for s in range(4):
                    v.tensor_copy(sel_rep[:, s, :].rearrange("p (e n) -> p e n", n=NS),
                                  blk[:, 8 * s:8 * s + 8].unsqueeze(2).broadcast_to((P, 8, NS)))
                    v.tensor_copy(sel_sum[:, s, 8 * s:8 * s + 8], m8[:])
                v.tensor_copy(sel_b[:].rearrange("p (e n) -> p e n", n=NS),
                              blk[:, 0:NS].unsqueeze(1).broadcast_to((P, 8, NS)))
                v.tensor_copy(sel_c[:].rearrange("p (e n) -> p e n", n=NS),
                              blk[:, NS:2 * NS].unsqueeze(1).broadcast_to((P, 8, NS)))
                v.wait_ge(d_w, 160)
                for c in range(KC):
                    v.tensor_scalar(w_in[:, c, :], w_in[:, c, :], rms[:, c:c + 1], None, ALU.mult)
                v.wait_ge(s_seta, 1)
                v.tensor_scalar(neg_a[:], neg_a[:], -1.0, None, ALU.mult)

            @block.tensor
            def _(pe):
                pe.wait_ge(s_set, 5)
                pe.wait_ge(d_a, 16)
                pe.wait_ge(d_w, 160)
                pe.transpose(po[:, 0:GROUPS], a_rows[:], ident[0:GROUPS, 0:GROUPS]).then_inc(s_sett, 1)
                for j in range(DC):
                    if j >= 2:
                        pe.wait_ge(s_seta, j)
                    for k in range(DC):
                        mm = pe.transpose(pp[:, j % 2, k * P:(k + 1) * P], wxs[:, k, j * P:(j + 1) * P], ident[:])
                    mm.then_inc(s_sett, 1)
                for k in range(DC):
                    pe.wait_ge(s_seta, DC + 1 if k < 2 else DC + k)
                    for j in range(DC):
                        mm = pe.matmul(pp[:, k % 2, :], wxt[:, j, k * P:(k + 1) * P], wdt[:, j, :],
                                       start=(j == 0), stop=(j == DC - 1))
                    mm.then_inc(s_sett, 1)

            @block.scalar
            def _(act):
                act.wait_ge(s_sett, 1)
                act.activation(neg_a[:], po[:, 0:GROUPS], ACT.Exp).then_inc(s_seta, 1)
                for j in range(DC):
                    act.wait_ge(s_sett, 2 + j)
                    act.copy(wxt[:, j, :], pp[:, j % 2, :]).then_inc(s_seta, 1)
                for k in range(DC):
                    act.wait_ge(s_sett, 2 + DC + k)
                    act.copy(w_dtx[:, k, :], pp[:, k % 2, :]).then_inc(s_seta, 1)

        s_rdt, s_ru = sem("rep_dt_ready"), sem("rep_u_ready")
        s_exp, s_bx, s_scan, s_carry = sem("decay_ready"), sem("bx_ready"), sem("h_ready"), sem("carry_saved")
        s_hc, s_sum, s_gate = sem("hc_ready"), sem("y_summed"), sem("y_gated")
        d_x, s_st, s_pw, s_xn = sem("x_loaded"), sem("stats_step"), sem("rstd_ready"), sem("x_normalised")
        s_r1 = sem("r1_kept")
        s_pp, s_ev = sem("prep_bank_full"), sem("prep_bank_copied")
        s_halo, s_conv = sem("halo_step"), sem("conv_step")
        s_xs, s_sg = sem("xs_ready"), sem("gate_ready")
        s_sp, s_spl, s_spv, s_dt = sem("softplus_e"), sem("softplus_ln"), sem("softplus_step"), sem("dt_ready")
        s_u, s_remd, s_lod, s_remu, s_lou = (sem("u_ready"), sem("dt_rest"), sem("dt_last_part"), sem("u_rest"),
                                             sem("u_last_part"))
        s_xd, s_xu = sem("dt_parts_ready"), sem("u_parts_ready")
        d_stk = [sem(f"stack_loaded_{c}") for c in range(DC)]
        d_xo, s_wo, s_z, s_dp, s_pw2 = (sem("xo_loaded"), sem("out_product"), sem("z_ready"), sem("post_step"),
                                        sem("post_rstd"))
        s_z2, s_x1, d_x1, s_hid, d_hid = (sem("z_normalised"), sem("x1_ready"), sem("x1_stored"), sem("hid_ready"),
                                          sem("hid_stored"))
        s_ht, s_hte, s_rh, s_rs, s_w2, s_lg, d_lg = (sem("ht_bank"), sem("ht_copied"), sem("router_hidden"),
                                                     sem("router_silu"), sem("logits_bank"), sem("logits_ready"),
                                                     sem("logits_stored"))

        def rows(i, par):
            if isinstance(i, int):
                return par * S + (i // 2) * T
            return (i - par) * (T // 2) + par * S

        def all_steps(eng, run):
            run(0, 0, False, False, True, True)
            run(1, 1, False, True, True, True)
            with eng.Fori(0, (TILES - 4) // 2) as k:
                run(2 * k + 2, 0, True, True, True, True)
                run(2 * k + 3, 1, True, True, True, True)
            run(TILES - 2, 0, True, True, True, True)
            run(TILES - 1, 1, True, True, True, False)
            run(TILES, 0, True, True, False, False)
            run(TILES + 1, 1, True, False, False, False)

        with nc.Block() as block:
            @block.sync
            def _(sp):
                def load_x(i, par):
                    atleast(sp, s_pp, NU * (i - 1) + KC)
                    sp.dma_start(xt[:], xf[bass.ds(rows(i, par), T), :].rearrange("(s p) d -> p s d", p=P)).then_inc(d_x, 16)

                def stack(c, i):
                    made, used = 4 * i + c + 1, 64 * (i - 1) + 16 * (c + 1)
                    if not isinstance(i, int):
                        sp.compute_val(made)
                        sp.compute_val(used)
                    sp.wait_ge(s_xd, made)
                    sp.wait_ge(s_xu, made)
                    sp.wait_ge(s_lod, made)
                    sp.wait_ge(s_lou, made)
                    atleast(sp, s_rdt, used)
                    atleast(sp, s_ru, used)
                    for q in range(4):
                        for m in range(PARTS):
                            sp.dma_start(stk[32 * m:32 * m + 32, :, 4 * c + q, :],
                                         parts[32 * q:32 * q + 32, c % 2, :, m, :]).then_inc(d_stk[c], 16)

                def prep(t, i, par):
                    for c in range(DC):
                        if t == PREP["stack"][c]:
                            stack(c, i)

                def post(t, j, par):
                    if t == POST["load"]:
                        atleast(sp, s_x1, j)
                        sp.dma_start(xo[:], xf[bass.ds(rows(j, par), T), :].rearrange("(s p) d -> p s d", p=P)).then_inc(d_xo, 16)
                    if t == POST["store_x1"]:
                        sp.wait_ge(s_x1, j + 1)
                        sp.dma_start(outf[bass.ds(rows(j, par), T), :].rearrange("(s p) d -> p s d", p=P), z[:]).then_inc(d_x1, 16)
                    if t == POST["store_hid"]:
                        sp.wait_ge(s_hid, j + 1)
                        sp.dma_start(hid_dram[bass.ds(rows(j, par), T), :].rearrange("(s p) d -> p s d", p=P), hid[:]).then_inc(d_hid, 16)
                    if t == POST["store_lg"]:
                        col = (j // 2) * T if isinstance(j, int) else (j - par) * (T // 2)
                        if not isinstance(j, int):
                            sp.compute_val(col * 4)
                        sp.wait_ge(s_lg, j + 1)
                        sp.dma_start(lg_dram[par * E:(par + 1) * E, bass.ds(col, T)], ht[0:E, 1, :]).then_inc(d_lg, 16)

                def step(i, par, has_late, has_prev, has_cur, has_next):
                    for t in range(GROUPS):
                        if has_late:
                            post(64 + t, i - 2, par)
                        if has_cur:
                            prep(64 + t, i, par)
                        if has_next:
                            prep(t, i + 1, 1 - par)
                        if has_prev:
                            post(t, i - 1, 1 - par)
                        if has_next and t == 20:
                            if isinstance(i, int) and i + 2 >= TILES:
                                continue
                            load_x(i + 2, par)

                load_x(0, 0)
                for t in range(GROUPS):
                    prep(t, 0, 0)
                    if t == 20:
                        load_x(1, 1)
                all_steps(sp, step)
                sp.wait_ge(d_x1, 16 * TILES)
                sp.wait_ge(d_hid, 16 * TILES)
                sp.wait_ge(d_lg, 16 * TILES)

            @block.tensor
            def _(pe):
                def bank_free(n, i):
                    atleast(pe, s_ev, NU * i + n - 1)

                def spread_dt(t, i, par):
                    c, s, q = t // 16, t // 4 % 4, t % 4
                    if t % 16 == 0:
                        pe.wait_ge(d_stk[c], STK_DMAS * (i + 1))
                    atleast(pe, s_exp, 64 * i + t - 1)
                    pe.matmul(pdt[:, t % 2, :], sel_rep[0:96, s, :], stk[0:96, 0, 4 * c + q, :],
                              start=True, stop=True).then_inc(s_rdt, 1)

                def spread_u(t, i, par):
                    c, s, q = t // 16, t // 4 % 4, t % 4
                    atleast(pe, s_bx, 64 * i + t - 1)
                    pe.matmul(pu[:, t % 2, :], sel_rep[0:96, s, :], stk[0:96, 1, 4 * c + q, :],
                              start=True, stop=True).then_inc(s_ru, 1)

                def sum_states(quad, i):
                    c, s = quad // 4, quad % 4
                    pe.wait_ge(s_hc, 32 * i + 2 * quad + 2)
                    if s == 0:
                        atleast(pe, s_gate, 4 * i + c)
                    for q in range(4):
                        mm = pe.matmul(py[32 * q:32 * q + 32, :], sel_sum[:, s, :], hc[:, (4 * quad + q) % 8, :],
                                       start=(s == 0), stop=(s == 3), tile_position=(0, 32 * q))
                    mm.then_inc(s_sum, 1)

                def prep(t, i, par):
                    def bank(n):
                        return pp[:, (par + n) % 2, :]

                    for k in range(KC):
                        if t == PREP["pe_turn"][k]:
                            n = use("turn", k)
                            pe.wait_ge(s_xn, i + 1)
                            bank_free(n, i)
                            for s in range(SUB):
                                mm = pe.transpose(bank(n)[:, s * P:(s + 1) * P], xt[:, s, k * P:(k + 1) * P], ident[:])
                            mm.then_inc(s_pp, 1)
                    for m in range(2 * DC):
                        for k in range(KC):
                            if t == PREP["pe_in"][2 * m + k]:
                                n = use("in", m)
                                if k == 0:
                                    if m == 0:
                                        pe.wait_ge(s_ev, NU * i + KC)
                                    bank_free(n, i)
                                mm = pe.matmul(bank(n), w_in[:, k, m * P:(m + 1) * P], xnt[:, k, :],
                                               start=(k == 0), stop=(k == KC - 1))
                                if k == KC - 1:
                                    mm.then_inc(s_pp, 1)
                    if t == PREP["pe_bc"]:
                        n = use("bc")
                        pe.wait_ge(s_xs, i + 1)
                        bank_free(n, i)
                        for k in range(DC):
                            mm = pe.matmul(bank(n)[32 * k:32 * k + 32, :], w_bc[:, k, :], xs[:, k, :],
                                           start=True, stop=True, tile_position=(0, 32 * k))
                        mm.then_inc(s_pp, 1)
                    for name, sel in (("b", sel_b), ("c", sel_c)):
                        if t == PREP["pe_" + name]:
                            n = use(name)
                            pe.wait_ge(s_ev, NU * i + use("bc") + 1)
                            bank_free(n, i)
                            pe.matmul(bank(n), sel[:], bc[:], start=True, stop=True).then_inc(s_pp, 1)
                    for c in range(DC):
                        for k in range(DC):
                            if t == PREP["pe_dt"][DC * c + k]:
                                n = use("dt", c)
                                if k == 0:
                                    pe.wait_ge(s_xs, i + 1)
                                    bank_free(n, i)
                                mm = pe.matmul(bank(n), w_dtx[:, k, c * P:(c + 1) * P], xs[:, k, :],
                                               start=(k == 0), stop=(k == DC - 1))
                                if k == DC - 1:
                                    mm.then_inc(s_pp, 1)

                def post(t, j, par):
                    for step in range(8):
                        if t == POST["pe_out"][step]:
                            half = step // 4
                            if step == 0:
                                pe.wait_ge(s_gate, 4 * j + 4)
                                atleast(pe, s_lg, j)
                            if step == 4:
                                pe.wait_ge(s_z, 2 * j + 1)
                            for n in range(2 * (step % 4), 2 * (step % 4) + 2):
                                s, k = 2 * half + n // DC, n % DC
                                mm = pe.matmul(po[:, (s % 2) * DM:(s % 2 + 1) * DM], gate[:, par, k, s * P:(s + 1) * P],
                                               w_out[:, k, :], start=(k == 0), stop=(k == DC - 1))
                            if step % 4 == 3:
                                mm.then_inc(s_wo, 1)
                    for k, at in enumerate(POST["pe_ht"]):
                        if t == at:
                            pe.wait_ge(s_hid, j + 1)
                            if k == 0:
                                pe.wait_ge(s_z, 2 * j + 2)
                            else:
                                pe.wait_ge(s_hte, 2 * j + 1)
                            for s in range(SUB):
                                mm = pe.transpose(po[:, s * P:(s + 1) * P], hid[:, s, k * P:(k + 1) * P], ident[:])
                            mm.then_inc(s_ht, 1)
                    for k in range(KC):
                        if t == POST["pe_w1"][k]:
                            if k == 0:
                                pe.wait_ge(s_hte, 2 * j + 2)
                            mm = pe.matmul(po[:], rw1[:, k, :], ht[:, k, :], start=(k == 0), stop=(k == KC - 1))
                            if k == KC - 1:
                                mm.then_inc(s_rh, 1)
                    if t == POST["pe_w2"]:
                        pe.wait_ge(s_rs, j + 1)
                        pe.matmul(po[0:E, :], rw2[:], ht[:, 0, :], start=True, stop=True).then_inc(s_w2, 1)

                def step(i, par, has_late, has_prev, has_cur, has_next):
                    for t in range(GROUPS):
                        if has_cur and t + 1 < GROUPS:
                            spread_u(t + 1, i, par)
                        elif has_next:
                            spread_u(0, i + 1, 1 - par)
                        if has_late:
                            post(64 + t, i - 2, par)
                        if has_cur:
                            prep(64 + t, i, par)
                        if has_next:
                            prep(t, i + 1, 1 - par)
                        if t % 4 == 1:
                            quad = (t - 9) // 4
                            if quad < 0 and has_prev:
                                sum_states(QUADS + quad, i - 1)
                            elif quad >= 0 and has_cur:
                                sum_states(quad, i)
                        if has_prev:
                            post(t, i - 1, 1 - par)
                        if has_cur and t + AHEAD < GROUPS:
                            spread_dt(t + AHEAD, i, par)
                        elif has_next:
                            spread_dt(t + AHEAD - GROUPS, i + 1, 1 - par)

                for t in range(GROUPS):
                    prep(t, 0, 0)
                for t in range(AHEAD):
                    spread_dt(t, 0, 0)
                spread_u(0, 0, 0)
                all_steps(pe, step)

            @block.scalar
            def _(act):
                def head(t, i):
                    if t == 8:
                        act.wait_ge(s_pw, i + 1)
                        act.wait_ge(s_st, 4 * i + 4)
                        for s in range(SUB):
                            ins = act.activation(xt[:, s, :], xt[:, s, :], ACT.Identity, scale=rs[:, SUB + s:SUB + s + 1],
                                                 bias=nm[:, s:s + 1])
                        ins.then_inc(s_xn, 1)

                def prep(t, i, par):
                    def bank(n):
                        return pp[:, (par + n) % 2, :]

                    def filled(name, k=0):
                        act.wait_ge(s_pp, NU * i + use(name, k) + 1)
                        return bank(use(name, k))

                    for k in range(KC):
                        if t == PREP["act_turn"][k]:
                            atleast(act, s_pp, NU * (i - 1) + use("in", 2 * DC - 1) + 1)
                            act.copy(xnt[:, k, :], filled("turn", k)).then_inc(s_ev, 1)
                    for m in range(2 * DC):
                        if t == PREP["act_in"][m]:
                            full = filled("in", m)
                            if m < DC:
                                c = m
                                atleast(act, s_conv, 12 * i + 3 * (c - 1))
                                act.copy(xsp[:, c % 2, TAPS - 1:], full)
                                atleast(act, s_pp, NU * i)
                                atleast(act, s_u, 4 * i + c - 3)
                                act.activation(xs[:, c, :], full, ACT.Identity, scale=cw[:, c, TAPS - 1:TAPS],
                                               bias=cb[:, c:c + 1]).then_inc(s_ev, 1)
                            else:
                                if m == DC:
                                    atleast(act, s_wo, 2 * (i - 1))
                                act.copy(gate[:, par, m - DC, :], full).then_inc(s_ev, 1)
                    if t == PREP["silu"]:
                        act.wait_ge(s_conv, 12 * i + 12)
                        act.activation(xs[:], xs[:], ACT.Silu).then_inc(s_xs, 1)
                    if t == PREP["gate"]:
                        act.wait_ge(s_ev, NU * i + use("in", 2 * DC - 1) + 1)
                        act.activation(gate[:, par], gate[:, par], ACT.Silu).then_inc(s_sg, 1)
                    if t == PREP["act_bc"]:
                        act.copy(bc[:], filled("bc")).then_inc(s_ev, 1)
                    if t == PREP["act_b"]:
                        full = filled("b")
                        atleast(act, s_bx, 64 * (i - 1))
                        act.copy(b_rep[:, par, :], full).then_inc(s_ev, 1)
                    if t == PREP["act_c"]:
                        full = filled("c")
                        atleast(act, s_hc, 32 * (i - 1))
                        act.copy(c_rep[:, par, :], full).then_inc(s_ev, 1)
                    for c in range(DC):
                        if t == PREP["act_dt"][c]:
                            full = filled("dt", c)
                            atleast(act, s_dt, 4 * i + c)
                            act.activation(spr[:], full, ACT.Relu)
                            act.activation(spe[:], full, ACT.Abs).then_inc(s_ev, 1)
                        if t == PREP["act_dt"][c] + 1:
                            act.wait_ge(s_ev, NU * i + use("dt", c) + 1)
                            act.activation(spe[:], spe[:], ACT.Exp, scale=-1.0).then_inc(s_sp, 1)
                            act.wait_ge(s_sp, 4 * i + c + 1)
                            act.activation(spl[:], spe[:], ACT.Ln, bias=1.0).then_inc(s_spl, 1)
                        if t == PREP["act_ext"][c]:
                            parts_free(c, i)
                            act.wait_ge(s_remd, 4 * i + c + 1)
                            extract(0, dtv, c)
                            extract(1, None, c, 0).then_inc(s_xd, 1)
                        if t == PREP["act_ext"][c] + 2:
                            act.wait_ge(s_remu, 4 * i + c + 1)
                            extract(0, uv, c, 1)
                            extract(1, None, c, 1).then_inc(s_xu, 1)

                def parts_free(c, i):
                    if c >= 2:
                        act.wait_ge(d_stk[c - 2], STK_DMAS * (i + 1))
                    else:
                        atleast(act, d_stk[c + 2], STK_DMAS * i)

                def extract(part, src, c, tensor=0):
                    words = src[:, c % 2, :] if part == 0 else rem[:, tensor, :]
                    return act.copy(parts[:, c % 2, tensor, part, :], words.bitcast(BF16)[:, 1::2])

                def post(t, j, par):
                    if t == POST["z2"]:
                        act.wait_ge(s_dp, 8 * j + 4)
                        for s in range(SUB):
                            ins = act.activation(z[:, s, :], z[:, s, :], ACT.Identity, scale=rs2[:, s:s + 1],
                                                 bias=nm2[:, s:s + 1])
                        ins.then_inc(s_z2, 1)
                    if t == POST["hid"]:
                        act.wait_ge(s_dp, 8 * j + 8)
                        atleast(act, d_hid, 16 * j)
                        atleast(act, s_ht, 2 * j)
                        for s in range(SUB):
                            ins = act.activation(hid[:, s, :], z[:, s, :], ACT.Identity, scale=rs2[:, s:s + 1],
                                                 bias=nm2[:, s:s + 1])
                        ins.then_inc(s_hid, 1)
                    for k, at in enumerate(POST["act_ht"]):
                        if t == at:
                            act.wait_ge(s_ht, 2 * j + k + 1)
                            if k == 0:
                                atleast(act, d_lg, 16 * j)
                                atleast(act, s_w2, j)
                            act.copy(ht[:, k, :], po[:]).then_inc(s_hte, 1)
                    if t == POST["silu"]:
                        act.wait_ge(s_rh, j + 1)
                        act.activation(ht[:, 0, :], po[:], ACT.Silu).then_inc(s_rs, 1)
                    if t == POST["act_lg"]:
                        act.wait_ge(s_w2, j + 1)
                        act.copy(ht[0:E, 1, :], po[0:E, :]).then_inc(s_lg, 1)

                def decays(t, i):
                    act.wait_ge(s_rdt, 64 * i + t + 1)
                    atleast(act, s_scan, 64 * i + t - 7)
                    act.activation(decay[:, t % 8, :], pdt[:, t % 2, :], ACT.Exp,
                                   scale=neg_a[:, group_column(t):group_column(t) + 1]).then_inc(s_exp, 1)

                def step(i, par, has_late, has_prev, has_cur, has_next):
                    for t in range(GROUPS):
                        if has_late:
                            post(64 + t, i - 2, par)
                        if has_cur and t + AHEAD < GROUPS:
                            decays(t + AHEAD, i)
                        elif has_next:
                            decays(t + AHEAD - GROUPS, i + 1)
                        if has_cur:
                            prep(64 + t, i, par)
                        if has_next:
                            prep(t, i + 1, 1 - par)
                        if has_next and not (isinstance(i, int) and i + 2 >= TILES):
                            head(t - HEAD_AT, i + 2)
                        if has_prev:
                            post(t, i - 1, 1 - par)

                for t in range(GROUPS - HEAD_AT):
                    head(t, 0)
                for t in range(GROUPS):
                    prep(t, 0, 0)
                    head(t - HEAD_AT, 1)
                for t in range(AHEAD):
                    decays(t, 0)
                all_steps(act, step)

            @block.vector
            def _(v):
                def head(t, i):
                    if t == 0:
                        v.wait_ge(d_x, 16 * (i + 1))
                        for s in range(SUB):
                            ins = v.bn_stats(st[:, s, :], xt[:, s, :])
                        ins.then_inc(s_st, 1)
                    if t == 1:
                        v.wait_ge(s_st, 4 * i + 1)
                        v.memset(pad[:], 0)
                        for s in range(SUB):
                            ins = v.bn_aggr(mv[:, s, :], st[:, s, :])
                        ins.then_inc(s_st, 1)
                    if t == 2:
                        v.wait_ge(s_st, 4 * i + 2)
                        atleast(v, s_pw, i)
                        v.tensor_scalar(var[:, 0:SUB], mv[:, :, 1], EPS, None, ALU.add)
                        v.tensor_scalar(var[:, SUB:], mv[:, :, 1], 1.0 + EPS, EPS * EPS, ALU.mult, ALU.add).then_inc(s_st, 1)
                    if t == 6:
                        v.wait_ge(s_pw, i + 1)
                        atleast(v, s_xn, i)
                        v.scalar_tensor_tensor(out=nm[:], in0=mv[:, :, 0], scalar=-1.0, in1=rs[:, SUB:], op0=ALU.mult,
                                               op1=ALU.mult).then_inc(s_st, 1)

                def prep(t, i, par):
                    if t == 30:
                        v.tensor_copy(r1[:, par, :], rs[:, 0:SUB]).then_inc(s_r1, 1)
                    for c in range(DC):
                        if t == PREP["conv"][c] - 1:
                            atleast(v, s_halo, 8 * i)
                            v.tensor_copy(xsp[:, c % 2, 0:TAPS - 1], halo[:, par, c, :]).then_inc(s_halo, 1)
                        for tap in range(TAPS - 1):
                            if t == PREP["conv"][c] + tap:
                                if tap == 0:
                                    v.wait_ge(s_ev, NU * i + use("in", c) + 1)
                                    v.wait_ge(s_halo, 8 * i + 2 * c + 1)
                                else:
                                    v.wait_ge(s_conv, 12 * i + 3 * c + tap)
                                v.scalar_tensor_tensor(out=xs[:, c, :], in0=xsp[:, c % 2, tap:tap + T],
                                                       scalar=cw[:, c, tap:tap + 1], in1=xs[:, c, :], op0=ALU.mult,
                                                       op1=ALU.add).then_inc(s_conv, 1)
                                if tap == 0:
                                    v.wait_ge(s_halo, 8 * i + 2 * c + 1)
                                    v.tensor_copy(halo[:, par, c, :], xsp[:, c % 2, T:]).then_inc(s_halo, 1)
                    for c in range(DC):
                        at = PREP["dve_dt"][c]
                        n = 4 * i + c
                        if t == at:
                            v.wait_ge(s_sp, n + 1)
                            v.tensor_scalar(spt[:], spe[:], 1.0, -1.0, ALU.add, ALU.add).then_inc(s_spv, 1)
                        if t == at + 1:
                            v.wait_ge(s_spv, 3 * n + 1)
                            v.wait_ge(s_spl, n + 1)
                            v.tensor_tensor(spe[:], spe[:], spt[:], ALU.subtract).then_inc(s_spv, 1)
                        if t == at + 2:
                            v.wait_ge(s_spv, 3 * n + 2)
                            v.tensor_tensor(spl[:], spe[:], spl[:], ALU.add).then_inc(s_spv, 1)
                        if t == at + 3:
                            v.wait_ge(s_spv, 3 * n + 3)
                            atleast(v, s_lod, n - 1)
                            atleast(v, s_xd, n - 1)
                            atleast(v, s_u, n - 1)
                            v.tensor_tensor(dtv[:, c % 2, :], spr[:], spl[:], ALU.add).then_inc(s_dt, 1)

                def stats(src, base, j, at):
                    if at == 0:
                        for s in range(SUB):
                            ins = v.bn_stats(st2[:, s, :], src[:, s, :])
                        ins.then_inc(s_dp, 1)
                    if at == 1:
                        v.wait_ge(s_dp, 8 * j + base + 1)
                        v.memset(pad2[:], 0)
                        for s in range(SUB):
                            ins = v.bn_aggr(mv2[:, s, :], st2[:, s, :])
                        ins.then_inc(s_dp, 1)
                    if at == 2:
                        v.wait_ge(s_dp, 8 * j + base + 2)
                        v.tensor_scalar(var2[:], mv2[:, :, 1], EPS, None, ALU.add).then_inc(s_dp, 1)

                def post(t, j, par):
                    for half, at in enumerate(POST["dve_z"]):
                        if t == at:
                            v.wait_ge(s_wo, 2 * j + half + 1)
                            if half == 0:
                                v.wait_ge(d_xo, 16 * (j + 1))
                                v.wait_ge(s_r1, j + 1)
                                atleast(v, d_x1, 16 * j)
                                atleast(v, s_hid, j)
                            for s in (2 * half, 2 * half + 1):
                                ins = v.scalar_tensor_tensor(out=z[:, s, :], in0=xo[:, s, :], scalar=r1[:, par, s:s + 1],
                                                             in1=po[:, (s % 2) * DM:(s % 2 + 1) * DM], op0=ALU.mult,
                                                             op1=ALU.add)
                            ins.then_inc(s_z, 1)
                    for k in range(3):
                        if t == POST["stats"][0] + k:
                            if k == 0:
                                v.wait_ge(s_z, 2 * j + 2)
                            stats(z, 0, j, k)
                        if t == POST["stats"][1] + k:
                            if k == 0:
                                v.wait_ge(s_x1, j + 1)
                            stats(z, 4, j, k)
                    for n, at in enumerate(POST["nm"]):
                        if t == at:
                            v.wait_ge(s_pw2, 2 * j + n + 1)
                            v.scalar_tensor_tensor(out=nm2[:], in0=mv2[:, :, 0], scalar=-1.0, in1=rs2[:], op0=ALU.mult,
                                                   op1=ALU.mult).then_inc(s_dp, 1)

                def inject(t, i, par):
                    v.wait_ge(s_ru, 64 * i + t + 1)
                    if t == 0:
                        v.wait_ge(s_ev, NU * i + use("b") + 1)
                    atleast(v, s_scan, 64 * i + t - 1)
                    v.tensor_tensor(bx[:, t % 2, :], pu[:, t % 2, :], b_rep[:, par, :], ALU.mult).then_inc(s_bx, 1)

                def scan(t, i, par):
                    v.wait_ge(s_exp, 64 * i + t + 1)
                    v.wait_ge(s_bx, 64 * i + t + 1)
                    if t % 2 == 0:
                        atleast(v, s_hc, 32 * i + t // 2 - 3)
                    if t == 0:
                        atleast(v, s_carry, 16 * (i - 1))
                    v.tensor_tensor_scan(h[:, t % 8, :], decay[:, t % 8, :], bx[:, t % 2, :], carry[:, par, t:t + 1],
                                         ALU.mult, ALU.add).then_inc(s_scan, 1)

                def save(quad, i, par):
                    v.wait_ge(s_scan, 64 * i + 4 * quad + 4)
                    b = 4 * (quad % 2)
                    v.tensor_copy(carry[:, par, 4 * quad:4 * quad + 4], h[:, b:b + 4, T - 1]).then_inc(s_carry, 1)

                def gated(c, i, par):
                    v.wait_ge(s_sum, 16 * i + 4 * c + 4)
                    v.wait_ge(s_sg, i + 1)
                    v.tensor_tensor(gate[:, par, c, :], py[:], gate[:, par, c, :], ALU.mult).then_inc(s_gate, 1)

                def step(i, par, has_late, has_prev, has_cur, has_next):
                    for t in range(GROUPS):
                        if has_late:
                            post(64 + t, i - 2, par)
                        if has_cur:
                            inject(t, i, par)
                            prep(64 + t, i, par)
                        if has_next:
                            prep(t, i + 1, 1 - par)
                        if has_next and not (isinstance(i, int) and i + 2 >= TILES):
                            head(t - HEAD_AT, i + 2)
                        if t == GATED_AT and has_prev:
                            gated(3, i - 1, 1 - par)
                        if t % 16 == GATED_AT and t > 16 and has_cur:
                            gated(t // 16 - 1, i, par)
                        if has_prev:
                            post(t, i - 1, 1 - par)
                        if t == 0 and has_prev:
                            scan(GROUPS - 1, i - 1, 1 - par)
                        elif t > 0 and has_cur:
                            scan(t - 1, i, par)
                        if t == 2 and has_prev:
                            save(QUADS - 1, i - 1, 1 - par)
                        elif t % 4 == 2 and t > 2 and has_cur:
                            save(t // 4 - 1, i, par)

                for t in range(GROUPS - HEAD_AT):
                    head(t, 0)
                for t in range(GROUPS):
                    prep(t, 0, 0)
                    head(t - HEAD_AT, 1)
                all_steps(v, step)

            @block.gpsimd
            def _(pool):
                def head(t, i):
                    if t == 3:
                        pool.wait_ge(s_st, 4 * i + 3)
                        atleast(pool, s_xn, i)
                        atleast(pool, s_r1, i)
                        pool.tensor_tensor(rs[:], var[:], mhalf[:], ALU.pow).then_inc(s_pw, 1)

                def prep(t, i, par):
                    for c in range(DC):
                        at = PREP["pool_dt"][c]
                        n = 4 * i + c
                        if t == at:
                            pool.wait_ge(s_dt, n + 1)
                            pool.wait_ge(s_xs, i + 1)
                            atleast(pool, s_xu, n - 1)
                            pool.tensor_tensor(uv[:, c % 2, :], dtv[:, c % 2, :], xs[:, c, :], ALU.mult).then_inc(s_u, 1)
                        for k, src, s_rem, s_lo, s_ext in ((0, dtv, s_remd, s_lod, s_xd), (1, uv, s_remu, s_lou, s_xu)):
                            if t == at + 1 + 2 * k:
                                if k == 1:
                                    pool.wait_ge(s_u, n + 1)
                                atleast(pool, s_ext, n)
                                pool.tensor_tensor(rem[:, k, :], src[:, c % 2, :], src[:, c % 2, :].bitcast(BF16)[:, 1::2],
                                                   ALU.subtract).then_inc(s_rem, 1)
                            if t == at + 2 + 2 * k:
                                pool.wait_ge(s_rem, n + 1)
                                if c >= 2:
                                    pool.wait_ge(d_stk[c - 2], STK_DMAS * (i + 1))
                                else:
                                    atleast(pool, d_stk[c + 2], STK_DMAS * i)
                                pool.tensor_tensor(parts[:, c % 2, k, 2, :], rem[:, k, :], rem[:, k, :].bitcast(BF16)[:, 1::2],
                                                   ALU.subtract).then_inc(s_lo, 1)

                def post(t, j, par):
                    for n, at in enumerate(POST["pow"]):
                        if t == at:
                            pool.wait_ge(s_dp, 8 * j + 4 * n + 3)
                            if n == 0:
                                atleast(pool, s_hid, j)
                            else:
                                pool.wait_ge(s_z2, j + 1)
                            pool.tensor_tensor(rs2[:], var2[:], mhalf[:, 0:SUB], ALU.pow).then_inc(s_pw2, 1)
                    if t == POST["x1"]:
                        pool.wait_ge(s_z2, j + 1)
                        pool.tensor_tensor(z[:], z[:], xo[:], ALU.add).then_inc(s_x1, 1)

                def pair(m, i, par):
                    pool.wait_ge(s_scan, 64 * i + 2 * m + 2)
                    atleast(pool, s_sum, 16 * i + m // 2 - 1)
                    b = (2 * m) % 8
                    pool.tensor_tensor(hc[:, b:b + 2, :], h[:, b:b + 2, :],
                                       c_rep[:, par, :].unsqueeze(1).broadcast_to((P, 2, T)), ALU.mult).then_inc(s_hc, 1)

                def step(i, par, has_late, has_prev, has_cur, has_next):
                    for t in range(GROUPS):
                        if has_late:
                            post(64 + t, i - 2, par)
                        if has_cur:
                            prep(64 + t, i, par)
                        if has_next:
                            prep(t, i + 1, 1 - par)
                        if has_next and not (isinstance(i, int) and i + 2 >= TILES):
                            head(t - HEAD_AT, i + 2)
                        if has_prev:
                            post(t, i - 1, 1 - par)
                        if t == 1 and has_prev:
                            pair(GROUPS // 2 - 1, i - 1, 1 - par)
                        elif t % 2 == 1 and t > 1 and has_cur:
                            if t == 3:
                                pool.wait_ge(s_ev, NU * i + use("c") + 1)
                            pair(t // 2 - 1, i, par)

                for t in range(GROUPS - HEAD_AT):
                    head(t, 0)
                for t in range(GROUPS):
                    prep(t, 0, 0)
                    head(t - HEAD_AT, 1)
                all_steps(pool, step)


def group_column(t):
    c, s, q = t // 16, t // 4 % 4, t % 4
    return 16 * c + 4 * q + s


def experts(nc, sem, B, S, ident, mhalf, outf, w1, w2, w3, hid_dram, acc_dram, lg_dram, tab_dram):
    R = B * E
    SEGS = P // R
    L = S // SEGS
    ROUNDS = CAP // 8
    RING = 8
    GROUP = 4
    TAKEN = -3.0e38
    with ExitStack() as ctx:
        def sb(name, shape, dt=F32):
            return ctx.enter_context(nc.sbuf_tensor(name, shape, dt))

        def ps(name, shape):
            return ctx.enter_context(nc.psum_tensor(name, shape, F32))

        lg = sb("lg", [P, L])
        lgx = sb("lgx", [P, L])
        best = sb("best", [P, CAP])
        place = sb("place", [P, CAP], U32)
        placef = sb("placef", [P, CAP])
        token = sb("token", [P, CAP], U32)
        mass = sb("mass", [P, 1])
        negm = sb("negm", [P, 1])
        seg0 = sb("seg0", [P, 1])
        second = sb("second", [P, 1])
        first_row = sb("first_row", [P, 1])
        cand = sb("cand", [R, SEGS * CAP])
        masses = sb("masses", [R, SEGS])
        tops = sb("tops", [R, SEGS])
        vals = sb("vals", [R, CAP])
        ids = sb("ids", [R, CAP], U32)
        idf = sb("idf", [R, CAP])
        small = sb("small", [R, 8])
        ramp = sb("ramp", [R, R])
        row_base = sb("row_base", [R, 1])
        of_batch = sb("of_batch", [R, B])
        pick = sb("pick", [R, E])
        spread = sb("spread", [R, 2, B * CAP])
        entry = sb("entry", [P, E], U32)
        rowid = sb("rowid", [P, E], U32)
        weight = sb("weight", [P, E])
        w1s = sb("w1s", [P, RING, KC, DFF])
        w2s = sb("w2s", [P, RING, KC, DFF])
        w3s = sb("w3s", [P, RING, FC, DM])
        taken = sb("taken", [P, 4, DM])
        tT = sb("tT", [P, 2, KC, P])
        act1 = sb("act1", [P, 2, DFF])
        x1 = sb("x1", [P, E, DM])
        comb = sb("comb", [P, E, CW])
        rowf = sb("rowf", [P, E])
        above = sb("above", [P, E])
        loser = sb("loser", [P, E])
        dest = sb("dest", [P, E], U32)
        fst = sb("fst", [P, E, 6])
        fmv = sb("fmv", [P, E, 2])
        fvar = sb("fvar", [P, E])
        frs = sb("frs", [P, E])
        fnm = sb("fnm", [P, E])
        pt = ps("pt", [P, 512])
        pg = ps("pg", [P, 2, DFF])
        pv = ps("pv", [P, 2, DFF])
        pY = ps("pY", [P, 2, 512])

        d_lg, s_k, s_ka, s_kt = sem("lg_loaded"), sem("selection_step"), sem("selection_exp"), sem("selection_spread")
        s_pos, d_tab, d_cand = sem("entries_ready"), sem("table_stored"), sem("candidates_loaded")
        s_tok, s_bit, s_lose, s_dest = sem("tokens_ready"), sem("bits_step"), sem("losers_step"), sem("dest_ready")
        FIRST = 1 + (R - 1).bit_length() + 2
        SEGMENTS_DONE = FIRST + 2 * ROUNDS + 1
        TOP_READY = SEGMENTS_DONE + 3
        ROWS_DONE = TOP_READY + 2 * ROUNDS - 1
        SPREAD_READY = ROWS_DONE + 9
        d_id = [sem(f"rowid_loaded_{r}") for r in range(4)]
        d_wt = [sem(f"weights_loaded_{r}") for r in range(RING)]
        d_tk = [sem(f"taken_loaded_{r}") for r in range(4)]
        s_tr, s_tc, s_g, s_v = sem("taken_transposed"), sem("taken_copied"), sem("gate_product"), sem("value_product")
        s_sl, s_m, s_o, s_y = sem("gate_silu"), sem("gated_value"), sem("expert_product"), sem("expert_ready")
        d_add, d_x1, d_fin = sem("combined"), sem("x1_loaded"), sem("final_stored")
        d_cb = [sem(f"combined_loaded_{g}") for g in range(E // GROUP)]
        s_f, s_fp, s_fn, s_fa, s_fo = (sem("final_stats_step"), sem("final_pow"), sem("final_mean"),
                                       sem("final_normalised"), sem("final_sum"))

        with nc.Block() as block:
            @block.sync
            def _(sp):
                def load(e):
                    if e >= RING:
                        sp.wait_ge(s_o, e - RING + 1)
                    for w, dst in ((w1, w1s), (w2, w2s), (w3, w3s)):
                        sp.dma_start(dst[:, e % RING], w[e].rearrange("(c p) f -> p c f", p=P)).then_inc(d_wt[e % RING], 16)

                for g in range(SEGS):
                    sp.dma_start(lg[R * g:R * (g + 1), :], lg_dram[:, g * L:(g + 1) * L]).then_inc(d_lg, 16)
                for e in range(2):
                    load(e)
                sp.wait_ge(s_k, SEGMENTS_DONE)
                sp.wait_ge(s_ka, 1)
                for g in range(SEGS):
                    sp.dma_start(cand[:, g * CAP:(g + 1) * CAP], best[R * g:R * (g + 1), :]).then_inc(d_cand, 16)
                    sp.dma_start(masses[:, g:g + 1], mass[R * g:R * (g + 1), :]).then_inc(d_cand, 16)
                sp.wait_ge(s_tok, 1)
                for g in range(SEGS):
                    sp.dma_start(tab_dram.rearrange("(r g k) o -> g r (k o)", g=SEGS, k=CAP)[g],
                                 token[R * g:R * (g + 1), :]).then_inc(d_tab, 16)
                sp.wait_ge(d_cand, 32 * SEGS)
                for e in range(2, 4):
                    load(e)
                sp.wait_ge(s_tr, 1)
                for e in range(4, E):
                    load(e)
                sp.wait_ge(d_tab, 16 * SEGS)

            @block.vector
            def _(v):
                n = [0]

                def link(ins):
                    n[0] += 1
                    ins.then_inc(s_k, 1)
                    v.wait_ge(s_k, n[0])

                for g in range(SEGS):
                    v.memset(seg0[R * g:R * (g + 1), :], float(g * L))
                v.tensor_reduce(second[:], ident[:].rearrange("p (g r) -> p g r", r=R)[:, :, E:R], AX.XY, ALU.add)
                v.tensor_tensor(pick[:], ident[0:R, 0:E], ident[0:R, E:2 * E], ALU.add)
                for b in range(B):
                    v.tensor_reduce(of_batch[:, b:b + 1], ident[0:R, b * E:(b + 1) * E], AX.X, ALU.add)
                v.memset(comb[:, :, DM:], 0.0).then_inc(s_bit, 1)
                v.wait_ge(s_bit, 1)
                for e in range(E):
                    v.memset(comb[:, e, DM:DM + 1], float(2 ** e))
                    ins = v.memset(above[:, e:e + 1], float(2 ** (e + 1)))
                ins.then_inc(s_bit, 1)
                link(v.memset(ramp[:, 0:1], 0.0))
                w = 1
                while w < R:
                    link(v.tensor_scalar(ramp[:, w:2 * w], ramp[:, 0:w], float(w * SEGS * CAP), None, ALU.add))
                    w *= 2
                v.tensor_scalar(first_row[:], second[:], float(S), seg0[:], ALU.mult, ALU.add)
                link(v.tensor_tensor(ramp[:], ramp[:], ident[0:R, 0:R], ALU.mult))
                link(v.tensor_reduce(row_base[:], ramp[:], AX.X, ALU.add))

                def rounds(values, places, src, after_first):
                    for r in range(ROUNDS):
                        eight = values[:, 8 * r:8 * r + 8]
                        link(v.max(eight, src[:]))
                        if r == 0:
                            after_first()
                        found = v.max_index(places[:, 8 * r:8 * r + 8], eight, src[:])
                        if r == ROUNDS - 1:
                            link(found)
                        else:
                            link(v.match_replace(src[:], eight, src[:], TAKEN))

                def minus_segment_maximum():
                    link(v.tensor_scalar(negm[:], best[:, 0:1], -1.0, None, ALU.mult))
                    v.wait_ge(s_ka, 1)

                v.wait_ge(d_lg, 16 * SEGS)
                rounds(best, place, lg, minus_segment_maximum)
                link(v.tensor_copy(placef[:], place[:]))
                v.tensor_scalar(token[:], placef[:], first_row[:], None, ALU.add).then_inc(s_tok, 1)

                v.wait_ge(d_cand, 32 * SEGS)
                v.tensor_copy(tops[:], cand[:].rearrange("p (g k) -> p g k", k=CAP)[:, :, 0])

                def minus_maximum():
                    link(v.tensor_scalar(small[:, 0:1], vals[:, 0:1], -1.0, None, ALU.mult))

                rounds(vals, ids, cand, minus_maximum)
                link(v.tensor_copy(idf[:], ids[:]))
                for b in range(B):
                    v.tensor_scalar(spread[:, 0, b * CAP:(b + 1) * CAP], idf[:], row_base[:], of_batch[:, b:b + 1],
                                    ALU.add, ALU.mult)
                v.wait_ge(s_ka, 3)
                link(v.tensor_tensor(masses[:], masses[:], tops[:], ALU.mult))
                link(v.tensor_reduce(small[:, 1:2], masses[:], AX.X, ALU.add))
                link(v.reciprocal(small[:, 2:3], small[:, 1:2]))
                link(v.tensor_scalar(vals[:], vals[:], small[:, 2:3], None, ALU.mult))
                link(v.tensor_reduce(small[:, 4:5], vals[:], AX.X, ALU.add))
                link(v.tensor_scalar(small[:, 4:5], small[:, 4:5], 1e-9, None, ALU.add))
                link(v.reciprocal(small[:, 5:6], small[:, 4:5]))
                for b in range(B):
                    ins = v.tensor_scalar(spread[:, 1, b * CAP:(b + 1) * CAP], vals[:], small[:, 5:6],
                                          of_batch[:, b:b + 1], ALU.mult, ALU.mult)
                link(ins)
                v.wait_ge(s_kt, 1)
                v.tensor_copy(entry[:], pg[:, 0, 0:E]).then_inc(s_pos, 1)
                v.tensor_copy(weight[:], pg[:, 1, 0:E]).then_inc(s_pos, 1)

                for e in range(E):
                    v.wait_ge(s_sl, e + 1)
                    v.wait_ge(s_v, e + 1)
                    v.tensor_tensor(act1[:, e % 2, :], act1[:, e % 2, :], pv[:, e % 2, :], ALU.mult).then_inc(s_m, 1)

                def statistics(g):
                    es = range(GROUP * g, GROUP * (g + 1))
                    v.wait_ge(d_cb[g], 16 * GROUP)
                    for e in es:
                        ins = v.bn_stats(fst[:, e, :], comb[:, e, 0:DM])
                    ins.then_inc(s_f, 1)
                    cols = slice(es.start, es.stop)
                    v.tensor_tensor(loser[:, cols], comb[:, cols, DM], above[:, cols], ALU.is_ge).then_inc(s_lose, 1)
                    v.wait_ge(s_f, 3 * g + 1)
                    for e in es:
                        ins = v.bn_aggr(fmv[:, e, :], fst[:, e, :])
                    ins.then_inc(s_f, 1)
                    v.wait_ge(s_f, 3 * g + 2)
                    v.tensor_scalar(fvar[:, cols], fmv[:, cols, 1], EPS, None, ALU.add).then_inc(s_f, 1)
                    v.wait_ge(s_lose, g + 2)
                    v.scalar_tensor_tensor(out=dest[:, cols], in0=loser[:, cols], scalar=float(2 * B * S), in1=rowf[:, cols],
                                           op0=ALU.mult, op1=ALU.add).then_inc(s_dest, 1)

                def mean(g):
                    cols = slice(GROUP * g, GROUP * (g + 1))
                    v.wait_ge(s_fp, g + 1)
                    v.scalar_tensor_tensor(out=fnm[:, cols], in0=fmv[:, cols, 0], scalar=-1.0, in1=frs[:, cols],
                                           op0=ALU.mult, op1=ALU.mult).then_inc(s_fn, 1)

                def total(g):
                    for e in range(GROUP * g, GROUP * (g + 1)):
                        v.wait_ge(s_fa, e + 1)
                        v.tensor_tensor(x1[:, e, :], comb[:, e, 0:DM], x1[:, e, :], ALU.add).then_inc(s_fo, 1)

                v.wait_ge(d_x1, 16 * E)
                v.tensor_copy(rowf[:], rowid[:]).then_inc(s_lose, 1)
                for g in range(E // GROUP + 2):
                    if g < E // GROUP:
                        statistics(g)
                    if 0 < g <= E // GROUP:
                        mean(g - 1)
                    if g > 1:
                        total(g - 2)

            @block.scalar
            def _(act):
                act.wait_ge(s_k, FIRST + 2)
                act.activation(lgx[:], lg[:], ACT.Exp, bias=negm[:], accum_out=mass[:]).then_inc(s_ka, 1)
                act.wait_ge(s_k, TOP_READY)
                act.activation(tops[:], tops[:], ACT.Exp, bias=small[:, 0:1]).then_inc(s_ka, 1)
                act.wait_ge(s_k, ROWS_DONE)
                act.activation(vals[:], vals[:], ACT.Exp, bias=small[:, 0:1]).then_inc(s_ka, 1)

                def copied(e):
                    act.wait_ge(s_tr, e + 1)
                    if e >= 2:
                        act.wait_ge(s_v, e - 1)
                    act.copy(tT[:, e % 2], pt[:, 0:KC * P]).then_inc(s_tc, 1)

                def weighted(e):
                    act.wait_ge(s_o, e + 1)
                    if e == 0:
                        act.wait_ge(s_pos, 2)
                    act.activation(comb[:, e, 0:DM], pY[:, e % 2, 0:DM], ACT.Identity, scale=weight[:, e:e + 1]).then_inc(s_y, 1)

                copied(0)
                for e in range(E):
                    act.wait_ge(s_g, e + 1)
                    if e >= 2:
                        act.wait_ge(s_o, e - 1)
                    act.activation(act1[:, e % 2, :], pg[:, e % 2, :], ACT.Silu).then_inc(s_sl, 1)
                    if e + 1 < E:
                        copied(e + 1)
                    if e > 0:
                        weighted(e - 1)
                weighted(E - 1)

                for e in range(E):
                    act.wait_ge(s_fn, e // GROUP + 1)
                    act.activation(comb[:, e, 0:DM], comb[:, e, 0:DM], ACT.Identity, scale=frs[:, e:e + 1],
                                   bias=fnm[:, e:e + 1]).then_inc(s_fa, 1)

            @block.tensor
            def _(pe):
                pe.wait_ge(s_k, SPREAD_READY)
                for k in range(2):
                    mm = pe.matmul(pg[:, k, 0:E], spread[:, k, :], pick[:], start=True, stop=True)
                mm.then_inc(s_kt, 1)

                def transposed(e):
                    pe.wait_ge(d_tk[e % 4], 16 * (e // 4 + 1))
                    if e > 0:
                        pe.wait_ge(s_tc, e)
                    for k in range(KC):
                        mm = pe.transpose(pt[:, k * P:(k + 1) * P], taken[:, e % 4, k * P:(k + 1) * P], ident[:])
                    mm.then_inc(s_tr, 1)

                def product(e):
                    pe.wait_ge(s_m, e + 1)
                    if e >= 2:
                        pe.wait_ge(s_y, e - 1)
                    for f in range(FC):
                        mm = pe.matmul(pY[:, e % 2, 0:DM], act1[:, e % 2, f * P:(f + 1) * P], w3s[:, e % RING, f, :],
                                       start=(f == 0), stop=(f == FC - 1))
                    mm.then_inc(s_o, 1)

                pe.wait_ge(s_pos, 2)
                transposed(0)
                for e in range(E):
                    pe.wait_ge(d_wt[e % RING], 48 * (e // RING + 1))
                    pe.wait_ge(s_tc, e + 1)
                    if e >= 2:
                        pe.wait_ge(s_m, e - 1)
                    for w, bank, s_w in ((w1s, pg, s_g), (w2s, pv, s_v)):
                        for f in range(FC):
                            for k in range(KC):
                                mm = pe.matmul(bank[:, e % 2, f * P:(f + 1) * P], w[:, e % RING, k, f * P:(f + 1) * P],
                                               tT[:, e % 2, k, :], start=(k == 0), stop=(k == KC - 1))
                        mm.then_inc(s_w, 1)
                        if w is w1s and e + 1 < E:
                            transposed(e + 1)
                    if e > 0:
                        product(e - 1)
                product(E - 1)

            @block.gpsimd
            def _(pool):
                def at(table, e):
                    return bass.IndirectOffsetOnAxis(ap=table[:, e:e + 1], axis=0)

                def find(e):
                    pool.indirect_dma_start(rowid[:, e:e + 1], None, tab_dram, at(entry, e)).then_inc(d_id[e % 4], 16)

                def take(e):
                    pool.wait_ge(d_id[e % 4], 16 * (e // 4 + 1))
                    if e >= 4:
                        pool.wait_ge(s_tr, e - 3)
                    pool.indirect_dma_start(taken[:, e % 4, :], None, hid_dram, at(rowid, e)).then_inc(d_tk[e % 4], 16)
                    if e + 4 < E:
                        find(e + 4)

                pool.wait_ge(d_tab, 16 * SEGS)
                pool.wait_ge(s_pos, 1)
                for e in range(4):
                    find(e)
                for e in range(4):
                    take(e)
                for e in range(E):
                    if e == 0:
                        pool.wait_ge(s_bit, 2)
                    pool.indirect_dma_start(x1[:, e, :], None, outf, at(rowid, e)).then_inc(d_x1, 16)
                    if e + 4 < E:
                        take(e + 4)
                    pool.wait_ge(s_y, e + 1)
                    if e > 0:
                        pool.wait_ge(d_add, 16 * e)
                    pool.indirect_dma_start(acc_dram, at(rowid, e), comb[:, e, :], None,
                                            compute_op=ALU.add).then_inc(d_add, 16)
                pool.wait_ge(d_add, 16 * E)

                def inverse(g):
                    cols = slice(GROUP * g, GROUP * (g + 1))
                    pool.wait_ge(s_f, 3 * g + 3)
                    pool.tensor_tensor(frs[:, cols], fvar[:, cols], mhalf[:, 0:GROUP], ALU.pow).then_inc(s_fp, 1)

                for g in range(E // GROUP):
                    for e in range(GROUP * g, GROUP * (g + 1)):
                        pool.indirect_dma_start(comb[:, e, :], None, acc_dram, at(rowid, e)).then_inc(d_cb[g], 16)
                    if g > 0:
                        inverse(g - 1)
                inverse(E // GROUP - 1)
                pool.wait_ge(d_x1, 16 * E)
                for e in range(E):
                    pool.wait_ge(s_dest, e // GROUP + 1)
                    pool.wait_ge(s_fo, e + 1)
                    pool.indirect_dma_start(outf, at(dest, e), x1[:, e, :], None, bounds_check=B * S - 1,
                                            oob_is_err=False).then_inc(d_fin, 16)
                pool.wait_ge(d_fin, 16 * E)


_INS = ['L0_attn_x', 'L0_attn_rms_w', 'L0_attn_W_in', 'L0_attn_conv_w', 'L0_attn_conv_b', 'L0_attn_W_x', 'L0_attn_W_dt',
        'L0_attn_A_log', 'L0_attn_W_out', 'L0_ffn_router_w1', 'L0_ffn_router_w2', 'L0_ffn_w1', 'L0_ffn_w2', 'L0_ffn_w3']


def kernel(**inputs):
    import numpy as _np
    import concourse.bacc as _bacc
    from concourse import mybir as _mybir
    from concourse.bass_utils import run_bass_kernel_spmd as _run

    nc = _bacc.Bacc("TRN2", target_bir_lowering=False, num_devices=1)
    arrays, args = {}, []
    for name in _INS:
        a = _np.ascontiguousarray(inputs[name])
        arrays[f"in_{name}_dram"] = a
        args.append(nc.dram_tensor(f"in_{name}_dram", a.shape, _mybir.dt.from_np(a.dtype), kind="ExternalInput").ap())
    out = nc.dram_tensor("out_dram", inputs['L0_attn_x'].shape, _mybir.dt.float32, kind="ExternalOutput").ap()
    sandwich(nc, *args, out)
    r = _run(nc, [arrays], core_ids=[0])
    return r.results[0]["out_dram"]
```

```python
from contextlib import ExitStack

import concourse.bass as bass
from concourse import mybir

ALU = mybir.AluOpType
ACT = mybir.ActivationFunctionType
AX = mybir.AxisListType
F32 = mybir.dt.float32
BF16 = mybir.dt.bfloat16
U32 = mybir.dt.uint32

P = 128
T = 512
SUB = T // P
DM = 256
DI = 512
NS = 16
TAPS = 4
KC = DM // P
DC = DI // P
GROUPS = DI // 8
QUADS = GROUPS // 4
EPS = 1e-5
ROUTER = 128
E = 16
DFF = 512
CAP = 64
FC = DFF // P
CW = DM + 4
AHEAD = 4
PARTS = 3
STK_DMAS = 4 * PARTS * 16

PREP = dict(
    pe_turn=(6, 8), act_turn=(6, 7), pe_in=(10, 11, 11, 12, 15, 15, 16, 17, 24, 26, 39, 40, 51, 52, 66, 68),
    act_in=(10, 11, 16, 18, 30, 42, 57, 70), conv=(12, 17, 20, 23), silu=25, pe_bc=38, act_bc=39, pe_b=42,
    act_b=42, pe_c=45, act_c=45, pe_dt=(32, 33, 35, 36, 45, 47, 47, 50, 55, 55, 56, 58, 59, 60, 63, 64),
    act_dt=(37, 52, 60, 65), dve_dt=(42, 56, 62, 69), pool_dt=(44, 60, 66, 75), act_ext=(48, 62, 69, 78),
    stack=(52, 63, 74, 82), gate=82)
POST = dict(
    load=4, pe_out=(19, 20, 22, 23, 27, 28, 31, 31), dve_z=(24, 34), stats=(35, 48), pow=(37, 51), nm=(39,
    55), z2=44, x1=45, store_x1=51, hid=57, store_hid=57, pe_ht=(62, 63), act_ht=(61, 64), pe_w1=(69, 71),
    silu=73, pe_w2=76, act_lg=78, store_lg=79)
HEAD_AT = 48
GATED_AT = 8

USES = sorted([(PREP["pe_turn"][k], "turn", k) for k in range(KC)]
              + [(PREP["pe_in"][2 * m], "in", m) for m in range(2 * DC)]
              + [(PREP["pe_bc"], "bc", 0), (PREP["pe_b"], "b", 0), (PREP["pe_c"], "c", 0)]
              + [(PREP["pe_dt"][4 * c], "dt", c) for c in range(DC)])
NU = len(USES)


def use(name, k=0):
    return [(n, m) for _, n, m in USES].index((name, k))


def atleast(eng, sem, value):
    if isinstance(value, int) and value <= 0:
        return
    eng.wait_ge(sem, value)


def sandwich(nc, x, rms_w, W_in, conv_w, conv_b, W_x, W_dt, A_log, W_out, r_w1, r_w2, w1, w2, w3, out):
    B, S, _ = x.shape
    assert B == 2 and S % T == 0
    TILES = B * (S // T)
    xf = x.rearrange("b s d -> (b s) d")
    outf = out.rearrange("b s d -> (b s) d")
    hid_dram = nc.dram_tensor("hidden_scratch", [B * S, DM], F32, kind="Internal").ap()
    acc_dram = nc.dram_tensor("combine_scratch", [B * S, CW], F32, kind="Internal").ap()
    lg_dram = nc.dram_tensor("logits_scratch", [B * E, S], F32, kind="Internal").ap()

    tab_dram = nc.dram_tensor("token_table", [B * E * (P // (B * E)) * CAP, 1], U32, kind="Internal").ap()

    with ExitStack() as whole:
        def sem(name):
            return whole.enter_context(nc.semaphore(name))

        ident = whole.enter_context(nc.sbuf_tensor("ident", [P, P], F32))
        mhalf = whole.enter_context(nc.sbuf_tensor("mhalf", [P, 2 * SUB], F32))

        scan_layers(nc, sem, TILES, S, ident, mhalf, xf, outf, rms_w, W_in, conv_w, conv_b, W_x, W_dt, A_log, W_out,
                    r_w1, r_w2, hid_dram, acc_dram, lg_dram)
        experts(nc, sem, B, S, ident, mhalf, outf, w1, w2, w3, hid_dram, acc_dram, lg_dram, tab_dram)


def scan_layers(nc, sem, TILES, S, ident, mhalf, xf, outf, rms_w, W_in, conv_w, conv_b, W_x, W_dt, A_log, W_out,
                r_w1, r_w2, hid_dram, acc_dram, lg_dram):
    with ExitStack() as ctx:
        def sb(name, shape, dt=F32):
            return ctx.enter_context(nc.sbuf_tensor(name, shape, dt))

        def ps(name, shape):
            return ctx.enter_context(nc.psum_tensor(name, shape, F32))

        pdt = ps("pdt", [P, 2, T])
        pu = ps("pu", [P, 2, T])
        py = ps("py", [P, T])
        pp = ps("pp", [P, 2, T])
        po = ps("po", [P, T])

        w_in = sb("w_in", [P, KC, 2 * DI])
        w_dtx = sb("w_dtx", [P, DC, DI])
        w_bc = sb("w_bc", [P, DC, 2 * NS])
        w_out = sb("w_out", [P, DC, DM])
        rw1 = sb("rw1", [P, KC, ROUTER])
        rw2 = sb("rw2", [P, E])
        cw = sb("cw", [P, DC, TAPS])
        cb = sb("cb", [P, DC])
        rms = sb("rms", [P, KC])
        neg_a = sb("neg_a", [P, GROUPS])
        a_rows = sb("a_rows", [GROUPS, P])
        blk = sb("blk", [P, 32])
        sel_rep = sb("sel_rep", [P, 4, P], BF16)
        sel_sum = sb("sel_sum", [P, 4, 32])
        sel_b = sb("sel_b", [P, P])
        sel_c = sb("sel_c", [P, P])
        m8 = sb("m8", [P, 8])

        xt = sb("xt", [P, SUB, DM])
        xnt = sb("xnt", [P, KC, T])
        st = sb("st", [P, SUB, 6])
        mv = sb("mv", [P, SUB, 2])
        var = sb("var", [P, 2 * SUB])
        rs = sb("rs", [P, 2 * SUB])
        nm = sb("nm", [P, SUB])
        pad = sb("pad", [P, 1], U32)
        r1 = sb("r1", [P, 2, SUB])
        xsp = sb("xsp", [P, 2, T + TAPS - 1])
        halo = sb("halo", [P, 2, DC, TAPS - 1])
        xs = sb("xs", [P, DC, T])
        gate = sb("gate", [P, 2, DC, T])
        bc = sb("bc", [P, T])
        b_rep = sb("b_rep", [P, 2, T])
        c_rep = sb("c_rep", [P, 2, T])
        spe = sb("spe", [P, T])
        spl = sb("spl", [P, T])
        spt = sb("spt", [P, T])
        spr = sb("spr", [P, T])
        dtv = sb("dtv", [P, T])
        uv = sb("uv", [P, T])
        rem = sb("rem", [P, 2, T])
        parts = sb("parts", [P, 2, 2, PARTS, T], BF16)
        stk = sb("stk", [P, 2, 4 * DC, T], BF16)

        decay = sb("decay", [P, 8, T])
        bx = sb("bx", [P, 4, T])
        h = sb("h", [P, 8, T])
        hc = sb("hc", [P, 8, T])
        carry = sb("carry", [P, 2, GROUPS])

        xo = sb("xo", [P, SUB, DM])
        z = sb("z", [P, SUB, DM])
        st2 = sb("st2", [P, SUB, 6])
        pad2 = sb("pad2", [P, 1], U32)
        mv2 = sb("mv2", [P, SUB, 2])
        var2 = sb("var2", [P, SUB])
        rs2 = sb("rs2", [P, SUB])
        nm2 = sb("nm2", [P, SUB])
        hid = sb("hid", [P, SUB, DM])
        ht = sb("ht", [P, KC, T])

        wxs = h[:, 0:DC, :]
        wxt = h[:, 4:4 + DC, :]
        wdt = hc[:, 0:DC, :]
        zeros = decay[:].rearrange("p a b -> p (a b)")[:, 0:SUB * CW].rearrange("p (s d) -> p s d", d=CW)
        d_wx, d_win, d_conv, d_wdt, d_alog, d_wout, d_zero = (
            sem("w_x_loaded"), sem("w_in_loaded"), sem("conv_loaded"), sem("w_dt_loaded"), sem("a_log_loaded"),
            sem("w_out_loaded"), sem("zeros_stored"))
        s_id, s_const, s_sel, s_zero, s_win, s_nega = (
            sem("identity_step"), sem("constants_ready"), sem("selectors_step"), sem("zeros_ready"), sem("w_in_scaled"),
            sem("neg_a_step"))
        s_alog, s_wxt, s_wxc, s_wp, s_wpc = (sem("a_log_transposed"), sem("w_x_transposed"), sem("w_x_copied"),
                                             sem("w_dtx_product"), sem("w_dtx_copied"))

        s_rdt, s_ru = sem("rep_dt_ready"), sem("rep_u_ready")
        s_exp, s_bx, s_scan, s_carry = sem("decay_ready"), sem("bx_ready"), sem("h_ready"), sem("carry_saved")
        s_hc, s_sum, s_gate = sem("hc_ready"), sem("y_summed"), sem("y_gated")
        d_x, s_st, s_pw, s_xn = sem("x_loaded"), sem("stats_step"), sem("rstd_ready"), sem("x_normalised")
        s_r1 = sem("r1_kept")
        s_pp, s_ev = sem("prep_bank_full"), sem("prep_bank_copied")
        s_halo, s_conv = sem("halo_step"), sem("conv_step")
        s_xs, s_sg = sem("xs_ready"), sem("gate_ready")
        s_sp, s_spl, s_spv, s_dt = sem("softplus_e"), sem("softplus_ln"), sem("softplus_step"), sem("dt_ready")
        s_u, s_remd, s_lod, s_remu, s_lou = (sem("u_ready"), sem("dt_rest"), sem("dt_last_part"), sem("u_rest"),
                                             sem("u_last_part"))
        s_xd, s_xu = sem("dt_parts_ready"), sem("u_parts_ready")
        d_stk = [sem(f"stack_loaded_{c}") for c in range(DC)]
        d_xo, s_wo, s_z, s_dp, s_pw2 = (sem("xo_loaded"), sem("out_product"), sem("z_ready"), sem("post_step"),
                                        sem("post_rstd"))
        s_z2, s_x1, d_x1, s_hid, d_hid = (sem("z_normalised"), sem("x1_ready"), sem("x1_stored"), sem("hid_ready"),
                                          sem("hid_stored"))
        s_ht, s_hte, s_rh, s_rs, s_w2, s_lg, d_lg = (sem("ht_bank"), sem("ht_copied"), sem("router_hidden"),
                                                     sem("router_silu"), sem("logits_bank"), sem("logits_ready"),
                                                     sem("logits_stored"))

        def rows(i, par):
            if isinstance(i, int):
                return par * S + (i // 2) * T
            return (i - par) * (T // 2) + par * S

        def all_steps(eng, run):
            run(0, 0, False, False, True, True)
            run(1, 1, False, True, True, True)
            with eng.Fori(0, (TILES - 4) // 2) as k:
                run(2 * k + 2, 0, True, True, True, True)
                run(2 * k + 3, 1, True, True, True, True)
            run(TILES - 2, 0, True, True, True, True)
            run(TILES - 1, 1, True, True, True, False)
            run(TILES, 0, True, True, False, False)
            run(TILES + 1, 1, True, False, False, False)

        with nc.Block() as block:
            @block.sync
            def _(sp):
                def load_x(i, par):
                    atleast(sp, s_pp, NU * (i - 1) + KC)
                    sp.dma_start(xt[:], xf[bass.ds(rows(i, par), T), :].rearrange("(s p) d -> p s d", p=P)).then_inc(d_x, 16)

                def stack(c, i):
                    made, used = 4 * i + c + 1, 64 * (i - 1) + 16 * (c + 1)
                    if not isinstance(i, int):
                        sp.compute_val(made)
                        sp.compute_val(used)
                    sp.wait_ge(s_xd, made)
                    sp.wait_ge(s_xu, made)
                    sp.wait_ge(s_lod, made)
                    sp.wait_ge(s_lou, made)
                    atleast(sp, s_rdt, used)
                    atleast(sp, s_ru, used)
                    for q in range(4):
                        for m in range(PARTS):
                            sp.dma_start(stk[32 * m:32 * m + 32, :, 4 * c + q, :],
                                         parts[32 * q:32 * q + 32, c % 2, :, m, :]).then_inc(d_stk[c], 16)

                def prep(t, i, par):
                    for c in range(DC):
                        if t == PREP["stack"][c]:
                            stack(c, i)

                def post(t, j, par):
                    if t == POST["load"]:
                        atleast(sp, s_x1, j)
                        sp.dma_start(xo[:], xf[bass.ds(rows(j, par), T), :].rearrange("(s p) d -> p s d", p=P)).then_inc(d_xo, 16)
                    if t == POST["store_x1"]:
                        sp.wait_ge(s_x1, j + 1)
                        sp.dma_start(outf[bass.ds(rows(j, par), T), :].rearrange("(s p) d -> p s d", p=P), z[:]).then_inc(d_x1, 16)
                    if t == POST["store_hid"]:
                        sp.wait_ge(s_hid, j + 1)
                        sp.dma_start(hid_dram[bass.ds(rows(j, par), T), :].rearrange("(s p) d -> p s d", p=P), hid[:]).then_inc(d_hid, 16)
                    if t == POST["store_lg"]:
                        col = (j // 2) * T if isinstance(j, int) else (j - par) * (T // 2)
                        if not isinstance(j, int):
                            sp.compute_val(col * 4)
                        sp.wait_ge(s_lg, j + 1)
                        sp.dma_start(lg_dram[par * E:(par + 1) * E, bass.ds(col, T)], ht[0:E, 1, :]).then_inc(d_lg, 16)

                def step(i, par, has_late, has_prev, has_cur, has_next):
                    for t in range(GROUPS):
                        if has_late:
                            post(64 + t, i - 2, par)
                        if has_cur:
                            prep(64 + t, i, par)
                        if has_next:
                            prep(t, i + 1, 1 - par)
                        if has_prev:
                            post(t, i - 1, 1 - par)
                        if has_next and t == 20:
                            if isinstance(i, int) and i + 2 >= TILES:
                                continue
                            load_x(i + 2, par)

                load_x(0, 0)
                sp.dma_start(wxs, W_x[:, 0:DI].rearrange("(c p) j -> p c j", p=P)).then_inc(d_wx, 16)
                sp.dma_start(a_rows[:], A_log.rearrange("(g e) n -> g (e n)", e=8)).then_inc(d_alog, 16)
                sp.dma_start(rms[:], rms_w.rearrange("(c p) -> p c", p=P), allow_slow_non_contiguous=True).then_inc(d_win, 16)
                sp.dma_start(w_in[:], W_in.rearrange("(c p) j -> p c j", p=P)).then_inc(d_win, 16)
                sp.dma_start(cw[:], conv_w.rearrange("(c p) o k -> p c (o k)", p=P)).then_inc(d_conv, 16)
                sp.dma_start(cb[:], conv_b.rearrange("(c p) -> p c", p=P), allow_slow_non_contiguous=True).then_inc(d_conv, 16)
                sp.dma_start(wdt, W_dt.rearrange("(c p) j -> p c j", p=P)).then_inc(d_wdt, 16)
                sp.dma_start(w_bc[:], W_x[:, DI:DI + 2 * NS].rearrange("(c p) j -> p c j", p=P)).then_inc(d_wdt, 16)
                sp.dma_start(w_out[:], W_out.rearrange("(c p) j -> p c j", p=P)).then_inc(d_wout, 16)
                sp.dma_start(rw1[:], r_w1.rearrange("(c p) j -> p c j", p=P)).then_inc(d_wout, 16)
                sp.dma_start(rw2[:], r_w2).then_inc(d_wout, 16)
                load_x(1, 1)
                sp.wait_ge(s_zero, 1)
                for r in range(0, acc_dram.shape[0], T):
                    sp.dma_start(acc_dram[r:r + T, :].rearrange("(s p) d -> p s d", p=P), zeros).then_inc(d_zero, 16)
                for t in range(GROUPS):
                    prep(t, 0, 0)
                all_steps(sp, step)
                sp.wait_ge(d_x1, 16 * TILES)
                sp.wait_ge(d_hid, 16 * TILES)
                sp.wait_ge(d_lg, 16 * TILES)

            @block.tensor
            def _(pe):
                def bank_free(n, i):
                    atleast(pe, s_ev, NU * i + n - 1)

                def spread_dt(t, i, par):
                    c, s, q = t // 16, t // 4 % 4, t % 4
                    if t % 16 == 0:
                        pe.wait_ge(d_stk[c], STK_DMAS * (i + 1))
                    atleast(pe, s_exp, 64 * i + t - 1)
                    pe.matmul(pdt[:, t % 2, :], sel_rep[0:96, s, :], stk[0:96, 0, 4 * c + q, :],
                              start=True, stop=True).then_inc(s_rdt, 1)

                def spread_u(t, i, par):
                    c, s, q = t // 16, t // 4 % 4, t % 4
                    atleast(pe, s_bx, 64 * i + t - 1)
                    pe.matmul(pu[:, t % 2, :], sel_rep[0:96, s, :], stk[0:96, 1, 4 * c + q, :],
                              start=True, stop=True).then_inc(s_ru, 1)

                def sum_states(quad, i):
                    c, s = quad // 4, quad % 4
                    pe.wait_ge(s_hc, 32 * i + 2 * quad + 2)
                    if s == 0:
                        atleast(pe, s_gate, 4 * i + c)
                    for q in range(4):
                        mm = pe.matmul(py[32 * q:32 * q + 32, :], sel_sum[:, s, :], hc[:, (4 * quad + q) % 8, :],
                                       start=(s == 0), stop=(s == 3), tile_position=(0, 32 * q))
                    mm.then_inc(s_sum, 1)

                def prep(t, i, par):
                    def bank(n):
                        return pp[:, (par + n) % 2, :]

                    for k in range(KC):
                        if t == PREP["pe_turn"][k]:
                            n = use("turn", k)
                            pe.wait_ge(s_xn, i + 1)
                            bank_free(n, i)
                            for s in range(SUB):
                                mm = pe.transpose(bank(n)[:, s * P:(s + 1) * P], xt[:, s, k * P:(k + 1) * P], ident[:])
                            mm.then_inc(s_pp, 1)
                    for m in range(2 * DC):
                        for k in range(KC):
                            if t == PREP["pe_in"][2 * m + k]:
                                n = use("in", m)
                                if k == 0:
                                    if m == 0:
                                        pe.wait_ge(s_ev, NU * i + KC)
                                    bank_free(n, i)
                                mm = pe.matmul(bank(n), w_in[:, k, m * P:(m + 1) * P], xnt[:, k, :],
                                               start=(k == 0), stop=(k == KC - 1))
                                if k == KC - 1:
                                    mm.then_inc(s_pp, 1)
                    if t == PREP["pe_bc"]:
                        n = use("bc")
                        pe.wait_ge(s_xs, i + 1)
                        bank_free(n, i)
                        for k in range(DC):
                            mm = pe.matmul(bank(n)[32 * k:32 * k + 32, :], w_bc[:, k, :], xs[:, k, :],
                                           start=True, stop=True, tile_position=(0, 32 * k))
                        mm.then_inc(s_pp, 1)
                    for name, sel in (("b", sel_b), ("c", sel_c)):
                        if t == PREP["pe_" + name]:
                            n = use(name)
                            pe.wait_ge(s_ev, NU * i + use("bc") + 1)
                            bank_free(n, i)
                            pe.matmul(bank(n), sel[:], bc[:], start=True, stop=True).then_inc(s_pp, 1)
                    for c in range(DC):
                        for k in range(DC):
                            if t == PREP["pe_dt"][DC * c + k]:
                                n = use("dt", c)
                                if k == 0:
                                    pe.wait_ge(s_xs, i + 1)
                                    bank_free(n, i)
                                mm = pe.matmul(bank(n), w_dtx[:, k, c * P:(c + 1) * P], xs[:, k, :],
                                               start=(k == 0), stop=(k == DC - 1))
                                if k == DC - 1:
                                    mm.then_inc(s_pp, 1)

                def post(t, j, par):
                    for step in range(8):
                        if t == POST["pe_out"][step]:
                            half = step // 4
                            if step == 0:
                                pe.wait_ge(s_gate, 4 * j + 4)
                                atleast(pe, s_lg, j)
                            if step == 4:
                                pe.wait_ge(s_z, 2 * j + 1)
                            for n in range(2 * (step % 4), 2 * (step % 4) + 2):
                                s, k = 2 * half + n // DC, n % DC
                                mm = pe.matmul(po[:, (s % 2) * DM:(s % 2 + 1) * DM], gate[:, par, k, s * P:(s + 1) * P],
                                               w_out[:, k, :], start=(k == 0), stop=(k == DC - 1))
                            if step % 4 == 3:
                                mm.then_inc(s_wo, 1)
                    for k, at in enumerate(POST["pe_ht"]):
                        if t == at:
                            pe.wait_ge(s_hid, j + 1)
                            if k == 0:
                                pe.wait_ge(s_z, 2 * j + 2)
                            else:
                                pe.wait_ge(s_hte, 2 * j + 1)
                            for s in range(SUB):
                                mm = pe.transpose(po[:, s * P:(s + 1) * P], hid[:, s, k * P:(k + 1) * P], ident[:])
                            mm.then_inc(s_ht, 1)
                    for k in range(KC):
                        if t == POST["pe_w1"][k]:
                            if k == 0:
                                pe.wait_ge(s_hte, 2 * j + 2)
                            mm = pe.matmul(po[:], rw1[:, k, :], ht[:, k, :], start=(k == 0), stop=(k == KC - 1))
                            if k == KC - 1:
                                mm.then_inc(s_rh, 1)
                    if t == POST["pe_w2"]:
                        pe.wait_ge(s_rs, j + 1)
                        pe.matmul(po[0:E, :], rw2[:], ht[:, 0, :], start=True, stop=True).then_inc(s_w2, 1)

                def step(i, par, has_late, has_prev, has_cur, has_next):
                    for t in range(GROUPS):
                        if has_cur and t + 1 < GROUPS:
                            spread_u(t + 1, i, par)
                        elif has_next:
                            spread_u(0, i + 1, 1 - par)
                        if has_late:
                            post(64 + t, i - 2, par)
                        if has_cur:
                            prep(64 + t, i, par)
                        if has_next:
                            prep(t, i + 1, 1 - par)
                        if t % 4 == 1:
                            quad = (t - 9) // 4
                            if quad < 0 and has_prev:
                                sum_states(QUADS + quad, i - 1)
                            elif quad >= 0 and has_cur:
                                sum_states(quad, i)
                        if has_prev:
                            post(t, i - 1, 1 - par)
                        if has_cur and t + AHEAD < GROUPS:
                            spread_dt(t + AHEAD, i, par)
                        elif has_next:
                            spread_dt(t + AHEAD - GROUPS, i + 1, 1 - par)

                pe.wait_ge(s_id, 5)
                pe.wait_ge(d_alog, 16)
                pe.transpose(po[:, 0:GROUPS], a_rows[:], ident[0:GROUPS, 0:GROUPS]).then_inc(s_alog, 1)
                pe.wait_ge(d_wx, 16)
                for j in range(DC):
                    if j >= 2:
                        pe.wait_ge(s_wxc, j - 1)
                    for k in range(DC):
                        mm = pe.transpose(pdt[:, j % 2, k * P:(k + 1) * P], wxs[:, k, j * P:(j + 1) * P], ident[:])
                    mm.then_inc(s_wxt, 1)
                for t in range(GROUPS):
                    if t == PREP["pe_in"][0]:
                        pe.wait_ge(s_win, 1)
                    if t == PREP["pe_in"][2 * DC - 1] + 1:
                        pe.wait_ge(d_wdt, 32)
                        pe.wait_ge(s_wxc, DC)
                        for k in range(DC):
                            if k >= 2:
                                pe.wait_ge(s_wpc, k - 1)
                            for j in range(DC):
                                mm = pe.matmul(pu[:, k % 2, :], wxt[:, j, k * P:(k + 1) * P], wdt[:, j, :],
                                               start=(j == 0), stop=(j == DC - 1))
                            mm.then_inc(s_wp, 1)
                        pe.wait_ge(s_sel, 2)
                        pe.wait_ge(s_wpc, DC)
                    prep(t, 0, 0)
                for t in range(AHEAD):
                    spread_dt(t, 0, 0)
                spread_u(0, 0, 0)
                pe.wait_ge(d_wout, 48)
                all_steps(pe, step)

            @block.scalar
            def _(act):
                def head(t, i):
                    if t == 8:
                        act.wait_ge(s_pw, i + 1)
                        act.wait_ge(s_st, 4 * i + 4)
                        for s in range(SUB):
                            ins = act.activation(xt[:, s, :], xt[:, s, :], ACT.Identity, scale=rs[:, SUB + s:SUB + s + 1],
                                                 bias=nm[:, s:s + 1])
                        ins.then_inc(s_xn, 1)

                def prep(t, i, par):
                    def bank(n):
                        return pp[:, (par + n) % 2, :]

                    def filled(name, k=0):
                        act.wait_ge(s_pp, NU * i + use(name, k) + 1)
                        return bank(use(name, k))

                    for k in range(KC):
                        if t == PREP["act_turn"][k]:
                            atleast(act, s_pp, NU * (i - 1) + use("in", 2 * DC - 1) + 1)
                            act.copy(xnt[:, k, :], filled("turn", k)).then_inc(s_ev, 1)
                    for m in range(2 * DC):
                        if t == PREP["act_in"][m]:
                            full = filled("in", m)
                            if m < DC:
                                c = m
                                atleast(act, s_conv, 12 * i + 3 * (c - 1))
                                act.copy(xsp[:, c % 2, TAPS - 1:], full)
                                atleast(act, s_pp, NU * i)
                                atleast(act, s_u, 4 * i + c - 3)
                                act.activation(xs[:, c, :], full, ACT.Identity, scale=cw[:, c, TAPS - 1:TAPS],
                                               bias=cb[:, c:c + 1]).then_inc(s_ev, 1)
                            else:
                                if m == DC:
                                    atleast(act, s_wo, 2 * (i - 1))
                                act.copy(gate[:, par, m - DC, :], full).then_inc(s_ev, 1)
                    if t == PREP["act_bc"]:
                        act.copy(bc[:], filled("bc")).then_inc(s_ev, 1)
                    if t == PREP["act_b"]:
                        full = filled("b")
                        atleast(act, s_bx, 64 * (i - 1))
                        act.copy(b_rep[:, par, :], full).then_inc(s_ev, 1)
                    if t == PREP["act_c"]:
                        full = filled("c")
                        atleast(act, s_hc, 32 * (i - 1))
                        act.copy(c_rep[:, par, :], full).then_inc(s_ev, 1)
                    for c in range(DC):
                        if t == PREP["act_dt"][c]:
                            full = filled("dt", c)
                            atleast(act, s_dt, 4 * i + c)
                            act.activation(spr[:], full, ACT.Relu)
                            act.activation(spe[:], full, ACT.Abs).then_inc(s_ev, 1)
                        if t == PREP["act_dt"][c] + 1:
                            act.wait_ge(s_ev, NU * i + use("dt", c) + 1)
                            act.activation(spe[:], spe[:], ACT.Exp, scale=-1.0).then_inc(s_sp, 1)
                            act.wait_ge(s_sp, 4 * i + c + 1)
                            act.activation(spt[:], spe[:], ACT.Identity, bias=1.0)
                            act.activation(spl[:], spe[:], ACT.Ln, bias=1.0).then_inc(s_spl, 1)
                        if t == PREP["act_ext"][c]:
                            parts_free(c, i)
                            act.wait_ge(s_remd, 4 * i + c + 1)
                            extract(0, dtv, c)
                            extract(1, None, c, 0).then_inc(s_xd, 1)
                        if t == PREP["act_ext"][c] + 2:
                            act.wait_ge(s_remu, 4 * i + c + 1)
                            extract(0, uv, c, 1)
                            extract(1, None, c, 1).then_inc(s_xu, 1)
                    if t == PREP["silu"]:
                        act.wait_ge(s_conv, 12 * i + 12)
                        act.activation(xs[:], xs[:], ACT.Silu).then_inc(s_xs, 1)
                    if t == PREP["gate"]:
                        act.wait_ge(s_ev, NU * i + use("in", 2 * DC - 1) + 1)
                        act.activation(gate[:, par], gate[:, par], ACT.Silu).then_inc(s_sg, 1)

                def parts_free(c, i):
                    if c >= 2:
                        act.wait_ge(d_stk[c - 2], STK_DMAS * (i + 1))
                    else:
                        atleast(act, d_stk[c + 2], STK_DMAS * i)

                def extract(part, src, c, tensor=0):
                    words = src[:] if part == 0 else rem[:, tensor, :]
                    return act.copy(parts[:, c % 2, tensor, part, :], words.bitcast(BF16)[:, 1::2])

                def post(t, j, par):
                    if t == POST["z2"]:
                        act.wait_ge(s_dp, 8 * j + 4)
                        for s in range(SUB):
                            ins = act.activation(z[:, s, :], z[:, s, :], ACT.Identity, scale=rs2[:, s:s + 1],
                                                 bias=nm2[:, s:s + 1])
                        ins.then_inc(s_z2, 1)
                    if t == POST["hid"]:
                        act.wait_ge(s_dp, 8 * j + 8)
                        atleast(act, d_hid, 16 * j)
                        atleast(act, s_ht, 2 * j)
                        for s in range(SUB):
                            ins = act.activation(hid[:, s, :], z[:, s, :], ACT.Identity, scale=rs2[:, s:s + 1],
                                                 bias=nm2[:, s:s + 1])
                        ins.then_inc(s_hid, 1)
                    for k, at in enumerate(POST["act_ht"]):
                        if t == at:
                            act.wait_ge(s_ht, 2 * j + k + 1)
                            if k == 0:
                                atleast(act, d_lg, 16 * j)
                                atleast(act, s_w2, j)
                            act.copy(ht[:, k, :], po[:]).then_inc(s_hte, 1)
                    if t == POST["silu"]:
                        act.wait_ge(s_rh, j + 1)
                        act.activation(ht[:, 0, :], po[:], ACT.Silu).then_inc(s_rs, 1)
                    if t == POST["act_lg"]:
                        act.wait_ge(s_w2, j + 1)
                        act.copy(ht[0:E, 1, :], po[0:E, :]).then_inc(s_lg, 1)

                def decays(t, i):
                    act.wait_ge(s_rdt, 64 * i + t + 1)
                    atleast(act, s_scan, 64 * i + t - 7)
                    act.activation(decay[:, t % 8, :], pdt[:, t % 2, :], ACT.Exp,
                                   scale=neg_a[:, group_column(t):group_column(t) + 1]).then_inc(s_exp, 1)

                def step(i, par, has_late, has_prev, has_cur, has_next):
                    for t in range(GROUPS):
                        if has_cur and t + AHEAD < GROUPS:
                            decays(t + AHEAD, i)
                        elif has_next:
                            decays(t + AHEAD - GROUPS, i + 1)
                        if has_cur:
                            prep(64 + t, i, par)
                        if has_next:
                            prep(t, i + 1, 1 - par)
                        if has_late:
                            post(64 + t, i - 2, par)
                        if has_next and not (isinstance(i, int) and i + 2 >= TILES):
                            head(t - HEAD_AT, i + 2)
                        if has_prev:
                            post(t, i - 1, 1 - par)

                act.wait_ge(s_alog, 1)
                act.activation(neg_a[:], po[:, 0:GROUPS], ACT.Exp).then_inc(s_nega, 1)
                for j in range(DC):
                    act.wait_ge(s_wxt, 1 + j)
                    act.copy(wxt[:, j, :], pdt[:, j % 2, :]).then_inc(s_wxc, 1)
                for t in range(GROUPS - HEAD_AT):
                    head(t, 0)
                act.wait_ge(d_conv, 32)
                for t in range(GROUPS):
                    prep(t, 0, 0)
                    head(t - HEAD_AT, 1)
                    if t == PREP["act_in"][DC - 1]:
                        for k in range(DC):
                            act.wait_ge(s_wp, 1 + k)
                            act.copy(w_dtx[:, k, :], pu[:, k % 2, :]).then_inc(s_wpc, 1)
                act.wait_ge(s_nega, 2)
                act.wait_ge(d_zero, 16 * (acc_dram.shape[0] // T))
                for t in range(AHEAD):
                    decays(t, 0)
                all_steps(act, step)

            @block.vector
            def _(v):
                def head(t, i):
                    if t == 0:
                        v.wait_ge(d_x, 16 * (i + 1))
                        for s in range(SUB):
                            ins = v.bn_stats(st[:, s, :], xt[:, s, :])
                        ins.then_inc(s_st, 1)
                    if t == 1:
                        v.wait_ge(s_st, 4 * i + 1)
                        v.memset(pad[:], 0)
                        for s in range(SUB):
                            ins = v.bn_aggr(mv[:, s, :], st[:, s, :])
                        ins.then_inc(s_st, 1)
                    if t == 2:
                        v.wait_ge(s_st, 4 * i + 2)
                        atleast(v, s_pw, i)
                        v.tensor_scalar(var[:, 0:SUB], mv[:, :, 1], EPS, None, ALU.add)
                        v.tensor_scalar(var[:, SUB:], mv[:, :, 1], 1.0 + EPS, EPS * EPS, ALU.mult, ALU.add).then_inc(s_st, 1)
                    if t == 6:
                        v.wait_ge(s_pw, i + 1)
                        atleast(v, s_xn, i)
                        v.scalar_tensor_tensor(out=nm[:], in0=mv[:, :, 0], scalar=-1.0, in1=rs[:, SUB:], op0=ALU.mult,
                                               op1=ALU.mult).then_inc(s_st, 1)

                def prep(t, i, par):
                    if t == POST["dve_z"][1] + 2:
                        atleast(v, s_z, 2 * (i - 1))
                        v.tensor_copy(r1[:, par, :], rs[:, 0:SUB]).then_inc(s_r1, 1)
                    for c in range(DC):
                        if t == PREP["conv"][c] - 1:
                            atleast(v, s_halo, 8 * i)
                            atleast(v, s_conv, 12 * i + 3 * (c - 1))
                            v.tensor_copy(xsp[:, c % 2, 0:TAPS - 1], halo[:, par, c, :]).then_inc(s_halo, 1)
                        for tap in range(TAPS - 1):
                            if t == PREP["conv"][c] + tap:
                                if tap == 0:
                                    v.wait_ge(s_ev, NU * i + use("in", c) + 1)
                                    v.wait_ge(s_halo, 8 * i + 2 * c + 1)
                                else:
                                    v.wait_ge(s_conv, 12 * i + 3 * c + tap)
                                v.scalar_tensor_tensor(out=xs[:, c, :], in0=xsp[:, c % 2, tap:tap + T],
                                                       scalar=cw[:, c, tap:tap + 1], in1=xs[:, c, :], op0=ALU.mult,
                                                       op1=ALU.add).then_inc(s_conv, 1)
                                if tap == 0:
                                    v.wait_ge(s_halo, 8 * i + 2 * c + 1)
                                    v.tensor_copy(halo[:, par, c, :], xsp[:, c % 2, T:]).then_inc(s_halo, 1)
                    for c in range(DC):
                        at = PREP["dve_dt"][c]
                        n = 4 * i + c
                        if t == at:
                            v.wait_ge(s_spl, n + 1)
                            v.scalar_tensor_tensor(out=spe[:], in0=spt[:], scalar=-1.0, in1=spe[:], op0=ALU.add,
                                                   op1=ALU.subtract).then_inc(s_spv, 1)
                        if t == at + 1:
                            v.wait_ge(s_spv, 2 * n + 1)
                            v.tensor_tensor(spl[:], spl[:], spe[:], ALU.subtract).then_inc(s_spv, 1)
                        if t == at + 2:
                            v.wait_ge(s_spv, 2 * n + 2)
                            atleast(v, s_lod, n)
                            atleast(v, s_xd, n)
                            atleast(v, s_u, n)
                            v.tensor_tensor(dtv[:], spr[:], spl[:], ALU.add).then_inc(s_dt, 1)

                def stats(src, base, j, at):
                    if at == 0:
                        for s in range(SUB):
                            ins = v.bn_stats(st2[:, s, :], src[:, s, :])
                        ins.then_inc(s_dp, 1)
                    if at == 1:
                        v.wait_ge(s_dp, 8 * j + base + 1)
                        v.memset(pad2[:], 0)
                        for s in range(SUB):
                            ins = v.bn_aggr(mv2[:, s, :], st2[:, s, :])
                        ins.then_inc(s_dp, 1)
                    if at == 2:
                        v.wait_ge(s_dp, 8 * j + base + 2)
                        v.tensor_scalar(var2[:], mv2[:, :, 1], EPS, None, ALU.add).then_inc(s_dp, 1)

                def post(t, j, par):
                    for half, at in enumerate(POST["dve_z"]):
                        if t == at:
                            v.wait_ge(s_wo, 2 * j + half + 1)
                            if half == 0:
                                v.wait_ge(d_xo, 16 * (j + 1))
                                v.wait_ge(s_r1, j + 1)
                                atleast(v, d_x1, 16 * j)
                                atleast(v, s_hid, j)
                            for s in (2 * half, 2 * half + 1):
                                ins = v.scalar_tensor_tensor(out=z[:, s, :], in0=xo[:, s, :], scalar=r1[:, par, s:s + 1],
                                                             in1=po[:, (s % 2) * DM:(s % 2 + 1) * DM], op0=ALU.mult,
                                                             op1=ALU.add)
                            ins.then_inc(s_z, 1)
                    for k in range(3):
                        if t == POST["stats"][0] + k:
                            if k == 0:
                                v.wait_ge(s_z, 2 * j + 2)
                            stats(z, 0, j, k)
                        if t == POST["stats"][1] + k:
                            if k == 0:
                                v.wait_ge(s_x1, j + 1)
                            stats(z, 4, j, k)
                    for n, at in enumerate(POST["nm"]):
                        if t == at:
                            v.wait_ge(s_pw2, 2 * j + n + 1)
                            v.scalar_tensor_tensor(out=nm2[:], in0=mv2[:, :, 0], scalar=-1.0, in1=rs2[:], op0=ALU.mult,
                                                   op1=ALU.mult).then_inc(s_dp, 1)

                def inject(t, i, par):
                    v.wait_ge(s_ru, 64 * i + t + 1)
                    if t == 0:
                        v.wait_ge(s_ev, NU * i + use("b") + 1)
                    atleast(v, s_scan, 64 * i + t - 3)
                    v.tensor_tensor(bx[:, t % 4, :], pu[:, t % 2, :], b_rep[:, par, :], ALU.mult).then_inc(s_bx, 1)

                def scan(t, i, par):
                    v.wait_ge(s_exp, 64 * i + t + 1)
                    v.wait_ge(s_bx, 64 * i + t + 1)
                    if t % 2 == 0:
                        atleast(v, s_hc, 32 * i + t // 2 - 3)
                    if t == 0:
                        atleast(v, s_carry, 16 * (i - 1))
                    v.tensor_tensor_scan(h[:, t % 8, :], decay[:, t % 8, :], bx[:, t % 4, :], carry[:, par, t:t + 1],
                                         ALU.mult, ALU.add).then_inc(s_scan, 1)

                def save(quad, i, par):
                    v.wait_ge(s_scan, 64 * i + 4 * quad + 4)
                    b = 4 * (quad % 2)
                    v.tensor_copy(carry[:, par, 4 * quad:4 * quad + 4], h[:, b:b + 4, T - 1]).then_inc(s_carry, 1)

                def gated(c, i, par):
                    v.wait_ge(s_sum, 16 * i + 4 * c + 4)
                    v.wait_ge(s_sg, i + 1)
                    v.tensor_tensor(gate[:, par, c, :], py[:], gate[:, par, c, :], ALU.mult).then_inc(s_gate, 1)

                def step(i, par, has_late, has_prev, has_cur, has_next):
                    for t in range(GROUPS):
                        if has_late:
                            post(64 + t, i - 2, par)
                        if has_cur:
                            inject(t, i, par)
                            prep(64 + t, i, par)
                        if has_next:
                            prep(t, i + 1, 1 - par)
                        if has_next and not (isinstance(i, int) and i + 2 >= TILES):
                            head(t - HEAD_AT, i + 2)
                        if t == GATED_AT and has_prev:
                            gated(3, i - 1, 1 - par)
                        if t % 16 == GATED_AT and t > 16 and has_cur:
                            gated(t // 16 - 1, i, par)
                        if has_prev:
                            post(t, i - 1, 1 - par)
                        if t == 0 and has_prev:
                            scan(GROUPS - 1, i - 1, 1 - par)
                        elif t > 0 and has_cur:
                            scan(t - 1, i, par)
                        if t == 2 and has_prev:
                            save(QUADS - 1, i - 1, 1 - par)
                        elif t % 4 == 2 and t > 2 and has_cur:
                            save(t // 4 - 1, i, par)

                v.memset(mhalf[:], -0.5).then_inc(s_const, 1)
                v.memset(zeros, 0.0).then_inc(s_zero, 1)
                v.memset(carry[:], 0.0).then_inc(s_const, 1)
                v.memset(halo[:], 0.0).then_inc(s_const, 1)
                v.memset(sel_sum[:], 0.0).then_inc(s_const, 1)
                v.wait_ge(s_id, 5)
                v.tensor_reduce(blk[:], ident[:].rearrange("p (k r) -> p r k", r=32), AX.X, ALU.add).then_inc(s_sel, 1)
                v.wait_ge(s_sel, 1)
                v.wait_ge(s_const, 4)
                for s in range(4):
                    v.tensor_copy(sel_rep[:, s, :].rearrange("p (e n) -> p e n", n=NS),
                                  blk[:, 8 * s:8 * s + 8].unsqueeze(2).broadcast_to((P, 8, NS)))
                    v.tensor_copy(sel_sum[:, s, 8 * s:8 * s + 8], m8[:])
                v.tensor_copy(sel_b[:].rearrange("p (e n) -> p e n", n=NS),
                              blk[:, 0:NS].unsqueeze(1).broadcast_to((P, 8, NS)))
                v.tensor_copy(sel_c[:].rearrange("p (e n) -> p e n", n=NS),
                              blk[:, NS:2 * NS].unsqueeze(1).broadcast_to((P, 8, NS))).then_inc(s_sel, 1)
                for t in range(GROUPS - HEAD_AT):
                    head(t, 0)
                v.wait_ge(d_win, 32)
                for c in range(KC):
                    ins = v.tensor_scalar(w_in[:, c, :], w_in[:, c, :], rms[:, c:c + 1], None, ALU.mult)
                ins.then_inc(s_win, 1)
                v.wait_ge(s_nega, 1)
                v.tensor_scalar(neg_a[:], neg_a[:], -1.0, None, ALU.mult).then_inc(s_nega, 1)
                v.wait_ge(d_conv, 32)
                for t in range(GROUPS):
                    prep(t, 0, 0)
                    head(t - HEAD_AT, 1)
                all_steps(v, step)

            @block.gpsimd
            def _(pool):
                def head(t, i):
                    if t == 3:
                        pool.wait_ge(s_st, 4 * i + 3)
                        atleast(pool, s_xn, i)
                        atleast(pool, s_r1, i)
                        pool.tensor_tensor(rs[:], var[:], mhalf[:], ALU.pow).then_inc(s_pw, 1)

                def prep(t, i, par):
                    for c in range(DC):
                        at = PREP["pool_dt"][c]
                        n = 4 * i + c
                        if t == at:
                            pool.wait_ge(s_dt, n + 1)
                            pool.wait_ge(s_xs, i + 1)
                            atleast(pool, s_lou, n)
                            atleast(pool, s_xu, n)
                            pool.tensor_tensor(uv[:], dtv[:], xs[:, c, :], ALU.mult).then_inc(s_u, 1)
                        for k, src, s_rem, s_lo, s_ext in ((0, dtv, s_remd, s_lod, s_xd), (1, uv, s_remu, s_lou, s_xu)):
                            if t == at + 1 + 2 * k:
                                if k == 1:
                                    pool.wait_ge(s_u, n + 1)
                                atleast(pool, s_ext, n)
                                pool.tensor_tensor(rem[:, k, :], src[:], src[:].bitcast(BF16)[:, 1::2],
                                                   ALU.subtract).then_inc(s_rem, 1)
                            if t == at + 2 + 2 * k:
                                pool.wait_ge(s_rem, n + 1)
                                if c >= 2:
                                    pool.wait_ge(d_stk[c - 2], STK_DMAS * (i + 1))
                                else:
                                    atleast(pool, d_stk[c + 2], STK_DMAS * i)
                                pool.tensor_tensor(parts[:, c % 2, k, 2, :], rem[:, k, :], rem[:, k, :].bitcast(BF16)[:, 1::2],
                                                   ALU.subtract).then_inc(s_lo, 1)

                def post(t, j, par):
                    for n, at in enumerate(POST["pow"]):
                        if t == at:
                            pool.wait_ge(s_dp, 8 * j + 4 * n + 3)
                            if n == 0:
                                atleast(pool, s_hid, j)
                            else:
                                pool.wait_ge(s_z2, j + 1)
                            pool.tensor_tensor(rs2[:], var2[:], mhalf[:, 0:SUB], ALU.pow).then_inc(s_pw2, 1)
                    if t == POST["x1"]:
                        pool.wait_ge(s_z2, j + 1)
                        pool.tensor_tensor(z[:], z[:], xo[:], ALU.add).then_inc(s_x1, 1)

                def pair(m, i, par):
                    pool.wait_ge(s_scan, 64 * i + 2 * m + 2)
                    atleast(pool, s_sum, 16 * i + m // 2 - 1)
                    b = (2 * m) % 8
                    pool.tensor_tensor(hc[:, b:b + 2, :], h[:, b:b + 2, :],
                                       c_rep[:, par, :].unsqueeze(1).broadcast_to((P, 2, T)), ALU.mult).then_inc(s_hc, 1)

                def step(i, par, has_late, has_prev, has_cur, has_next):
                    for t in range(GROUPS):
                        if has_late:
                            post(64 + t, i - 2, par)
                        if has_cur:
                            prep(64 + t, i, par)
                        if has_next:
                            prep(t, i + 1, 1 - par)
                        if has_next and not (isinstance(i, int) and i + 2 >= TILES):
                            head(t - HEAD_AT, i + 2)
                        if has_prev:
                            post(t, i - 1, 1 - par)
                        if t == 1 and has_prev:
                            pair(GROUPS // 2 - 1, i - 1, 1 - par)
                        elif t % 2 == 1 and t > 1 and has_cur:
                            if t == 3:
                                pool.wait_ge(s_ev, NU * i + use("c") + 1)
                            pair(t // 2 - 1, i, par)

                pool.memset(ident[:], 1.0).then_inc(s_id, 1)
                pool.memset(m8[:], 1.0).then_inc(s_id, 1)
                pool.wait_ge(s_id, 2)
                pool.affine_select(out=ident[:], in_=ident[:], compare_op=ALU.is_equal, fill=0.0, base=0,
                                   pattern=[[-1, P]], channel_multiplier=1).then_inc(s_id, 1)
                pool.affine_select(out=m8[:], in_=m8[:], compare_op=ALU.is_ge, fill=0.0, base=0,
                                   pattern=[[-16, 8]], channel_multiplier=1).then_inc(s_id, 1)
                pool.wait_ge(s_id, 4)
                pool.affine_select(out=m8[:], in_=m8[:], compare_op=ALU.is_ge, fill=0.0, base=15,
                                   pattern=[[16, 8]], channel_multiplier=-1).then_inc(s_id, 1)
                pool.wait_ge(s_const, 1)
                for t in range(GROUPS - HEAD_AT):
                    head(t, 0)
                for t in range(GROUPS):
                    prep(t, 0, 0)
                    head(t - HEAD_AT, 1)
                all_steps(pool, step)


def group_column(t):
    c, s, q = t // 16, t // 4 % 4, t % 4
    return 16 * c + 4 * q + s


def experts(nc, sem, B, S, ident, mhalf, outf, w1, w2, w3, hid_dram, acc_dram, lg_dram, tab_dram):
    R = B * E
    SEGS = P // R
    L = S // SEGS
    ROUNDS = CAP // 8
    RING = 8
    GROUP = 4
    TAKEN = -3.0e38
    with ExitStack() as ctx:
        def sb(name, shape, dt=F32):
            return ctx.enter_context(nc.sbuf_tensor(name, shape, dt))

        def ps(name, shape):
            return ctx.enter_context(nc.psum_tensor(name, shape, F32))

        lg = sb("lg", [P, L])
        lgx = sb("lgx", [P, L])
        best = sb("best", [P, CAP])
        place = sb("place", [P, CAP], U32)
        placef = sb("placef", [P, CAP])
        token = sb("token", [P, CAP], U32)
        mass = sb("mass", [P, 1])
        negm = sb("negm", [P, 1])
        seg0 = sb("seg0", [P, 1])
        second = sb("second", [P, 1])
        first_row = sb("first_row", [P, 1])
        cand = sb("cand", [R, SEGS * CAP])
        masses = sb("masses", [R, SEGS])
        tops = sb("tops", [R, SEGS])
        vals = sb("vals", [R, CAP])
        ids = sb("ids", [R, CAP], U32)
        idf = sb("idf", [R, CAP])
        small = sb("small", [R, 8])
        ramp = sb("ramp", [R, R])
        row_base = sb("row_base", [R, 1])
        of_batch = sb("of_batch", [R, B])
        pick = sb("pick", [R, E])
        spread = sb("spread", [R, 2, B * CAP])
        entry = sb("entry", [P, E], U32)
        rowid = sb("rowid", [P, E], U32)
        weight = sb("weight", [P, E])
        w1s = sb("w1s", [P, RING, KC, DFF])
        w2s = sb("w2s", [P, RING, KC, DFF])
        w3s = sb("w3s", [P, RING, FC, DM])
        taken = sb("taken", [P, RING, DM])
        tT = sb("tT", [P, 2, KC, P])
        act1 = sb("act1", [P, 2, DFF])
        x1 = sb("x1", [P, E, DM])
        comb = sb("comb", [P, E, CW])
        rowf = sb("rowf", [P, E])
        above = sb("above", [P, E])
        loser = sb("loser", [P, E])
        dest = sb("dest", [P, E], U32)
        fst = sb("fst", [P, E, 6])
        fmv = sb("fmv", [P, E, 2])
        fvar = sb("fvar", [P, E])
        frs = sb("frs", [P, E])
        fnm = sb("fnm", [P, E])
        pt = ps("pt", [P, 512])
        pg = ps("pg", [P, 2, DFF])
        pv = ps("pv", [P, 2, DFF])
        pY = ps("pY", [P, 2, 512])

        d_lg, s_k, s_ka, s_kt = sem("lg_loaded"), sem("selection_step"), sem("selection_exp"), sem("selection_spread")
        s_pos, d_tab, d_cand, d_mass = (sem("entries_ready"), sem("table_stored"), sem("candidates_loaded"),
                                        sem("masses_loaded"))
        s_tok, s_bit, s_lose, s_dest = sem("tokens_ready"), sem("bits_step"), sem("losers_step"), sem("dest_ready")
        FIRST = 1 + (R - 1).bit_length() + 2
        SEGMENTS_DONE = FIRST + 2 * ROUNDS + 1
        TOP_READY = SEGMENTS_DONE + 3
        ROWS_DONE = TOP_READY + 2 * ROUNDS - 1
        PLACES_READY = ROWS_DONE + 2
        WEIGHTS_READY = PLACES_READY + 8
        d_id = [sem(f"rowid_loaded_{r}") for r in range(4)]
        d_wt = [sem(f"weights_loaded_{r}") for r in range(RING)]
        d_tk = [sem(f"taken_loaded_{r}") for r in range(RING)]
        s_tr, s_tc, s_g, s_v = sem("taken_transposed"), sem("taken_copied"), sem("gate_product"), sem("value_product")
        s_sl, s_m, s_o, s_y = sem("gate_silu"), sem("gated_value"), sem("expert_product"), sem("expert_ready")
        d_add, d_x1, d_fin = sem("combined"), sem("x1_loaded"), sem("final_stored")
        d_cb = [sem(f"combined_loaded_{g}") for g in range(E // GROUP)]
        s_f, s_fp, s_fn, s_fa, s_fo = (sem("final_stats_step"), sem("final_pow"), sem("final_mean"),
                                       sem("final_normalised"), sem("final_sum"))

        with nc.Block() as block:
            @block.sync
            def _(sp):
                def load(e):
                    if e >= RING:
                        sp.wait_ge(s_o, e - RING + 1)
                    for w, dst in ((w1, w1s), (w2, w2s), (w3, w3s)):
                        sp.dma_start(dst[:, e % RING], w[e].rearrange("(c p) f -> p c f", p=P)).then_inc(d_wt[e % RING], 16)

                for g in range(SEGS):
                    sp.dma_start(lg[R * g:R * (g + 1), :], lg_dram[:, g * L:(g + 1) * L]).then_inc(d_lg, 16)
                for e in range(2):
                    load(e)
                sp.wait_ge(s_k, SEGMENTS_DONE)
                sp.wait_ge(s_ka, 1)
                for g in range(SEGS):
                    sp.dma_start(cand[:, g * CAP:(g + 1) * CAP], best[R * g:R * (g + 1), :]).then_inc(d_cand, 16)
                for g in range(SEGS):
                    sp.dma_start(masses[:, g:g + 1], mass[R * g:R * (g + 1), :]).then_inc(d_mass, 16)
                sp.wait_ge(s_tok, 1)
                for g in range(SEGS):
                    sp.dma_start(tab_dram.rearrange("(r g k) o -> g r (k o)", g=SEGS, k=CAP)[g],
                                 token[R * g:R * (g + 1), :]).then_inc(d_tab, 16)
                sp.wait_ge(d_cand, 16 * SEGS)
                for e in range(2, 4):
                    load(e)
                sp.wait_ge(s_tr, 1)
                for e in range(4, E):
                    load(e)
                sp.wait_ge(d_tab, 16 * SEGS)

            @block.vector
            def _(v):
                n = [0]

                def link(ins):
                    n[0] += 1
                    ins.then_inc(s_k, 1)
                    v.wait_ge(s_k, n[0])

                for g in range(SEGS):
                    v.memset(seg0[R * g:R * (g + 1), :], float(g * L))
                v.tensor_reduce(second[:], ident[:].rearrange("p (g r) -> p g r", r=R)[:, :, E:R], AX.XY, ALU.add)
                v.tensor_tensor(pick[:], ident[0:R, 0:E], ident[0:R, E:2 * E], ALU.add)
                for b in range(B):
                    v.tensor_reduce(of_batch[:, b:b + 1], ident[0:R, b * E:(b + 1) * E], AX.X, ALU.add)
                v.memset(comb[:, :, DM:], 0.0).then_inc(s_bit, 1)
                v.wait_ge(s_bit, 1)
                for e in range(E):
                    v.memset(comb[:, e, DM:DM + 1], float(2 ** e))
                    ins = v.memset(above[:, e:e + 1], float(2 ** (e + 1)))
                ins.then_inc(s_bit, 1)
                link(v.memset(ramp[:, 0:1], 0.0))
                w = 1
                while w < R:
                    link(v.tensor_scalar(ramp[:, w:2 * w], ramp[:, 0:w], float(w * SEGS * CAP), None, ALU.add))
                    w *= 2
                v.tensor_scalar(first_row[:], second[:], float(S), seg0[:], ALU.mult, ALU.add)
                link(v.tensor_tensor(ramp[:], ramp[:], ident[0:R, 0:R], ALU.mult))
                link(v.tensor_reduce(row_base[:], ramp[:], AX.X, ALU.add))

                def rounds(values, places, src, after_first):
                    for r in range(ROUNDS):
                        eight = values[:, 8 * r:8 * r + 8]
                        link(v.max(eight, src[:]))
                        if r == 0:
                            after_first()
                        found = v.max_index(places[:, 8 * r:8 * r + 8], eight, src[:])
                        if r == ROUNDS - 1:
                            link(found)
                        else:
                            link(v.match_replace(src[:], eight, src[:], TAKEN))

                def minus_segment_maximum():
                    link(v.tensor_scalar(negm[:], best[:, 0:1], -1.0, None, ALU.mult))
                    v.wait_ge(s_ka, 1)

                v.wait_ge(d_lg, 16 * SEGS)
                rounds(best, place, lg, minus_segment_maximum)
                link(v.tensor_copy(placef[:], place[:]))
                v.tensor_scalar(token[:], placef[:], first_row[:], None, ALU.add).then_inc(s_tok, 1)

                v.wait_ge(d_cand, 16 * SEGS)
                v.tensor_copy(tops[:], cand[:].rearrange("p (g k) -> p g k", k=CAP)[:, :, 0])

                def minus_maximum():
                    link(v.tensor_scalar(small[:, 0:1], vals[:, 0:1], -1.0, None, ALU.mult))

                rounds(vals, ids, cand, minus_maximum)
                link(v.tensor_copy(idf[:], ids[:]))
                for b in range(B):
                    ins = v.tensor_scalar(spread[:, 0, b * CAP:(b + 1) * CAP], idf[:], row_base[:], of_batch[:, b:b + 1],
                                          ALU.add, ALU.mult)
                link(ins)
                v.wait_ge(s_kt, 1)
                v.tensor_copy(entry[:], pg[:, 0, 0:E]).then_inc(s_pos, 1)
                v.wait_ge(s_ka, 3)
                v.wait_ge(d_mass, 16 * SEGS)
                link(v.tensor_tensor(masses[:], masses[:], tops[:], ALU.mult))
                link(v.tensor_reduce(small[:, 1:2], masses[:], AX.X, ALU.add))
                link(v.reciprocal(small[:, 2:3], small[:, 1:2]))
                link(v.tensor_scalar(vals[:], vals[:], small[:, 2:3], None, ALU.mult))
                link(v.tensor_reduce(small[:, 4:5], vals[:], AX.X, ALU.add))
                link(v.tensor_scalar(small[:, 4:5], small[:, 4:5], 1e-9, None, ALU.add))
                link(v.reciprocal(small[:, 5:6], small[:, 4:5]))
                for b in range(B):
                    ins = v.tensor_scalar(spread[:, 1, b * CAP:(b + 1) * CAP], vals[:], small[:, 5:6],
                                          of_batch[:, b:b + 1], ALU.mult, ALU.mult)
                link(ins)
                v.wait_ge(s_kt, 2)
                v.tensor_copy(weight[:], pg[:, 1, 0:E]).then_inc(s_pos, 1)

                for e in range(E):
                    v.wait_ge(s_sl, e + 1)
                    v.wait_ge(s_v, e + 1)
                    v.tensor_tensor(act1[:, e % 2, :], act1[:, e % 2, :], pv[:, e % 2, :], ALU.mult).then_inc(s_m, 1)

                def statistics(g):
                    es = range(GROUP * g, GROUP * (g + 1))
                    v.wait_ge(d_cb[g], 16 * GROUP)
                    for e in es:
                        ins = v.bn_stats(fst[:, e, :], comb[:, e, 0:DM])
                    ins.then_inc(s_f, 1)
                    cols = slice(es.start, es.stop)
                    v.tensor_tensor(loser[:, cols], comb[:, cols, DM], above[:, cols], ALU.is_ge).then_inc(s_lose, 1)
                    v.wait_ge(s_f, 3 * g + 1)
                    for e in es:
                        ins = v.bn_aggr(fmv[:, e, :], fst[:, e, :])
                    ins.then_inc(s_f, 1)
                    v.wait_ge(s_f, 3 * g + 2)
                    v.tensor_scalar(fvar[:, cols], fmv[:, cols, 1], EPS, None, ALU.add).then_inc(s_f, 1)
                    v.wait_ge(s_lose, g + 2)
                    v.scalar_tensor_tensor(out=dest[:, cols], in0=loser[:, cols], scalar=float(2 * B * S), in1=rowf[:, cols],
                                           op0=ALU.mult, op1=ALU.add).then_inc(s_dest, 1)

                def mean(g):
                    cols = slice(GROUP * g, GROUP * (g + 1))
                    v.wait_ge(s_fp, g + 1)
                    v.scalar_tensor_tensor(out=fnm[:, cols], in0=fmv[:, cols, 0], scalar=-1.0, in1=frs[:, cols],
                                           op0=ALU.mult, op1=ALU.mult).then_inc(s_fn, 1)

                def total(g):
                    for e in range(GROUP * g, GROUP * (g + 1)):
                        v.wait_ge(s_fa, e + 1)
                        v.tensor_tensor(x1[:, e, :], comb[:, e, 0:DM], x1[:, e, :], ALU.add).then_inc(s_fo, 1)

                v.wait_ge(d_x1, 16 * E)
                v.tensor_copy(rowf[:], rowid[:]).then_inc(s_lose, 1)
                for g in range(E // GROUP + 2):
                    if g < E // GROUP:
                        statistics(g)
                    if 0 < g <= E // GROUP:
                        mean(g - 1)
                    if g > 1:
                        total(g - 2)

            @block.scalar
            def _(act):
                act.wait_ge(s_k, FIRST + 2)
                act.activation(lgx[:], lg[:], ACT.Exp, bias=negm[:], accum_out=mass[:]).then_inc(s_ka, 1)
                act.wait_ge(s_k, TOP_READY)
                act.activation(tops[:], tops[:], ACT.Exp, bias=small[:, 0:1]).then_inc(s_ka, 1)
                act.wait_ge(s_k, ROWS_DONE)
                act.activation(vals[:], vals[:], ACT.Exp, bias=small[:, 0:1]).then_inc(s_ka, 1)

                def copied(e):
                    act.wait_ge(s_tr, e + 1)
                    if e >= 2:
                        act.wait_ge(s_v, e - 1)
                    act.copy(tT[:, e % 2], pt[:, 0:KC * P]).then_inc(s_tc, 1)

                def weighted(e):
                    act.wait_ge(s_o, e + 1)
                    if e == 0:
                        act.wait_ge(s_pos, 2)
                    act.activation(comb[:, e, 0:DM], pY[:, e % 2, 0:DM], ACT.Identity, scale=weight[:, e:e + 1]).then_inc(s_y, 1)

                copied(0)
                for e in range(E):
                    act.wait_ge(s_g, e + 1)
                    if e >= 2:
                        act.wait_ge(s_o, e - 1)
                    act.activation(act1[:, e % 2, :], pg[:, e % 2, :], ACT.Silu).then_inc(s_sl, 1)
                    if e + 1 < E:
                        copied(e + 1)
                    if e > 0:
                        weighted(e - 1)
                weighted(E - 1)

                for e in range(E):
                    act.wait_ge(s_fn, e // GROUP + 1)
                    act.activation(comb[:, e, 0:DM], comb[:, e, 0:DM], ACT.Identity, scale=frs[:, e:e + 1],
                                   bias=fnm[:, e:e + 1]).then_inc(s_fa, 1)

            @block.tensor
            def _(pe):
                for k, ready in ((0, PLACES_READY), (1, WEIGHTS_READY)):
                    pe.wait_ge(s_k, ready)
                    pe.matmul(pg[:, k, 0:E], spread[:, k, :], pick[:], start=True, stop=True).then_inc(s_kt, 1)

                def transposed(e):
                    pe.wait_ge(d_tk[e % RING], 16 * (e // RING + 1))
                    if e > 0:
                        pe.wait_ge(s_tc, e)
                    for k in range(KC):
                        mm = pe.transpose(pt[:, k * P:(k + 1) * P], taken[:, e % RING, k * P:(k + 1) * P], ident[:])
                    mm.then_inc(s_tr, 1)

                def product(e):
                    pe.wait_ge(s_m, e + 1)
                    if e >= 2:
                        pe.wait_ge(s_y, e - 1)
                    for f in range(FC):
                        mm = pe.matmul(pY[:, e % 2, 0:DM], act1[:, e % 2, f * P:(f + 1) * P], w3s[:, e % RING, f, :],
                                       start=(f == 0), stop=(f == FC - 1))
                    mm.then_inc(s_o, 1)

                pe.wait_ge(s_pos, 2)
                transposed(0)
                for e in range(E):
                    pe.wait_ge(d_wt[e % RING], 48 * (e // RING + 1))
                    pe.wait_ge(s_tc, e + 1)
                    if e >= 2:
                        pe.wait_ge(s_m, e - 1)
                    for w, bank, s_w in ((w1s, pg, s_g), (w2s, pv, s_v)):
                        for f in range(FC):
                            for k in range(KC):
                                mm = pe.matmul(bank[:, e % 2, f * P:(f + 1) * P], w[:, e % RING, k, f * P:(f + 1) * P],
                                               tT[:, e % 2, k, :], start=(k == 0), stop=(k == KC - 1))
                        mm.then_inc(s_w, 1)
                        if w is w1s and e + 1 < E:
                            transposed(e + 1)
                    if e > 0:
                        product(e - 1)
                product(E - 1)

            @block.gpsimd
            def _(pool):
                def at(table, e):
                    return bass.IndirectOffsetOnAxis(ap=table[:, e:e + 1], axis=0)

                def find(e):
                    pool.indirect_dma_start(rowid[:, e:e + 1], None, tab_dram, at(entry, e)).then_inc(d_id[e % 4], 16)

                def take(e):
                    pool.wait_ge(d_id[e % 4], 16 * (e // 4 + 1))
                    if e >= RING:
                        pool.wait_ge(s_tr, e - RING + 1)
                    pool.indirect_dma_start(taken[:, e % RING, :], None, hid_dram, at(rowid, e)).then_inc(d_tk[e % RING], 16)
                    if e + 4 < E:
                        find(e + 4)

                pool.wait_ge(d_tab, 16 * SEGS)
                pool.wait_ge(s_pos, 1)
                for e in range(4):
                    find(e)
                for e in range(RING):
                    take(e)
                for e in range(E):
                    if e == 0:
                        pool.wait_ge(s_bit, 2)
                    pool.indirect_dma_start(x1[:, e, :], None, outf, at(rowid, e)).then_inc(d_x1, 16)
                    if e + RING < E:
                        take(e + RING)
                    pool.wait_ge(s_y, e + 1)
                    if e > 0:
                        pool.wait_ge(d_add, 16 * e)
                    pool.indirect_dma_start(acc_dram, at(rowid, e), comb[:, e, :], None,
                                            compute_op=ALU.add).then_inc(d_add, 16)
                pool.wait_ge(d_add, 16 * E)

                def inverse(g):
                    cols = slice(GROUP * g, GROUP * (g + 1))
                    pool.wait_ge(s_f, 3 * g + 3)
                    pool.tensor_tensor(frs[:, cols], fvar[:, cols], mhalf[:, 0:GROUP], ALU.pow).then_inc(s_fp, 1)

                def gather(g):
                    for e in range(GROUP * g, GROUP * (g + 1)):
                        pool.indirect_dma_start(comb[:, e, :], None, acc_dram, at(rowid, e)).then_inc(d_cb[g], 16)

                def store(g):
                    pool.wait_ge(s_dest, g + 1)
                    for e in range(GROUP * g, GROUP * (g + 1)):
                        pool.wait_ge(s_fo, e + 1)
                        pool.indirect_dma_start(outf, at(dest, e), x1[:, e, :], None, bounds_check=B * S - 1,
                                                oob_is_err=False).then_inc(d_fin, 16)

                for g in range(E // GROUP + 3):
                    if g < E // GROUP:
                        gather(g)
                    if 0 < g <= E // GROUP:
                        inverse(g - 1)
                    if g >= 3:
                        store(g - 3)
                pool.wait_ge(d_fin, 16 * E)


_INS = ['L0_attn_x', 'L0_attn_rms_w', 'L0_attn_W_in', 'L0_attn_conv_w', 'L0_attn_conv_b', 'L0_attn_W_x', 'L0_attn_W_dt',
        'L0_attn_A_log', 'L0_attn_W_out', 'L0_ffn_router_w1', 'L0_ffn_router_w2', 'L0_ffn_w1', 'L0_ffn_w2', 'L0_ffn_w3']


def kernel(**inputs):
    import numpy as _np
    import concourse.bacc as _bacc
    from concourse import mybir as _mybir
    from concourse.bass_utils import run_bass_kernel_spmd as _run

    nc = _bacc.Bacc("TRN2", target_bir_lowering=False, num_devices=1)
    arrays, args = {}, []
    for name in _INS:
        a = _np.ascontiguousarray(inputs[name])
        arrays[f"in_{name}_dram"] = a
        args.append(nc.dram_tensor(f"in_{name}_dram", a.shape, _mybir.dt.from_np(a.dtype), kind="ExternalInput").ap())
    out = nc.dram_tensor("out_dram", inputs['L0_attn_x'].shape, _mybir.dt.float32, kind="ExternalOutput").ap()
    sandwich(nc, *args, out)
    r = _run(nc, [arrays], core_ids=[0])
    return r.results[0]["out_dram"]
```
